# Optimizing a Trainium2 kernel written in Bass

```python
import numpy as np
import jax
import jax.numpy as jnp

def _softmax(x, axis=-1):
    return jax.nn.softmax(x, axis=axis)

def _gelu(x):
    return jax.nn.gelu(x, approximate=True)

def _silu(x):
    return jax.nn.silu(x)

def _sigmoid(x):
    return jax.nn.sigmoid(x)

def _layernorm(x, axis=-1, eps=1e-05):
    m = jnp.mean(x, axis=axis, keepdims=True)
    v = jnp.var(x, axis=axis, keepdims=True)
    return (x - m) / jnp.sqrt(v + eps)

def _scatter_add(tgt, idx, src, axis=0):
    return tgt.at[idx].add(src)

def _segment_sum(src, seg, n):
    return jax.ops.segment_sum(src, seg, n)
kernel_name = 'mk_decoder_preln_d4_seqx_r8_6a79be'

def setup_inputs(seed: int=0):
    np.random.seed(seed)
    _w = jnp.asarray

    def _rec_inputs():
        import jax
        import jax.numpy as jnp
        _rk = jax.random.key(seed)
        x = 0.0002417 + 0.9998 * jax.random.normal(jax.random.fold_in(_rk, 1), (4, 512, 128), jnp.float32)
        _lenS = 512 - jax.random.randint(jax.random.fold_in(_rk, 7), (4,), 0, max(1, 512 // 4) + 1, jnp.int32)
        _lenS2 = 154 - jax.random.randint(jax.random.fold_in(_rk, 8), (4,), 0, max(1, 154 // 4) + 1, jnp.int32)
        _ctx_1024P = jax.random.normal(jax.random.fold_in(_rk, 11), (4, 16, 128), jnp.float32)
        _ctx_1024c = jax.random.dirichlet(jax.random.fold_in(_rk, 511), 0.3 * jnp.ones((16,), jnp.float32), (4, 154))
        _ctx_1024t = jnp.einsum('bsk,bkd->bsd', _ctx_1024c, _ctx_1024P)
        _ctx_1024t = _ctx_1024t * jax.lax.rsqrt(jnp.mean(jnp.square(_ctx_1024t)) + 1e-12) * 0.953939
        ctx_1024 = 7.22013e-05 + 1.00017 * (_ctx_1024t + 0.3 * jax.random.normal(jax.random.fold_in(_rk, 611), (4, 154, 128), jnp.float32))
        _validS = jnp.arange(512)[None, :] < _lenS[:, None]
        _validS2 = jnp.arange(154)[None, :] < _lenS2[:, None]
        _causal = jnp.tril(jnp.ones((512, 512), dtype=bool))
        mask_Bx1x1xS2_ik0 = jnp.where(jnp.broadcast_to(_validS2[:, None, None, :], (4, 1, 1, 154)), 0, 1).astype(jnp.int32)
        mask_Bx1x1xS2_ff0 = jnp.where(jnp.ones((4, 1, 1, 154), dtype=bool), 0.0, -1000000000.0).astype(jnp.float32)
        mask_BxS2_ik0 = jnp.where(jnp.broadcast_to(_validS2[:, :], (4, 154)), 0, 1).astype(jnp.int32)
        mask_SxS2_ik1 = jnp.where(jnp.broadcast_to(_validS2[0:1, :], (512, 154)), 1, 0).astype(jnp.int32)
        return (x, ctx_1024, _lenS2, mask_Bx1x1xS2_ik0, mask_Bx1x1xS2_ff0, mask_BxS2_ik0, mask_SxS2_ik1)
    x, ctx_1024, _lenS2, mask_Bx1x1xS2_ik0, mask_Bx1x1xS2_ff0, mask_BxS2_ik0, mask_SxS2_ik1 = _rec_inputs()

    def _L0_attn_setup():
        import jax, jax.numpy as jnp
        import numpy as np
        B, S, D_IN, D_OUT = (4, 256, 128, 128)
        key = jax.random.key(seed)
        ks = jax.random.split(key, 7)
        return {'X': jax.random.normal(ks[0], (B, S, D_IN), dtype=jnp.float32), 'Wq': jax.random.normal(ks[1], (D_IN, D_OUT), dtype=jnp.float32) * (1.0 / np.sqrt(D_IN)), 'bq': jax.random.normal(ks[2], (D_OUT,), dtype=jnp.float32) * 0.02, 'Wk': jax.random.normal(ks[3], (D_IN, D_OUT), dtype=jnp.float32) * (1.0 / np.sqrt(D_IN)), 'bk': jax.random.normal(ks[4], (D_OUT,), dtype=jnp.float32) * 0.02, 'Wv': jax.random.normal(ks[5], (D_IN, D_OUT), dtype=jnp.float32) * (1.0 / np.sqrt(D_IN)), 'bv': jax.random.normal(ks[6], (D_OUT,), dtype=jnp.float32) * 0.02}
    _L0_attn_all = _L0_attn_setup()
    _L0_attn_in = {k: v for k, v in _L0_attn_all.items() if k in ('Wq', 'bq', 'Wk', 'bk', 'Wv', 'bv')}
    del _L0_attn_all

    def _L0_xattn_setup():
        import jax, jax.numpy as jnp
        import numpy as np
        import math
        D_MODEL = 128
        HEADS = 16
        D_K = D_MODEL // HEADS
        N, L = (4, 256)
        key0 = jax.random.key(seed)
        ks = jax.random.split(key0, 12)
        s = 1.0 / math.sqrt(D_MODEL)
        return {'value': jax.random.normal(ks[0], (N, L, D_MODEL), jnp.float32), 'key': jax.random.normal(ks[1], (N, L, D_MODEL), jnp.float32), 'query': jax.random.normal(ks[2], (N, L, D_MODEL), jnp.float32), 'mask': jax.random.randint(ks[3], (N, 1, 1, L), 0, 2, jnp.int32), 'wq': jax.random.normal(ks[4], (D_MODEL, D_MODEL), jnp.float32) * s, 'bq': jax.random.normal(ks[5], (D_MODEL,), jnp.float32) * s, 'wk': jax.random.normal(ks[6], (D_MODEL, D_MODEL), jnp.float32) * s, 'bk': jax.random.normal(ks[7], (D_MODEL,), jnp.float32) * s, 'wv': jax.random.normal(ks[8], (D_MODEL, D_MODEL), jnp.float32) * s, 'bv': jax.random.normal(ks[9], (D_MODEL,), jnp.float32) * s, 'wo': jax.random.normal(ks[10], (D_MODEL, D_MODEL), jnp.float32) * s, 'bo': jax.random.normal(ks[11], (D_MODEL,), jnp.float32) * s}
    _L0_xattn_all = _L0_xattn_setup()
    _L0_xattn_in = {k: v for k, v in _L0_xattn_all.items() if k in ('wq', 'bq', 'wk', 'bk', 'wv', 'bv', 'wo', 'bo')}
    del _L0_xattn_all

    def _L0_ffn_setup():
        import jax, jax.numpy as jnp
        import numpy as np
        TOP_K = 2
        key = jax.random.key(seed)
        ks = jax.random.split(key, 5)
        B, S, H, I, E = (4, 256, 128, 512, 8)
        scale_hi = (2.0 / (H + I)) ** 0.5
        scale_he = (2.0 / (H + E)) ** 0.5
        return {'x': jax.random.normal(ks[0], (B, S, H), dtype=jnp.float32), 'router_w': jax.random.normal(ks[1], (E, H), dtype=jnp.float32) * scale_he, 'gate_w': jax.random.normal(ks[2], (E, I, H), dtype=jnp.float32) * scale_hi, 'up_w': jax.random.normal(ks[3], (E, I, H), dtype=jnp.float32) * scale_hi, 'down_w': jax.random.normal(ks[4], (E, H, I), dtype=jnp.float32) * scale_hi}
    _L0_ffn_all = _L0_ffn_setup()
    _L0_ffn_in = {k: v for k, v in _L0_ffn_all.items() if k in ('router_w', 'gate_w', 'up_w', 'down_w')}
    del _L0_ffn_all

    def _L1_attn_setup():
        import jax, jax.numpy as jnp
        import numpy as np
        N_HEAD = 16
        PAGE_SIZE = 32
        ROPE_THETA = 10000.0

        def _rope_tables(T, D, dtype):
            inv = 1.0 / ROPE_THETA ** (np.arange(0, D, 2, dtype=np.float32) / D)
            ang = np.outer(np.arange(T, dtype=np.float32), inv)
            return (jnp.asarray(np.cos(ang), dtype), jnp.asarray(np.sin(ang), dtype))

        def _apply_rope(x, cos, sin):
            x1 = x[..., 0::2]
            x2 = x[..., 1::2]
            c = cos[None, :, None, :]
            s = sin[None, :, None, :]
            out = jnp.stack([x1 * c - x2 * s, x1 * s + x2 * c], axis=-1)
            return out.reshape(x.shape)
        key = jax.random.key(seed)
        ks = jax.random.split(key, 6)
        B, T, E = (2, 256, 128)
        L = E // 2
        sc = lambda fan: 1.0 / np.sqrt(fan)
        return {'x': jax.random.normal(ks[0], (B, T, E), jnp.float32), 'wq': jax.random.normal(ks[1], (E, E), jnp.float32) * sc(E), 'w_down': jax.random.normal(ks[2], (E, L), jnp.float32) * sc(E), 'wk_up': jax.random.normal(ks[3], (L, E), jnp.float32) * sc(L), 'wv_up': jax.random.normal(ks[4], (L, E), jnp.float32) * sc(L), 'wo': jax.random.normal(ks[5], (E, E), jnp.float32) * sc(E)}
    _L1_attn_all = _L1_attn_setup()
    _L1_attn_in = {k: v for k, v in _L1_attn_all.items() if k in ('wq', 'w_down', 'wk_up', 'wv_up', 'wo')}
    del _L1_attn_all

    def _L1_xattn_setup():
        import jax, jax.numpy as jnp
        import numpy as np
        B, S, D, H = (2, 256, 128, 16)
        HD = D // H
        key = jax.random.key(seed)
        ks = jax.random.split(key, 8)
        sc = 0.02
        return {'q': jax.random.normal(ks[0], (B, S, D), jnp.float32), 'k': jax.random.normal(ks[1], (B, S, D), jnp.float32), 'v': jax.random.normal(ks[2], (B, S, D), jnp.float32), 'padding_mask': jnp.zeros((B, 1, 1, S), jnp.float32), 'Wq': jax.random.normal(ks[3], (D, D), jnp.float32) * sc, 'bq': jnp.zeros((D,), jnp.float32), 'Wk': jax.random.normal(ks[4], (D, D), jnp.float32) * sc, 'bk': jnp.zeros((D,), jnp.float32), 'Wv': jax.random.normal(ks[5], (D, D), jnp.float32) * sc, 'bv': jnp.zeros((D,), jnp.float32), 'Wo': jax.random.normal(ks[6], (D, D), jnp.float32) * sc, 'bo': jnp.zeros((D,), jnp.float32)}
    _L1_xattn_all = _L1_xattn_setup()
    _L1_xattn_in = {k: v for k, v in _L1_xattn_all.items() if k in ('Wq', 'bq', 'Wk', 'bk', 'Wv', 'bv', 'Wo', 'bo')}
    del _L1_xattn_all

    def _L1_ffn_setup():
        import jax, jax.numpy as jnp
        import numpy as np
        DIM = 128
        HIDDEN = 384
        SCALE = 1.0 / 127.0

        def _dequant(w_int, dtype):
            return w_int.astype(dtype) * jnp.asarray(SCALE, dtype)
        key = jax.random.key(seed)
        k_x, k_g, k_u, k_d = jax.random.split(key, 4)
        x = jax.random.normal(k_x, (4, 256, DIM), dtype=jnp.float32)
        w_gate = jax.random.randint(k_g, (HIDDEN, DIM), -127, 128, dtype=jnp.int32)
        w_up = jax.random.randint(k_u, (HIDDEN, DIM), -127, 128, dtype=jnp.int32)
        w_down = jax.random.randint(k_d, (DIM, HIDDEN), -127, 128, dtype=jnp.int32)
        return {'x': x, 'w_gate': w_gate, 'w_up': w_up, 'w_down': w_down}
    _L1_ffn_all = _L1_ffn_setup()
    _L1_ffn_in = {k: v for k, v in _L1_ffn_all.items() if k in ('w_gate', 'w_up', 'w_down')}
    del _L1_ffn_all

    def _L2_attn_setup():
        import jax, jax.numpy as jnp
        from jax import lax
        import numpy as np
        D_MODEL, D_STATE, D_CONV, EXPAND = (128, 16, 4, 2)
        D_INNER = D_MODEL * EXPAND
        BATCH, SEQ = (2, 256)
        LN_EPS = 1e-05

        def _forward(x, in_proj_w, in_proj_b, conv_w, conv_b, x_proj_w, x_proj_b, A_log, D, out_proj_w, out_proj_b, ln_gamma, ln_beta):
            d_state = A_log.shape[1]
            d_conv = conv_w.shape[-1]
            residual = x
            xz = x @ in_proj_w.T + in_proj_b
            x_main, z = jnp.split(xz, 2, axis=-1)
            xc = jnp.transpose(x_main, (0, 2, 1))
            xc = lax.conv_general_dilated(xc, conv_w, window_strides=(1,), padding=[(d_conv - 1, 0)], dimension_numbers=('NCH', 'OIH', 'NCH'), feature_group_count=xc.shape[1])
            xc = xc + conv_b[None, :, None]
            xc = jax.nn.silu(jnp.transpose(xc, (0, 2, 1)))
            ssm = xc @ x_proj_w.T + x_proj_b
            B_param = ssm[..., :d_state]
            C_param = ssm[..., d_state:2 * d_state]
            delta = jax.nn.softplus(ssm[..., -1:])
            A = -jnp.exp(A_log)

            def step(h, ts):
                dt, B_t, C_t, x_t = ts
                dA = jnp.exp(A[None] * dt[:, :, None])
                dBx = dt[:, :, None] * B_t[:, None, :] * x_t[:, :, None]
                h = dA * h + dBx
                y = jnp.einsum('bdn,bn->bd', h, C_t) + D * x_t
                return (h, y)
            h0 = jnp.zeros((x.shape[0], xc.shape[-1], d_state), xc.dtype)
            xs = (jnp.swapaxes(delta, 0, 1), jnp.swapaxes(B_param, 0, 1), jnp.swapaxes(C_param, 0, 1), jnp.swapaxes(xc, 0, 1))
            _, ys = lax.scan(step, h0, xs)
            y = jnp.swapaxes(ys, 0, 1)
            y = y * jax.nn.silu(z)
            y = y @ out_proj_w.T + out_proj_b
            r = y + residual
            mu = jnp.mean(r, axis=-1, keepdims=True)
            var = jnp.mean(jnp.square(r - mu), axis=-1, keepdims=True)
            return (r - mu) * lax.rsqrt(var + LN_EPS) * ln_gamma + ln_beta
        key = jax.random.key(seed)
        ks = jax.random.split(key, 6)
        x = jax.random.normal(ks[0], (BATCH, SEQ, D_MODEL), dtype=jnp.float32)
        in_proj_w = jax.random.normal(ks[1], (2 * D_INNER, D_MODEL), dtype=jnp.float32) * 0.02
        in_proj_b = jnp.zeros((2 * D_INNER,), jnp.float32)
        conv_w = jax.random.normal(ks[2], (D_INNER, 1, D_CONV), dtype=jnp.float32) * 0.2
        conv_b = jnp.zeros((D_INNER,), jnp.float32)
        x_proj_w = jax.random.normal(ks[3], (2 * D_STATE + 1, D_INNER), dtype=jnp.float32) * 0.02
        x_proj_b = jnp.zeros((2 * D_STATE + 1,), jnp.float32)
        A_log = jnp.log(jnp.tile(jnp.arange(1, D_STATE + 1, dtype=jnp.float32)[None, :], (D_INNER, 1)))
        D = jnp.ones((D_INNER,), jnp.float32)
        out_proj_w = jax.random.normal(ks[4], (D_MODEL, D_INNER), dtype=jnp.float32) * 0.02
        out_proj_b = jnp.zeros((D_MODEL,), jnp.float32)
        ln_gamma = jnp.ones((D_MODEL,), jnp.float32)
        ln_beta = jnp.zeros((D_MODEL,), jnp.float32)
        return dict(x=x, in_proj_w=in_proj_w, in_proj_b=in_proj_b, conv_w=conv_w, conv_b=conv_b, x_proj_w=x_proj_w, x_proj_b=x_proj_b, A_log=A_log, D=D, out_proj_w=out_proj_w, out_proj_b=out_proj_b, ln_gamma=ln_gamma, ln_beta=ln_beta)
    _L2_attn_all = _L2_attn_setup()
    _L2_attn_in = {k: v for k, v in _L2_attn_all.items() if k in ('in_proj_w', 'in_proj_b', 'conv_w', 'conv_b', 'x_proj_w', 'x_proj_b', 'A_log', 'D', 'out_proj_w', 'out_proj_b', 'ln_gamma', 'ln_beta')}
    del _L2_attn_all

    def _L2_xattn_setup():
        import jax, jax.numpy as jnp
        import numpy as np
        B, S, H, NH = (4, 256, 128, 16)
        DH = H // NH
        key = jax.random.key(seed)
        ks = jax.random.split(key, 12)
        s = 1.0 / np.sqrt(H)
        return {'query': jax.random.normal(ks[0], (B, S, H), jnp.float32), 'key_value': jax.random.normal(ks[1], (B, S, H), jnp.float32), 'key_ignorance_mask': jax.random.randint(ks[2], (B, S), 0, 2, jnp.int32), 'attention_mask': jax.random.randint(ks[3], (S, S), 0, 2, jnp.int32), 'Wq': jax.random.normal(ks[4], (H, H), jnp.float32) * s, 'bq': jnp.zeros((H,), jnp.float32), 'Wk': jax.random.normal(ks[5], (H, H), jnp.float32) * s, 'bk': jnp.zeros((H,), jnp.float32), 'Wv': jax.random.normal(ks[6], (H, H), jnp.float32) * s, 'bv': jnp.zeros((H,), jnp.float32), 'Wo': jax.random.normal(ks[7], (H, H), jnp.float32) * s, 'bo': jnp.zeros((H,), jnp.float32)}
    _L2_xattn_all = _L2_xattn_setup()
    _L2_xattn_in = {k: v for k, v in _L2_xattn_all.items() if k in ('Wq', 'bq', 'Wk', 'bk', 'Wv', 'bv', 'Wo', 'bo')}
    del _L2_xattn_all

    def _L2_ffn_setup():
        import jax, jax.numpy as jnp
        import numpy as np
        B, T, D, E, FF, K = (4, 128, 128, 8, 256, 2)
        SINKHORN_ITERS = 3

        def _sinkhorn(log_alpha, iters=SINKHORN_ITERS):
            for _ in range(iters):
                log_alpha = log_alpha - jax.nn.logsumexp(log_alpha, axis=-1, keepdims=True)
                log_alpha = log_alpha - jax.nn.logsumexp(log_alpha, axis=-2, keepdims=True)
            gates = jnp.exp(log_alpha)
            return gates / (jnp.sum(gates, axis=-1, keepdims=True) + 1e-08)
        key = jax.random.key(seed)
        ks = jax.random.split(key, 7)
        scale = 0.02
        return {'x': jax.random.normal(ks[0], (B, T, D), dtype=jnp.float32), 'router_w': jax.random.normal(ks[1], (E, D), dtype=jnp.float32) * scale, 'router_b': jnp.zeros((E,), dtype=jnp.float32), 'temperature': jnp.ones((1,), dtype=jnp.float32) * 0.5, 'wg': jax.random.normal(ks[2], (E, D, FF), dtype=jnp.float32) * scale, 'wp': jax.random.normal(ks[3], (E, D, FF), dtype=jnp.float32) * scale, 'wo': jax.random.normal(ks[4], (E, FF, D), dtype=jnp.float32) * scale}
    _L2_ffn_all = _L2_ffn_setup()
    _L2_ffn_in = {k: v for k, v in _L2_ffn_all.items() if k in ('router_w', 'router_b', 'temperature', 'wg', 'wp', 'wo')}
    del _L2_ffn_all

    def _L3_attn_setup():
        import jax, jax.numpy as jnp
        import numpy as np
        HEADS = 16
        DIM = 128
        INNER = DIM
        SCALE = (INNER / HEADS) ** (-0.5)

        def _layernorm(x, gamma, beta, eps=1e-05):
            mu = jnp.mean(x, axis=-1, keepdims=True)
            var = jnp.var(x, axis=-1, keepdims=True)
            return (x - mu) * jax.lax.rsqrt(var + eps) * gamma + beta
        key = jax.random.key(seed)
        k1, k2, k3, k4, k5 = jax.random.split(key, 5)
        B, N = (4, 256)
        x = jax.random.normal(k1, (B, N, DIM), dtype=jnp.float32)
        ln_gamma = jnp.ones((DIM,), dtype=jnp.float32)
        ln_beta = jnp.zeros((DIM,), dtype=jnp.float32)
        w_qkv = jax.random.normal(k2, (DIM, INNER * 3), dtype=jnp.float32) * DIM ** (-0.5)
        w_out = jax.random.normal(k3, (INNER, DIM), dtype=jnp.float32) * INNER ** (-0.5)
        return {'x': x, 'ln_gamma': ln_gamma, 'ln_beta': ln_beta, 'w_qkv': w_qkv, 'w_out': w_out}
    _L3_attn_all = _L3_attn_setup()
    _L3_attn_in = {k: v for k, v in _L3_attn_all.items() if k in ('ln_gamma', 'ln_beta', 'w_qkv', 'w_out')}
    del _L3_attn_all

    def _L3_xattn_setup():
        import jax, jax.numpy as jnp
        import numpy as np
        import math
        B, S, DM, H, DK, DV = (2, 256, 128, 16, 64, 64)
        NEG = -1000000.0
        key = jax.random.key(seed)
        ks = jax.random.split(key, 12)
        inp = {'queries': jax.random.normal(ks[0], (B, S, DM), jnp.float32), 'keys': jax.random.normal(ks[1], (B, S, DM), jnp.float32), 'values': jax.random.normal(ks[2], (B, S, DM), jnp.float32), 'WQ': jax.random.normal(ks[3], (H, DM, DK), jnp.float32) / math.sqrt(DM), 'bQ': jax.random.normal(ks[4], (H, DK), jnp.float32) * 0.02, 'WK': jax.random.normal(ks[5], (H, DM, DK), jnp.float32) / math.sqrt(DM), 'bK': jax.random.normal(ks[6], (H, DK), jnp.float32) * 0.02, 'WV': jax.random.normal(ks[7], (H, DM, DV), jnp.float32) / math.sqrt(DM), 'bV': jax.random.normal(ks[8], (H, DV), jnp.float32) * 0.02, 'WO': jax.random.normal(ks[9], (H * DV, DM), jnp.float32) / math.sqrt(H * DV), 'bO': jax.random.normal(ks[10], (DM,), jnp.float32) * 0.02, 'source_seq_len': jax.random.randint(ks[11], (B,), 1, S + 1).astype(jnp.int64)}
        return inp
    _L3_xattn_all = _L3_xattn_setup()
    _L3_xattn_in = {k: v for k, v in _L3_xattn_all.items() if k in ('WQ', 'bQ', 'WK', 'bK', 'WV', 'bV', 'WO', 'bO')}
    del _L3_xattn_all

    def _L3_ffn_setup():
        import jax, jax.numpy as jnp
        import numpy as np
        B, S, D, F, E, K = (4, 256, 128, 256, 8, 2)
        key = jax.random.key(seed)
        ks = jax.random.split(key, 6)
        scale = 0.02
        return {'x': jax.random.normal(ks[0], (B, S, D), dtype=jnp.float32), 'gate_w': jax.random.normal(ks[1], (D, E), dtype=jnp.float32) * scale, 'w1': jax.random.normal(ks[2], (E, D, F), dtype=jnp.float32) * scale, 'b1': jnp.zeros((E, F), dtype=jnp.float32), 'w2': jax.random.normal(ks[3], (E, F, D), dtype=jnp.float32) * scale, 'b2': jnp.zeros((E, D), dtype=jnp.float32)}
    _L3_ffn_all = _L3_ffn_setup()
    _L3_ffn_in = {k: v for k, v in _L3_ffn_all.items() if k in ('gate_w', 'w1', 'b1', 'w2', 'b2')}
    del _L3_ffn_all
    return {'x': x, 'ctx_1024': ctx_1024, '_lenS2': _lenS2, 'mask_Bx1x1xS2_ik0': mask_Bx1x1xS2_ik0, 'mask_Bx1x1xS2_ff0': mask_Bx1x1xS2_ff0, 'mask_BxS2_ik0': mask_BxS2_ik0, 'mask_SxS2_ik1': mask_SxS2_ik1, 'L0_attn_Wq': _L0_attn_in['Wq'], 'L0_attn_bq': _L0_attn_in['bq'], 'L0_attn_Wk': _L0_attn_in['Wk'], 'L0_attn_bk': _L0_attn_in['bk'], 'L0_attn_Wv': _L0_attn_in['Wv'], 'L0_attn_bv': _L0_attn_in['bv'], 'L0_xattn_wq': _L0_xattn_in['wq'], 'L0_xattn_bq': _L0_xattn_in['bq'], 'L0_xattn_wk': _L0_xattn_in['wk'], 'L0_xattn_bk': _L0_xattn_in['bk'], 'L0_xattn_wv': _L0_xattn_in['wv'], 'L0_xattn_bv': _L0_xattn_in['bv'], 'L0_xattn_wo': _L0_xattn_in['wo'], 'L0_xattn_bo': _L0_xattn_in['bo'], 'L0_ffn_router_w': _L0_ffn_in['router_w'], 'L0_ffn_gate_w': _L0_ffn_in['gate_w'], 'L0_ffn_up_w': _L0_ffn_in['up_w'], 'L0_ffn_down_w': _L0_ffn_in['down_w'], 'L1_attn_wq': _L1_attn_in['wq'], 'L1_attn_w_down': _L1_attn_in['w_down'], 'L1_attn_wk_up': _L1_attn_in['wk_up'], 'L1_attn_wv_up': _L1_attn_in['wv_up'], 'L1_attn_wo': _L1_attn_in['wo'], 'L1_xattn_Wq': _L1_xattn_in['Wq'], 'L1_xattn_bq': _L1_xattn_in['bq'], 'L1_xattn_Wk': _L1_xattn_in['Wk'], 'L1_xattn_bk': _L1_xattn_in['bk'], 'L1_xattn_Wv': _L1_xattn_in['Wv'], 'L1_xattn_bv': _L1_xattn_in['bv'], 'L1_xattn_Wo': _L1_xattn_in['Wo'], 'L1_xattn_bo': _L1_xattn_in['bo'], 'L1_ffn_w_gate': _L1_ffn_in['w_gate'], 'L1_ffn_w_up': _L1_ffn_in['w_up'], 'L1_ffn_w_down': _L1_ffn_in['w_down'], 'L2_attn_in_proj_w': _L2_attn_in['in_proj_w'], 'L2_attn_in_proj_b': _L2_attn_in['in_proj_b'], 'L2_attn_conv_w': _L2_attn_in['conv_w'], 'L2_attn_conv_b': _L2_attn_in['conv_b'], 'L2_attn_x_proj_w': _L2_attn_in['x_proj_w'], 'L2_attn_x_proj_b': _L2_attn_in['x_proj_b'], 'L2_attn_A_log': _L2_attn_in['A_log'], 'L2_attn_D': _L2_attn_in['D'], 'L2_attn_out_proj_w': _L2_attn_in['out_proj_w'], 'L2_attn_out_proj_b': _L2_attn_in['out_proj_b'], 'L2_attn_ln_gamma': _L2_attn_in['ln_gamma'], 'L2_attn_ln_beta': _L2_attn_in['ln_beta'], 'L2_xattn_Wq': _L2_xattn_in['Wq'], 'L2_xattn_bq': _L2_xattn_in['bq'], 'L2_xattn_Wk': _L2_xattn_in['Wk'], 'L2_xattn_bk': _L2_xattn_in['bk'], 'L2_xattn_Wv': _L2_xattn_in['Wv'], 'L2_xattn_bv': _L2_xattn_in['bv'], 'L2_xattn_Wo': _L2_xattn_in['Wo'], 'L2_xattn_bo': _L2_xattn_in['bo'], 'L2_ffn_router_w': _L2_ffn_in['router_w'], 'L2_ffn_router_b': _L2_ffn_in['router_b'], 'L2_ffn_temperature': _L2_ffn_in['temperature'], 'L2_ffn_wg': _L2_ffn_in['wg'], 'L2_ffn_wp': _L2_ffn_in['wp'], 'L2_ffn_wo': _L2_ffn_in['wo'], 'L3_attn_ln_gamma': _L3_attn_in['ln_gamma'], 'L3_attn_ln_beta': _L3_attn_in['ln_beta'], 'L3_attn_w_qkv': _L3_attn_in['w_qkv'], 'L3_attn_w_out': _L3_attn_in['w_out'], 'L3_xattn_WQ': _L3_xattn_in['WQ'], 'L3_xattn_bQ': _L3_xattn_in['bQ'], 'L3_xattn_WK': _L3_xattn_in['WK'], 'L3_xattn_bK': _L3_xattn_in['bK'], 'L3_xattn_WV': _L3_xattn_in['WV'], 'L3_xattn_bV': _L3_xattn_in['bV'], 'L3_xattn_WO': _L3_xattn_in['WO'], 'L3_xattn_bO': _L3_xattn_in['bO'], 'L3_ffn_gate_w': _L3_ffn_in['gate_w'], 'L3_ffn_w1': _L3_ffn_in['w1'], 'L3_ffn_b1': _L3_ffn_in['b1'], 'L3_ffn_w2': _L3_ffn_in['w2'], 'L3_ffn_b2': _L3_ffn_in['b2']}

def reference(x, ctx_1024, _lenS2, mask_Bx1x1xS2_ik0, mask_Bx1x1xS2_ff0, mask_BxS2_ik0, mask_SxS2_ik1, L0_attn_Wq, L0_attn_bq, L0_attn_Wk, L0_attn_bk, L0_attn_Wv, L0_attn_bv, L0_xattn_wq, L0_xattn_bq, L0_xattn_wk, L0_xattn_bk, L0_xattn_wv, L0_xattn_bv, L0_xattn_wo, L0_xattn_bo, L0_ffn_router_w, L0_ffn_gate_w, L0_ffn_up_w, L0_ffn_down_w, L1_attn_wq, L1_attn_w_down, L1_attn_wk_up, L1_attn_wv_up, L1_attn_wo, L1_xattn_Wq, L1_xattn_bq, L1_xattn_Wk, L1_xattn_bk, L1_xattn_Wv, L1_xattn_bv, L1_xattn_Wo, L1_xattn_bo, L1_ffn_w_gate, L1_ffn_w_up, L1_ffn_w_down, L2_attn_in_proj_w, L2_attn_in_proj_b, L2_attn_conv_w, L2_attn_conv_b, L2_attn_x_proj_w, L2_attn_x_proj_b, L2_attn_A_log, L2_attn_D, L2_attn_out_proj_w, L2_attn_out_proj_b, L2_attn_ln_gamma, L2_attn_ln_beta, L2_xattn_Wq, L2_xattn_bq, L2_xattn_Wk, L2_xattn_bk, L2_xattn_Wv, L2_xattn_bv, L2_xattn_Wo, L2_xattn_bo, L2_ffn_router_w, L2_ffn_router_b, L2_ffn_temperature, L2_ffn_wg, L2_ffn_wp, L2_ffn_wo, L3_attn_ln_gamma, L3_attn_ln_beta, L3_attn_w_qkv, L3_attn_w_out, L3_xattn_WQ, L3_xattn_bQ, L3_xattn_WK, L3_xattn_bK, L3_xattn_WV, L3_xattn_bV, L3_xattn_WO, L3_xattn_bO, L3_ffn_gate_w, L3_ffn_w1, L3_ffn_b1, L3_ffn_w2, L3_ffn_b2):
    import jax
    import jax.numpy as jnp

    def _L0_attn_ref(X, Wq, bq, Wk, bk, Wv, bv):
        import jax, jax.numpy as jnp
        import numpy as np
        B, S, D_IN, D_OUT = (4, 256, 128, 128)
        Q = X @ Wq + bq
        K = X @ Wk + bk
        V = X @ Wv + bv
        dk = jnp.sqrt(jnp.asarray(D_OUT, dtype=X.dtype))
        S_ = jnp.einsum('bqd,bkd->bqk', Q, K)
        S_ = jnp.tril(S_) / dk
        A = jax.nn.softmax(S_, axis=2)
        out = jnp.einsum('bqk,bql->bql', A, V)
        return out

    def _L0_xattn_ref(value, key, query, mask, wq, bq, wk, bk, wv, bv, wo, bo):
        import jax, jax.numpy as jnp
        import numpy as np
        import math
        D_MODEL = 128
        HEADS = 16
        D_K = D_MODEL // HEADS
        N, L = (4, 256)
        n, qlen = (query.shape[0], query.shape[1])
        h, dk = (HEADS, D_K)
        v = (value @ wv.T + bv).reshape(n, -1, h, dk).transpose(0, 2, 1, 3)
        k = (key @ wk.T + bk).reshape(n, -1, h, dk).transpose(0, 2, 1, 3)
        q = (query @ wq.T + bq).reshape(n, qlen, h, dk).transpose(0, 2, 1, 3)
        scores = jnp.einsum('nhqd,nhkd->nhqk', q, k)
        scores = jnp.where(mask == 0, jnp.float32(-1000000000.0), scores)
        attn = jax.nn.softmax(scores / math.sqrt(dk), axis=-1)
        out = jnp.einsum('nhqk,nhkd->nhqd', attn, v)
        out = out.transpose(0, 2, 1, 3).reshape(n, qlen, h * dk)
        return out @ wo.T + bo

    def _L0_ffn_ref(x, router_w, gate_w, up_w, down_w):
        import jax, jax.numpy as jnp
        import numpy as np
        TOP_K = 2
        B, S, H = x.shape
        E = router_w.shape[0]
        xf = x.reshape(-1, H)
        logits = xf @ router_w.T
        probs = jax.nn.softmax(logits, axis=-1)
        topk_p, topk_i = jax.lax.top_k(probs, TOP_K)
        topk_p = topk_p / topk_p.sum(axis=-1, keepdims=True)

        def body(out, inputs):
            e, gw, uw, dw = inputs
            sel = topk_i == e
            mask = sel.any(axis=-1)
            w_tok = (topk_p * sel).sum(axis=-1)
            cnt = mask.sum().astype(xf.dtype)
            mean_w = jnp.where(cnt > 0, w_tok.sum() / jnp.maximum(cnt, 1.0), 0.0)
            h = jax.nn.silu(xf @ gw.T) * (xf @ uw.T)
            eo = h @ dw.T
            out = out + mask[:, None].astype(xf.dtype) * eo * mean_w
            return (out, None)
        out0 = jnp.zeros_like(xf)
        out, _ = jax.lax.scan(body, out0, (jnp.arange(E), gate_w, up_w, down_w))
        return out.reshape(B, S, H)

    def _L1_attn_ref(x, wq, w_down, wk_up, wv_up, wo):
        import jax, jax.numpy as jnp
        import numpy as np
        N_HEAD = 16
        PAGE_SIZE = 32
        ROPE_THETA = 10000.0

        def _rope_tables(T, D, dtype):
            inv = 1.0 / ROPE_THETA ** (np.arange(0, D, 2, dtype=np.float32) / D)
            ang = np.outer(np.arange(T, dtype=np.float32), inv)
            return (jnp.asarray(np.cos(ang), dtype), jnp.asarray(np.sin(ang), dtype))

        def _apply_rope(x, cos, sin):
            x1 = x[..., 0::2]
            x2 = x[..., 1::2]
            c = cos[None, :, None, :]
            s = sin[None, :, None, :]
            out = jnp.stack([x1 * c - x2 * s, x1 * s + x2 * c], axis=-1)
            return out.reshape(x.shape)
        B, T, E = x.shape
        H = N_HEAD
        D = E // H
        q = (x @ wq).reshape(B, T, H, D)
        lat = x @ w_down
        k = (lat @ wk_up).reshape(B, T, H, D)
        v = (lat @ wv_up).reshape(B, T, H, D)
        cos, sin = _rope_tables(T, D, x.dtype)
        q = _apply_rope(q, cos, sin)
        k = _apply_rope(k, cos, sin)
        scale = 1.0 / jnp.sqrt(jnp.asarray(D, x.dtype))
        scores = jnp.einsum('bqhd,bkhd->bhqk', q, k) * scale
        pages = jnp.arange(T) // PAGE_SIZE
        allowed = pages[None, :] <= pages[:, None]
        scores = jnp.where(allowed[None, None], scores, jnp.finfo(scores.dtype).min)
        attn = jax.nn.softmax(scores, axis=-1)
        out = jnp.einsum('bhqk,bkhd->bqhd', attn, v).reshape(B, T, E)
        return out @ wo

    def _L1_xattn_ref(q, k, v, padding_mask, Wq, bq, Wk, bk, Wv, bv, Wo, bo):
        import jax, jax.numpy as jnp
        import numpy as np
        B, S, D, H = (2, 256, 128, 16)
        HD = D // H
        b = q.shape[0]
        qh = (q @ Wq + bq).reshape(b, -1, H, HD)
        kh = (k @ Wk + bk).reshape(b, -1, H, HD)
        vh = (v @ Wv + bv).reshape(b, -1, H, HD)
        qk = jnp.einsum('bjhd,bkhd->bhjk', qh, kh) / jnp.sqrt(jnp.float32(HD))
        qk = qk + padding_mask * -1000000000000.0
        attn = jax.nn.softmax(qk, axis=-1)
        qkv = jnp.einsum('bhjk,bkhd->bjhd', attn, vh).reshape(b, -1, D)
        return qkv @ Wo + bo

    def _L1_ffn_ref(x, w_gate, w_up, w_down):
        import jax, jax.numpy as jnp
        import numpy as np
        DIM = 128
        HIDDEN = 384
        SCALE = 1.0 / 127.0

        def _dequant(w_int, dtype):
            return w_int.astype(dtype) * jnp.asarray(SCALE, dtype)
        wg = _dequant(w_gate, x.dtype)
        wu = _dequant(w_up, x.dtype)
        wd = _dequant(w_down, x.dtype)
        gate = jnp.einsum('bsd,hd->bsh', x, wg)
        up = jnp.einsum('bsd,hd->bsh', x, wu)
        h = jax.nn.silu(gate) * up
        return jnp.einsum('bsh,dh->bsd', h, wd)

    def _L2_attn_ref(x, in_proj_w, in_proj_b, conv_w, conv_b, x_proj_w, x_proj_b, A_log, D, out_proj_w, out_proj_b, ln_gamma, ln_beta):
        import jax, jax.numpy as jnp
        from jax import lax
        import numpy as np
        D_MODEL, D_STATE, D_CONV, EXPAND = (128, 16, 4, 2)
        D_INNER = D_MODEL * EXPAND
        BATCH, SEQ = (2, 256)
        LN_EPS = 1e-05

        def _forward(x, in_proj_w, in_proj_b, conv_w, conv_b, x_proj_w, x_proj_b, A_log, D, out_proj_w, out_proj_b, ln_gamma, ln_beta):
            d_state = A_log.shape[1]
            d_conv = conv_w.shape[-1]
            residual = x
            xz = x @ in_proj_w.T + in_proj_b
            x_main, z = jnp.split(xz, 2, axis=-1)
            xc = jnp.transpose(x_main, (0, 2, 1))
            xc = lax.conv_general_dilated(xc, conv_w, window_strides=(1,), padding=[(d_conv - 1, 0)], dimension_numbers=('NCH', 'OIH', 'NCH'), feature_group_count=xc.shape[1])
            xc = xc + conv_b[None, :, None]
            xc = jax.nn.silu(jnp.transpose(xc, (0, 2, 1)))
            ssm = xc @ x_proj_w.T + x_proj_b
            B_param = ssm[..., :d_state]
            C_param = ssm[..., d_state:2 * d_state]
            delta = jax.nn.softplus(ssm[..., -1:])
            A = -jnp.exp(A_log)

            def step(h, ts):
                dt, B_t, C_t, x_t = ts
                dA = jnp.exp(A[None] * dt[:, :, None])
                dBx = dt[:, :, None] * B_t[:, None, :] * x_t[:, :, None]
                h = dA * h + dBx
                y = jnp.einsum('bdn,bn->bd', h, C_t) + D * x_t
                return (h, y)
            h0 = jnp.zeros((x.shape[0], xc.shape[-1], d_state), xc.dtype)
            xs = (jnp.swapaxes(delta, 0, 1), jnp.swapaxes(B_param, 0, 1), jnp.swapaxes(C_param, 0, 1), jnp.swapaxes(xc, 0, 1))
            _, ys = lax.scan(step, h0, xs)
            y = jnp.swapaxes(ys, 0, 1)
            y = y * jax.nn.silu(z)
            y = y @ out_proj_w.T + out_proj_b
            r = y + residual
            mu = jnp.mean(r, axis=-1, keepdims=True)
            var = jnp.mean(jnp.square(r - mu), axis=-1, keepdims=True)
            return (r - mu) * lax.rsqrt(var + LN_EPS) * ln_gamma + ln_beta
        return _forward(x, in_proj_w, in_proj_b, conv_w, conv_b, x_proj_w, x_proj_b, A_log, D, out_proj_w, out_proj_b, ln_gamma, ln_beta)

    def _L2_xattn_ref(query, key_value, key_ignorance_mask, attention_mask, Wq, bq, Wk, bk, Wv, bv, Wo, bo):
        import jax, jax.numpy as jnp
        import numpy as np
        B, S, H, NH = (4, 256, 128, 16)
        DH = H // NH
        b, q_len, _ = query.shape
        k_len = key_value.shape[1]
        NEG = jnp.float32(-1000000000000.0)
        q = (query @ Wq.T + bq) / jnp.sqrt(jnp.float32(DH))
        k = key_value @ Wk.T + bk
        q = q.reshape(b, q_len, NH, DH)
        k = k.reshape(b, k_len, NH, DH)
        scores = jnp.einsum('bqhd,bkhd->bhqk', q, k)
        scores = jnp.where(attention_mask.astype(bool)[None, None, :, :], NEG, scores)
        scores = jnp.where(key_ignorance_mask.astype(bool)[:, None, None, :], NEG, scores)
        attn = jax.nn.softmax(scores, axis=-1)
        attn = jnp.where(jnp.isnan(attn), 0.0, attn)
        v = (key_value @ Wv.T + bv).reshape(b, k_len, NH, DH)
        out = jnp.einsum('bhqk,bkhd->bqhd', attn, v).reshape(b, q_len, H)
        return out @ Wo.T + bo

    def _L2_ffn_ref(x, router_w, router_b, temperature, wg, wp, wo):
        import jax, jax.numpy as jnp
        import numpy as np
        B, T, D, E, FF, K = (4, 128, 128, 8, 256, 2)
        SINKHORN_ITERS = 3

        def _sinkhorn(log_alpha, iters=SINKHORN_ITERS):
            for _ in range(iters):
                log_alpha = log_alpha - jax.nn.logsumexp(log_alpha, axis=-1, keepdims=True)
                log_alpha = log_alpha - jax.nn.logsumexp(log_alpha, axis=-2, keepdims=True)
            gates = jnp.exp(log_alpha)
            return gates / (jnp.sum(gates, axis=-1, keepdims=True) + 1e-08)
        temp = jnp.maximum(temperature, 0.1)
        scores = (jnp.einsum('btd,ed->bte', x, router_w) + router_b) / temp
        gates = _sinkhorn(scores)
        topk_vals, topk_idx = jax.lax.top_k(gates, K)
        topk_gates = topk_vals / (jnp.sum(topk_vals, axis=-1, keepdims=True) + 1e-08)
        g = jax.nn.relu(jnp.einsum('btd,edf->btef', x, wg))
        p = jnp.einsum('btd,edf->btef', x, wp)
        all_out = jnp.einsum('btef,efd->bted', g * p, wo)
        gathered = jnp.take_along_axis(all_out, topk_idx[..., None], axis=2)
        expert_out = jnp.sum(gathered * topk_gates[..., None], axis=2)
        return x + expert_out

    def _L3_attn_ref(x, ln_gamma, ln_beta, w_qkv, w_out):
        import jax, jax.numpy as jnp
        import numpy as np
        HEADS = 16
        DIM = 128
        INNER = DIM
        SCALE = (INNER / HEADS) ** (-0.5)

        def _layernorm(x, gamma, beta, eps=1e-05):
            mu = jnp.mean(x, axis=-1, keepdims=True)
            var = jnp.var(x, axis=-1, keepdims=True)
            return (x - mu) * jax.lax.rsqrt(var + eps) * gamma + beta
        B, N, _ = x.shape
        h = HEADS
        xn = _layernorm(x, ln_gamma, ln_beta)
        qkv = xn @ w_qkv
        q, k, v = jnp.split(qkv, 3, axis=-1)

        def split_heads(t):
            return t.reshape(B, N, h, INNER // h).transpose(0, 2, 1, 3)
        q, k, v = (split_heads(q) * SCALE, split_heads(k), split_heads(v))
        sim = jnp.einsum('bhid,bhjd->bhij', q, k)
        attn = jax.nn.softmax(sim, axis=-1)
        out = jnp.einsum('bhij,bhjd->bhid', attn, v)
        out = out.transpose(0, 2, 1, 3).reshape(B, N, INNER)
        return out @ w_out

    def _L3_xattn_ref(queries, keys, values, WQ, bQ, WK, bK, WV, bV, WO, bO, source_seq_len):
        import jax, jax.numpy as jnp
        import numpy as np
        import math
        B, S, DM, H, DK, DV = (2, 256, 128, 16, 64, 64)
        NEG = -1000000.0
        Bq, Sq, _ = queries.shape
        Sk = keys.shape[1]
        Q = jnp.einsum('bsd,hdk->bhsk', queries, WQ) + bQ[None, :, None, :]
        K = jnp.einsum('btd,hdk->bhtk', keys, WK) + bK[None, :, None, :]
        V = jnp.einsum('btd,hdv->bhtv', values, WV) + bV[None, :, None, :]
        scores = jnp.einsum('bhsk,bhtk->bhst', Q, K) / math.sqrt(Q.shape[-1])
        causal_ok = jnp.arange(Sk)[None, :] <= jnp.arange(Sq)[:, None]
        pad_ok = jnp.arange(Sk)[None, :] < source_seq_len[:, None]
        allowed = causal_ok[None, None, :, :] & pad_ok[:, None, None, :]
        attn = jax.nn.softmax(jnp.where(allowed, scores, NEG), axis=-1)
        heads = jnp.einsum('bhst,bhtv->bhsv', attn, V)
        concat = heads.transpose(0, 2, 1, 3).reshape(Bq, Sq, -1)
        return concat @ WO + bO

    def _L3_ffn_ref(x, gate_w, w1, b1, w2, b2):
        import jax, jax.numpy as jnp
        import numpy as np
        B, S, D, F, E, K = (4, 256, 128, 256, 8, 2)
        gate_logits = jnp.einsum('bsd,de->bse', x, gate_w)
        weights, sel = jax.lax.top_k(gate_logits, K)
        weights = jax.nn.softmax(weights, axis=1)
        out = jnp.zeros_like(x)
        for e in range(E):
            w_e = jnp.sum(weights * (sel == e), axis=-1, keepdims=True)
            h = jax.nn.relu(jnp.einsum('bsd,df->bsf', x, w1[e]) + b1[e])
            y = jnp.einsum('bsf,fd->bsd', h, w2[e]) + b2[e]
            out = out + w_e * y
        return out
    x = x + _L0_attn_ref(_layernorm(x, axis=-1), L0_attn_Wq, L0_attn_bq, L0_attn_Wk, L0_attn_bk, L0_attn_Wv, L0_attn_bv)
    x = x + _L0_xattn_ref(ctx_1024, ctx_1024, _layernorm(x, axis=-1), mask_Bx1x1xS2_ik0, L0_xattn_wq, L0_xattn_bq, L0_xattn_wk, L0_xattn_bk, L0_xattn_wv, L0_xattn_bv, L0_xattn_wo, L0_xattn_bo)
    x = x + _L0_ffn_ref(_layernorm(x, axis=-1), L0_ffn_router_w, L0_ffn_gate_w, L0_ffn_up_w, L0_ffn_down_w)
    x = x + _L1_attn_ref(_layernorm(x, axis=-1), L1_attn_wq, L1_attn_w_down, L1_attn_wk_up, L1_attn_wv_up, L1_attn_wo)
    x = x + _L1_xattn_ref(_layernorm(x, axis=-1), ctx_1024, ctx_1024, mask_Bx1x1xS2_ff0, L1_xattn_Wq, L1_xattn_bq, L1_xattn_Wk, L1_xattn_bk, L1_xattn_Wv, L1_xattn_bv, L1_xattn_Wo, L1_xattn_bo)
    x = x + _L1_ffn_ref(_layernorm(x, axis=-1), L1_ffn_w_gate, L1_ffn_w_up, L1_ffn_w_down)
    x = x + _L2_attn_ref(_layernorm(x, axis=-1), L2_attn_in_proj_w, L2_attn_in_proj_b, L2_attn_conv_w, L2_attn_conv_b, L2_attn_x_proj_w, L2_attn_x_proj_b, L2_attn_A_log, L2_attn_D, L2_attn_out_proj_w, L2_attn_out_proj_b, L2_attn_ln_gamma, L2_attn_ln_beta)
    x = x + _L2_xattn_ref(_layernorm(x, axis=-1), ctx_1024, mask_BxS2_ik0, mask_SxS2_ik1, L2_xattn_Wq, L2_xattn_bq, L2_xattn_Wk, L2_xattn_bk, L2_xattn_Wv, L2_xattn_bv, L2_xattn_Wo, L2_xattn_bo)
    x = x + _L2_ffn_ref(_layernorm(x, axis=-1), L2_ffn_router_w, L2_ffn_router_b, L2_ffn_temperature, L2_ffn_wg, L2_ffn_wp, L2_ffn_wo)
    x = x + _L3_attn_ref(_layernorm(x, axis=-1), L3_attn_ln_gamma, L3_attn_ln_beta, L3_attn_w_qkv, L3_attn_w_out)
    x = x + _L3_xattn_ref(_layernorm(x, axis=-1), ctx_1024, ctx_1024, L3_xattn_WQ, L3_xattn_bQ, L3_xattn_WK, L3_xattn_bK, L3_xattn_WV, L3_xattn_bV, L3_xattn_WO, L3_xattn_bO, _lenS2)
    x = x + _L3_ffn_ref(_layernorm(x, axis=-1), L3_ffn_gate_w, L3_ffn_w1, L3_ffn_b1, L3_ffn_w2, L3_ffn_b2)
    return x

_drawn_inputs = setup_inputs


def setup_inputs(seed=0):
    import zlib

    import numpy as np

    out = dict(_drawn_inputs(seed))
    spreads = {'L1_xattn_bq': (0.0, 0.1),
     'L1_xattn_bk': (0.0, 0.1),
     'L1_xattn_bv': (0.0, 0.445),
     'L1_xattn_bo': (0.0, 0.1),
     'L2_attn_in_proj_b': (0.0, 2.0),
     'L2_attn_conv_b': (0.0, 2.0),
     'L2_attn_x_proj_b': (0.0, 2.0),
     'L2_attn_D': (1.0, 0.6),
     'L2_attn_out_proj_b': (0.0, 2.0),
     'L2_attn_ln_gamma': (1.0, 0.6),
     'L2_attn_ln_beta': (0.0, 2.0),
     'L2_xattn_bq': (0.0, 0.8),
     'L2_xattn_bk': (0.0, 2.0),
     'L2_xattn_bv': (0.0, 0.8),
     'L2_xattn_bo': (0.0, 2.0),
     'L2_ffn_router_b': (0.0, 2.0),
     'L3_attn_ln_gamma': (1.0, 0.6),
     'L3_attn_ln_beta': (0.0, 0.8),
     'L3_ffn_b1': (0.0, 2.0),
     'L3_ffn_b2': (0.0, 2.0)}
    factors = {'L0_attn_Wq': 64.0,
     'L0_attn_bq': 64.0,
     'L0_attn_Wk': 64.0,
     'L0_attn_bk': 64.0,
     'L0_xattn_bk': 64.0,
     'L2_attn_in_proj_w': 8.0,
     'L2_attn_conv_w': 8.0,
     'L2_attn_x_proj_w': 8.0,
     'L2_attn_A_log': 8.0,
     'L2_attn_out_proj_w': 8.0,
     'L2_xattn_Wq': 8.0,
     'L2_xattn_Wk': 8.0,
     'L2_xattn_Wv': 8.0,
     'L2_xattn_Wo': 8.0,
     'L2_ffn_router_w': 8.0,
     'L2_ffn_wg': 8.0,
     'L2_ffn_wp': 8.0,
     'L2_ffn_wo': 8.0,
     'L3_attn_w_qkv': 8.0,
     'L3_attn_w_out': 8.0,
     'L3_xattn_WQ': 8.0,
     'L3_xattn_bQ': 23.66,
     'L3_xattn_WK': 8.0,
     'L3_xattn_bK': 64.0,
     'L3_xattn_WV': 8.0,
     'L3_xattn_bV': 64.0,
     'L3_xattn_WO': 8.0,
     'L3_xattn_bO': 64.0,
     'L3_ffn_gate_w': 64.0,
     'L3_ffn_w1': 64.0,
     'L3_ffn_w2': 64.0}
    for name, (base, spread) in spreads.items():
        noise = np.random.default_rng([zlib.crc32(name.encode()), seed]).standard_normal(out[name].shape)
        drawn = base * np.exp(spread * noise) if base else spread * noise
        out[name] = jnp.asarray(drawn.astype(out[name].dtype))
    for name, factor in factors.items():
        out[name] = (out[name] * factor).astype(out[name].dtype)
    return out
```

```python
from contextlib import ExitStack

import numpy as np

import concourse.bass as bass
from concourse import mybir

F32 = mybir.dt.float32
F32R = mybir.dt.float32r
BF16 = mybir.dt.bfloat16
I32 = mybir.dt.int32
ALU = mybir.AluOpType
ACT = mybir.ActivationFunctionType
AX = mybir.AxisListType.X

P = 128
B, S, S2 = 4, 512, 154
QT = S // P
HEADS = 16
HD = P // HEADS
XHD = 64
KMAIN, KREM = P, S2 - P
KPAD = KMAIN + 32
E8 = 8
EPS = 1e-5
NEG = -1e30
PAGE = 32
LN_BN = 6
GROUP = 4
GROUPS = HEADS // GROUP
MROW, MASKROW = 96, 104
ONEROW = 64



def chunked(a, n):
    return a.reshape(n, P, a.shape[-1]).transpose(1, 0, 2).reshape(P, -1)


def col(a):
    return a.reshape(-1, P).T


def row(a):
    return a.reshape(1, -1)


def swap_pairs(w):
    return w.reshape(w.shape[0], -1, 2)[:, :, ::-1].reshape(w.shape[0], -1)


def quads(a):
    out = np.ones((P, a.shape[1]), a.dtype)
    for j in range(4):
        out[32 * j:32 * j + KREM] = a[KMAIN:]
    return out


def by_group(a):
    out = np.zeros((P, GROUPS, P), a.dtype)
    for h in range(HEADS):
        out[32 * (h % GROUP):32 * (h % GROUP) + HD, h // GROUP] = a[HD * h:HD * (h + 1)]
    return out.reshape(P, -1)


ATTN = {
    "ctxT": (B * KPAD, lambda i: np.pad(i["ctx_1024"].transpose(2, 0, 1), ((0, 0), (0, 0), (0, KPAD - S2))).reshape(P, -1)),
    "a0_wq": (P, lambda i: i["L0_attn_Wq"]), "a0_wk": (P, lambda i: i["L0_attn_Wk"]), "a0_wv": (P, lambda i: i["L0_attn_Wv"]),
    "a0_bq": (1, lambda i: col(i["L0_attn_bq"])), "a0_bk": (1, lambda i: col(i["L0_attn_bk"])), "a0_bv": (P, lambda i: row(i["L0_attn_bv"])),
    "x0_wq": (P, lambda i: i["L0_xattn_wq"].T), "x0_wk": (P, lambda i: i["L0_xattn_wk"].T),
    "x0_wv": (P, lambda i: i["L0_xattn_wv"].T), "x0_wo": (GROUPS * P, lambda i: by_group(i["L0_xattn_wo"].T)),
    "x0_bq": (1, lambda i: col(i["L0_xattn_bq"])), "x0_bk": (1, lambda i: col(i["L0_xattn_bk"])),
    "x0_bv": (P, lambda i: row(i["L0_xattn_bv"])), "x0_bo": (P, lambda i: row(i["L0_xattn_bo"])),
    "f0_router": (E8, lambda i: i["L0_ffn_router_w"].T),
    "a1_wq": (P, lambda i: i["L1_attn_wq"]), "a1_wqs": (P, lambda i: swap_pairs(i["L1_attn_wq"])),
    "a1_down": (64, lambda i: i["L1_attn_w_down"]),
    "a1_wk": (P, lambda i: i["L1_attn_wk_up"]), "a1_wks": (P, lambda i: swap_pairs(i["L1_attn_wk_up"])),
    "a1_wv": (P, lambda i: i["L1_attn_wv_up"]), "a1_wo": (GROUPS * P, lambda i: by_group(i["L1_attn_wo"])),
    "x1_wq": (P, lambda i: i["L1_xattn_Wq"]), "x1_wk": (P, lambda i: i["L1_xattn_Wk"]),
    "x1_wv": (P, lambda i: i["L1_xattn_Wv"]), "x1_wo": (GROUPS * P, lambda i: by_group(i["L1_xattn_Wo"])),
    "x1_bq": (1, lambda i: col(i["L1_xattn_bq"])), "x1_bk": (1, lambda i: col(i["L1_xattn_bk"])),
    "x1_bv": (P, lambda i: row(i["L1_xattn_bv"])), "x1_bo": (P, lambda i: row(i["L1_xattn_bo"])),
    "x1_pad": (B * KPAD, lambda i: np.broadcast_to(np.pad(i["mask_Bx1x1xS2_ff0"].reshape(B, S2), ((0, 0), (0, KPAD - S2))).reshape(1, -1), (P, B * KPAD))),
    "m_in": (4 * P, lambda i: i["L2_attn_in_proj_w"].T), "m_in_b": (4, lambda i: col(i["L2_attn_in_proj_b"])),
    "m_conv": (8, lambda i: chunked(i["L2_attn_conv_w"].reshape(2 * P, 4), 2)), "m_conv_b": (2, lambda i: col(i["L2_attn_conv_b"])),
    "m_xp": (2 * 32, lambda i: chunked(i["L2_attn_x_proj_w"].T[:, 0:32], 2)),
    "m_xp_b": (1, lambda i: i["L2_attn_x_proj_b"][0:32].reshape(32, 1)),
    "m_dt": (2 * P, lambda i: np.repeat(chunked(i["L2_attn_x_proj_w"].T[:, 32:33], 2), P, axis=1)),
    "m_dt_b": (1, lambda i: np.broadcast_to(i["L2_attn_x_proj_b"][32:33].reshape(1, 1), (P, 1))),
    "m_alog": (32, lambda i: chunked(i["L2_attn_A_log"], 2)), "m_d": (2, lambda i: col(i["L2_attn_D"])),
    "m_out": (2 * P, lambda i: chunked(i["L2_attn_out_proj_w"].T, 2)), "m_out_b": (P, lambda i: row(i["L2_attn_out_proj_b"])),
    "m_gamma": (P, lambda i: np.broadcast_to(row(i["L2_attn_ln_gamma"]), (P, P))), "m_beta": (P, lambda i: np.broadcast_to(row(i["L2_attn_ln_beta"]), (P, P))),
    "x2_wq": (P, lambda i: i["L2_xattn_Wq"].T), "x2_wk": (P, lambda i: i["L2_xattn_Wk"].T),
    "x2_wv": (P, lambda i: i["L2_xattn_Wv"].T), "x2_wo": (GROUPS * P, lambda i: by_group(i["L2_xattn_Wo"].T)),
    "x2_bq": (1, lambda i: col(i["L2_xattn_bq"])), "x2_bk": (1, lambda i: col(i["L2_xattn_bk"])),
    "x2_bv": (P, lambda i: row(i["L2_xattn_bv"])), "x2_bo": (P, lambda i: row(i["L2_xattn_bo"])),
    "f2_router": (E8, lambda i: i["L2_ffn_router_w"].T), "f2_router_b": (E8, lambda i: np.broadcast_to(row(i["L2_ffn_router_b"]), (P, E8))),
    "f2_temp": (1, lambda i: np.broadcast_to(i["L2_ffn_temperature"].reshape(1, 1), (P, 1))),
    "a3_g": (P, lambda i: np.broadcast_to(row(i["L3_attn_ln_gamma"]), (P, P))), "a3_b": (P, lambda i: np.broadcast_to(row(i["L3_attn_ln_beta"]), (P, P))),
    "a3_wq": (P, lambda i: i["L3_attn_w_qkv"][:, 0:P]), "a3_wk": (P, lambda i: i["L3_attn_w_qkv"][:, P:2 * P]),
    "a3_wv": (P, lambda i: i["L3_attn_w_qkv"][:, 2 * P:3 * P]), "a3_wo": (GROUPS * P, lambda i: by_group(i["L3_attn_w_out"])),
    "f3_router": (E8, lambda i: i["L3_ffn_gate_w"]),
}
WIDE = {
    "x3_wq": (8 * P, lambda i: i["L3_xattn_WQ"].transpose(1, 0, 2).reshape(P, -1)), "x3_wk": (8 * P, lambda i: i["L3_xattn_WK"].transpose(1, 0, 2).reshape(P, -1)),
    "x3_wv": (8 * P, lambda i: i["L3_xattn_WV"].transpose(1, 0, 2).reshape(P, -1)),
    "x3_bq": (8, lambda i: col(i["L3_xattn_bQ"])), "x3_bk": (8, lambda i: col(i["L3_xattn_bK"])), "x3_bv": (8 * P, lambda i: row(i["L3_xattn_bV"])),
    "x3_wo": (8 * P, lambda i: chunked(i["L3_xattn_WO"], 8)), "x3_bo": (P, lambda i: row(i["L3_xattn_bO"])),
}
FFN0 = {}
for _e in range(E8):
    FFN0[f"g{_e}"] = (512, lambda i, e=_e: i["L0_ffn_gate_w"][e].T)
    FFN0[f"u{_e}"] = (512, lambda i, e=_e: i["L0_ffn_up_w"][e].T)
    FFN0[f"d{_e}"] = (512, lambda i, e=_e: chunked(i["L0_ffn_down_w"][e].T, 4))
FFN2, FFN3 = {}, {}
for _e in range(E8):
    FFN2[f"g{_e}"] = (256, lambda i, e=_e: i["L2_ffn_wg"][e])
    FFN2[f"u{_e}"] = (256, lambda i, e=_e: i["L2_ffn_wp"][e])
    FFN2[f"d{_e}"] = (256, lambda i, e=_e: chunked(i["L2_ffn_wo"][e], 2))
for _e in range(E8):
    FFN3[f"w{_e}"] = (256, lambda i, e=_e: i["L3_ffn_w1"][e])
    FFN3[f"o{_e}"] = (256, lambda i, e=_e: chunked(i["L3_ffn_w2"][e], 2))
    FFN3[f"b{_e}"] = (2, lambda i, e=_e: col(i["L3_ffn_b1"][e]))
FFN3["b2"] = (E8 * P, lambda i: row(i["L3_ffn_b2"]))
FFN1 = {
    "L1_g": (384, lambda i: i["L1_ffn_w_gate"].T), "L1_u": (384, lambda i: i["L1_ffn_w_up"].T), "L1_d": (384, lambda i: chunked(i["L1_ffn_w_down"].T, 3)),
}
INTS = {
    "m0": (B * KPAD, lambda i: np.broadcast_to(np.pad(i["mask_Bx1x1xS2_ik0"].reshape(B, S2), ((0, 0), (0, KPAD - S2))).reshape(1, -1), (P, B * KPAD))),
    "kq": (B * KPAD, lambda i: np.broadcast_to(np.pad(i["mask_BxS2_ik0"], ((0, 0), (0, KPAD - S2))).reshape(1, -1), (P, B * KPAD))),
    "kt": (B, lambda i: i["mask_BxS2_ik0"].T[0:KMAIN]), "kr": (B, lambda i: quads(i["mask_BxS2_ik0"].T)),
    "aq": (QT * KPAD, lambda i: chunked(np.pad(i["mask_SxS2_ik1"], ((0, 0), (0, KPAD - S2))), QT)),
    "at": (S, lambda i: i["mask_SxS2_ik1"].T[0:KMAIN]), "ar": (S, lambda i: quads(i["mask_SxS2_ik1"].T)),
    "len": (B, lambda i: np.broadcast_to(i["_lenS2"].reshape(1, B), (P, B))),
}


def rope():
    inv = 1.0 / 10000.0 ** (np.arange(0, HD, 2, dtype=np.float32) / HD)
    ang = np.outer(np.arange(S, dtype=np.float32), inv)
    cos, sin = np.cos(ang), np.sin(ang)
    c = np.repeat(cos.T, 2, axis=0)
    s = np.stack([-sin.T, sin.T], axis=1).reshape(HD, S)
    return np.tile(c, (HEADS, 1)).astype(np.float32), np.tile(s, (HEADS, 1)).astype(np.float32)


def keys_of_rest():
    return KMAIN + np.arange(P) % 32


CONSTF = {
    "ident": (P, lambda: np.eye(P)), "cos": (S, lambda: rope()[0]), "sin": (S, lambda: rope()[1]),
    "headsel": (HEADS, lambda: np.arange(P)[:, None] // HD == np.arange(HEADS)), "halfsel": (2, lambda: np.arange(P)[:, None] // XHD == np.arange(2)),
    "sums": (GROUP, lambda: np.arange(P)[:, None] == 32 * np.arange(GROUP) + HD), "stackheads": (GROUP, lambda: stack_heads()), "rank": (E8, lambda: np.broadcast_to(E8 - np.arange(E8), (P, E8))), "ones": (P, lambda: np.ones((P, P))),
    "kidx": (KPAD, lambda: np.broadcast_to(np.arange(KPAD), (P, KPAD))), "kcol": (1, lambda: np.arange(P)[:, None]), "krem": (1, lambda: keys_of_rest()[:, None]),
}
CONSTB = {
    "identb": (P, lambda: np.eye(P)), "negi": (P, lambda: NEG * np.eye(P)), "onesb": (S, lambda: np.ones((P, S))),
    "sel": (32 * P, lambda: np.repeat((np.arange(P)[:, None] % 32 == np.arange(32)) & (np.arange(P)[:, None] < 96), P, axis=1)),
    "tril": (QT * S, lambda: chunked(np.tril(np.ones((S, S))), QT)),
    "pageq": (P, lambda: np.arange(P)[None] // PAGE > np.arange(P)[:, None] // PAGE),
    "paget": (P, lambda: np.arange(P)[:, None] // PAGE > np.arange(P)[None] // PAGE),
    "cq": (QT * KPAD, lambda: chunked(np.arange(KPAD)[None] > np.arange(S)[:, None], QT)),
    "ct": (S, lambda: np.arange(P)[:, None] > np.arange(S)[None]),
    "cr": (S, lambda: keys_of_rest()[:, None] > np.arange(S)[None]),
}




def placer(group, targets):
    out = np.zeros((P, P))
    for t in targets:
        out[32 * group + np.arange(32), 32 * t + np.arange(32)] = 1
    return out


def key_rows():
    out = np.zeros((P, P))
    out[0, MASKROW] = out[32, MASKROW + 1] = 1
    out[ONEROW, MROW:MROW + 2 * GROUP] = 1
    return out


def query_rows():
    out = np.zeros((P, P))
    out[ONEROW, MASKROW:MASKROW + 2] = 1
    return out


def stack_heads():
    out = np.zeros((P, GROUP))
    for j in range(GROUP):
        for t in range(3):
            out[32 * t + HD * j:32 * t + HD * (j + 1), j] = 1
        out[MROW + 2 * j:MROW + 2 * j + 2, j] = 1
    out[MASKROW:MASKROW + 2] = 1
    return out


PLACE = {}
for _g in range(GROUPS):
    PLACE[f"q_hi{_g}"] = (P, lambda g=_g: placer(g, (0, 1)))
    PLACE[f"q_lo{_g}"] = (P, lambda g=_g: placer(g, (2,)))
    PLACE[f"k_hi{_g}"] = (P, lambda g=_g: placer(g, (0, 2)))
    PLACE[f"k_lo{_g}"] = (P, lambda g=_g: placer(g, (1,)))
PLACE["key_rows"] = (P, key_rows)
PLACE["query_rows"] = (P, query_rows)


def offsets(table):
    at, out = 0, {}
    for name, (n, _) in table.items():
        out[name] = (at, n)
        at += n
    return out, at



class Sems:

    def __init__(self, nc):
        self.nc, self.by = nc, {}

    def __call__(self, name):
        if name not in self.by:
            self.by[name] = self.nc.alloc_semaphore(name)
        return self.by[name]


class Chain:

    def __init__(self, eng, sem):
        self.eng, self.sem, self.n = eng, sem, 0

    def link(self, ins):
        self.n += 1
        ins.then_inc(self.sem, 1)
        self.eng.wait_ge(self.sem, self.n)


def over(ap, axis, n):
    v = ap.unsqueeze(axis)
    shape = list(v.shape)
    shape[axis] = n
    return v.to_broadcast(shape)


class Net:

    def __init__(self, nc, ctx):
        self.nc, self.ctx = nc, ctx
        self.sem = Sems(nc)
        self.names = 0
        self.x = self.sb("x", [P, B * QT, P])
        self.xnT_all = self.sb("xnT_all", [P, B * S])
        self.logits = self.sb("logits", [P, QT, B, E8])
        self.coef = self.sb("coef", [P, QT, B, E8])
        self.ps = [ctx.enter_context(nc.psum_tensor(f"bank{n}", [P, 512], F32)) for n in range(8)]
        self.weights = {}

    def sb(self, name, shape, dt=F32):
        return self.ctx.enter_context(self.nc.sbuf_tensor(name, shape, dt))

    def table(self, name, table, dt=F32, tile=None):
        offs, n = offsets(table)
        t = self.sb(name, [P, n], dt) if tile is None else tile
        return t, offs, n

    def w(self, name):
        t, (at, n) = self.weights[name]
        return t[:, at:at + n]


def end_of_block(net):
    nums = sorted(s.num for s in net.sem.by.values())
    assert nums[-1] - nums[0] + 1 == len(nums)
    net.nc.vector.sem_clear(range(nums[0], nums[-1] + 1))
    net.nc.all_engine_barrier()



def vector_layernorm(dve, ch, xin, xn, n, done=None):
    for t in range(n.tiles):
        last = dve.bn_stats(n.stats[:, t, :], xin[:, t, :])
    ch.link(last)
    for t in range(n.tiles):
        last = dve.bn_aggr(n.aggr[:, t, :], n.stats[:, t, :])
    ch.link(last)
    ch.link(dve.tensor_scalar(n.var[:], n.aggr[:, :, 1], EPS, None, ALU.add))
    dve.tensor_scalar(n.vh[:], n.var[:], -0.5, None, ALU.mult)
    ch.link(dve.tensor_scalar(n.bits[:], n.var[:].bitcast(I32), 1, None, ALU.logical_shift_right))
    ch.link(dve.tensor_scalar(n.rstd[:].bitcast(I32), n.bits[:], -1.0, float(0x5F3759DF), ALU.mult, ALU.add))
    for _ in range(3):
        ch.link(dve.tensor_tensor(n.sq[:], n.rstd[:], n.rstd[:], ALU.mult))
        ch.link(dve.tensor_tensor(n.sq[:], n.sq[:], n.vh[:], ALU.mult))
        ch.link(dve.scalar_tensor_tensor(n.rstd[:], n.sq[:], 1.5, n.rstd[:], ALU.add, ALU.mult))
    for t in range(n.tiles):
        last = dve.tensor_scalar(xn[:, t, :], xin[:, t, :], n.aggr[:, t, 0:1], n.rstd[:, t:t + 1], ALU.subtract, ALU.mult)
        if done is not None and t % QT == QT - 1:
            last.then_inc(done, 1)
    return last


def tensor_transpose_tiles(pe, out, tiles, ident):
    for t in range(QT):
        last = pe.transpose(out[:, t * P:(t + 1) * P], tiles[:, t, :], ident)
    return last


class Norm:

    def __init__(self, net, sb, tiles=QT):
        self.tiles = tiles
        self.xn = sb("xn", [P, tiles, P])
        self.stats = sb("stats", [P, tiles, LN_BN])
        self.aggr = sb("aggr", [P, tiles, 2])
        self.rstd = sb("rstd", [P, tiles])
        self.var, self.vh, self.sq = sb("var", [P, tiles]), sb("vh", [P, tiles]), sb("sq", [P, tiles])
        self.bits = sb("bits", [P, tiles], I32)
        if tiles == QT:
            self.xnT = sb("xnT", [P, S])


def x_of(net, b):
    return net.x[:, bass.ts(b, QT), :]



def single_head_block(net, b, k):
    nc, sem, ps, w = net.nc, net.sem, net.ps, net.w
    scale = 1.0 / float(np.sqrt(np.float32(P)))
    with nc.Block() as block:

        @block.vector
        def _(dve):
            ch = Chain(dve, sem("dve_chain"))
            vector_layernorm(dve, ch, x_of(net, b), k.n.xn, k.n).then_inc(sem("xn_ready"), 1)
            dve.wait_ge(sem("q_done"), 1)
            dve.tensor_scalar(k.qT[:], ps[0][:], w("a0_bq"), None, ALU.add).then_inc(sem("qT_ready"), 1)
            dve.wait_ge(sem("k_done"), 1)
            dve.tensor_scalar(k.kT[:], ps[1][:], w("a0_bk"), None, ALU.add).then_inc(sem("kT_ready"), 1)
            tril = w("tril").rearrange("p (t k) -> p t k", t=QT)
            for t in range(QT):
                dve.wait_ge(sem("scores_done"), t + 1)
                ch.link(dve.scalar_tensor_tensor(k.s[:, t, :], ps[t][:], scale, tril[:, t, :], ALU.mult, ALU.mult))
                ch.link(dve.reduce_max(k.mx[:, t:t + 1], k.s[:, t, :], AX))
                dve.tensor_scalar(k.negm[:, t:t + 1], k.mx[:, t:t + 1], -1.0, None, ALU.mult).then_inc(sem("negm_ready"), 1)
            dve.wait_ge(sem("exp_done"), QT)
            dve.wait_ge(sem("v_done"), 1)
            ch.link(dve.reciprocal(k.rs[:], k.sum[:]))
            ch.link(dve.tensor_tensor(k.rs[:], k.rs[:], k.sum[:], ALU.mult))
            for t in range(QT):
                last = dve.scalar_tensor_tensor(x_of(net, b)[:, t, :], ps[4][:, t * P:(t + 1) * P], k.rs[:, t:t + 1],
                                                x_of(net, b)[:, t, :], ALU.mult, ALU.add)
            ch.link(last)

        @block.scalar
        def _(act):
            act.wait_ge(sem("xT_done"), 1)
            nc.scalar.copy(k.n.xnT[:], ps[7][:]).then_inc(sem("xnT_ready"), 1)
            for t in range(QT):
                act.wait_ge(sem("negm_ready"), t + 1)
                nc.scalar.activation(k.p[:, t, :], k.s[:, t, :], ACT.Exp, bias=k.negm[:, t:t + 1],
                                     accum_out=k.sum[:, t:t + 1]).then_inc(sem("exp_done"), 1)

        @block.tensor
        def _(pe):
            pe.wait_ge(sem("xn_ready"), 1)
            tensor_transpose_tiles(pe, ps[7], k.n.xn, w("ident")).then_inc(sem("xT_done"), 1)
            pe.wait_ge(sem("xnT_ready"), 1)
            pe.matmul(ps[0][:], w("a0_wq"), k.n.xnT[:], start=True, stop=True).then_inc(sem("q_done"), 1)
            pe.matmul(ps[1][:], w("a0_wk"), k.n.xnT[:], start=True, stop=True).then_inc(sem("k_done"), 1)
            for t in range(QT):
                pe.matmul(ps[4][:, t * P:(t + 1) * P], k.n.xnT[:, t * P:(t + 1) * P], w("a0_wv"), start=True, stop=False)
                last = pe.matmul(ps[4][:, t * P:(t + 1) * P], w("ones")[0:1, :], w("a0_bv")[0:1, :], start=False, stop=True)
            last.then_inc(sem("v_done"), 1)
            pe.wait_ge(sem("qT_ready"), 1)
            pe.wait_ge(sem("kT_ready"), 1)
            for t in range(QT):
                pe.matmul(ps[t][:], k.qT[:, t * P:(t + 1) * P], k.kT[:], start=True, stop=True).then_inc(sem("scores_done"), 1)
    end_of_block(net)



class Heads:

    def __init__(self, net, sb, kind, ctx_keys, wide=False):
        self.kind, self.ctx_keys, self.wide = kind, ctx_keys, wide
        self.dv = XHD if wide else HD
        self.nq = 8 if wide else 1
        self.n = Norm(net, sb)
        self.nk = KPAD if ctx_keys else S
        self.nkt = 1 if ctx_keys else QT
        self.src = sb("src", [P, KPAD]) if ctx_keys else None
        self.qT = sb("qT", [P, self.nq, S])
        self.kk = sb("kk", [P, HEADS, self.nk])
        self.v = sb("v", [P, self.nkt, HEADS, self.dv + 1])
        self.vr = sb("vr", [P, HEADS, self.dv + 1]) if ctx_keys else None
        self.p = sb("p", [P, 3, S])
        self.pr = net.xnT_all[:, 2 * S:4 * S].rearrange("p (c q) -> p c q", c=2)
        self.m = sb("m", [P, QT, HEADS])
        self.r = sb("r", [P, QT, HEADS])
        self.mp = sb("mp", [P, QT, P], BF16)
        self.negm = sb("negm", [P, S], BF16)
        self.rs = sb("rs", [P, QT, HEADS])
        self.o = sb("o", [P, QT, HEADS * self.dv])
        self.oT = net.xnT_all[:, 0:2 * S].rearrange("p (c q) -> p c q", c=2)
        if kind in ("row", "add"):
            self.rowm = sb("rowm", [P, KPAD], BF16)
            self.rf = sb("rf", [P, KPAD])
            self.rb = sb("rb", [P, 3, KPAD], BF16)
        if kind in ("full", "len"):
            self.mq = sb("mq", [P, QT, KPAD], BF16)
            self.mt = sb("mt", [P, S], BF16)
            self.mr = sb("mr", [P, S], BF16)
            self.kf = sb("kf", [P, KPAD])
            self.kc = sb("kc", [P, 2])
            self.lf = sb("lf", [P, 1])
        if kind == "page":
            self.lat = sb("lat", [64, S])
            self.t1 = sb("t1", [P, S])
            self.t2 = sb("t2", [P, S])
            self.kT = sb("kT", [P, S])

    def chunks(self):
        if not self.ctx_keys:
            return [(t, h, 1, (t + 1) * P if self.kind == "page" else S) for t in range(QT) for h in range(HEADS)]
        n = 2 if self.wide else 3
        return [(t, h, min(n, HEADS - h), S2) for t in range(QT) for h in range(0, HEADS, n)]

    def units(self):
        if self.ctx_keys:
            return [u for g in range(HEADS // 4) for u in [("rest", g, 0, 0)] + [("main", h, 0, 0) for h in range(4 * g, 4 * g + 4)]]
        return [("main", h, c, c * P if self.kind == "page" else 0) for h in range(HEADS) for c in range(QT)]


def heads_prepare(net, k):
    with net.nc.Block() as block:

        @block.vector
        def _(dve):
            sem = net.sem("prepared")
            dve.memset(k.mp[:], 0.0).then_inc(sem, 1)
            dve.memset(k.v[:], 1.0).then_inc(sem, 1)
            if k.ctx_keys:
                dve.memset(k.kk[:], 0.0).then_inc(sem, 1)
                dve.memset(k.vr[:], 0.0).then_inc(sem, 1)
            if k.kind in ("row", "add"):
                dve.memset(k.rowm[:], 0.0).then_inc(sem, 1)
            n = 2 + 2 * k.ctx_keys + (k.kind in ("row", "add"))
            dve.wait_ge(sem, n)
            if k.ctx_keys:
                for j in range(4):
                    dve.memset(k.vr[32 * j:32 * j + KREM, j::4, k.dv:k.dv + 1], 1.0).then_inc(sem, 1)
                    n += 1
                if k.kind in ("row", "add"):
                    dve.memset(k.rowm[0:1, S2:KPAD], NEG).then_inc(sem, 1)
                    n += 1
                dve.wait_ge(sem, n)
    end_of_block(net)


def vector_masks(net, dve, ch, k, b):
    w = net.w
    if k.kind == "row":
        m0 = w("m0").rearrange("p (b k) -> p b k", b=B)
        ch.link(dve.tensor_copy(k.rf[:], m0[:, b, :]))
        ch.link(dve.tensor_scalar(k.rowm[0:1, 0:S2], k.rf[0:1, 0:S2], 0.0, NEG, ALU.is_equal, ALU.mult))
    if k.kind == "add":
        pad = w("x1_pad").rearrange("p (b k) -> p b k", b=B)
        ch.link(dve.tensor_scalar(k.rf[:], pad[:, b, :], -1e12, None, ALU.mult))
        for n in range(3):
            ch.link(dve.tensor_copy(k.rb[:, n, :], k.rf[:]))
            ch.link(dve.tensor_copy(k.rowm[32 * n:32 * n + 1, 0:S2], k.rb[32 * n:32 * n + 1, n, 0:S2]))
            if n < 2:
                ch.link(dve.tensor_tensor(k.rf[:], k.rf[:], k.rb[:, n, :], ALU.subtract))
    if k.kind == "full":
        kq = w("kq").rearrange("p (b k) -> p b k", b=B)
        aq = w("aq").rearrange("p (t k) -> p t k", t=QT)
        dve.tensor_scalar(k.kf[:], kq[:, b, :], 0, None, ALU.not_equal)
        dve.tensor_scalar(k.kc[:, 0:1], w("kt")[:, bass.ts(b, 1)], 0, None, ALU.not_equal)
        ch.link(dve.tensor_scalar(k.kc[:, 1:2], w("kr")[:, bass.ts(b, 1)], 0, None, ALU.not_equal))
        for t in range(QT):
            dve.scalar_tensor_tensor(k.mq[:, t, :], aq[:, t, :], 0.0, k.kf[:], ALU.not_equal, ALU.max)
        dve.tensor_scalar(k.mt[:], w("at"), 0.0, k.kc[:, 0:1], ALU.not_equal, ALU.max)
        ch.link(dve.tensor_scalar(k.mr[:], w("ar"), 0.0, k.kc[:, 1:2], ALU.not_equal, ALU.max))
    if k.kind == "len":
        cq = w("cq").rearrange("p (t k) -> p t k", t=QT)
        ch.link(dve.tensor_copy(k.lf[:], w("len")[:, bass.ts(b, 1)]))
        dve.tensor_scalar(k.kf[:], w("kidx"), k.lf[:], None, ALU.is_ge)
        dve.tensor_scalar(k.kc[:, 0:1], w("kcol"), k.lf[:], None, ALU.is_ge)
        ch.link(dve.tensor_scalar(k.kc[:, 1:2], w("krem"), k.lf[:], None, ALU.is_ge))
        for t in range(QT):
            dve.tensor_tensor(k.mq[:, t, :], cq[:, t, :], k.kf[:], ALU.max)
        dve.tensor_scalar(k.mt[:], w("ct"), k.kc[:, 0:1], None, ALU.max)
        ch.link(dve.tensor_scalar(k.mr[:], w("cr"), k.kc[:, 1:2], None, ALU.max))



def heads_block(net, b, k, pre, scale):
    nc, sem, ps, w = net.nc, net.sem, net.ps, net.w
    chunks, units = k.chunks(), k.units()
    mains = [n for n, u in enumerate(units) if u[0] == "main"]
    bias = pre.startswith("x")
    headsel = w("halfsel") if k.wide else w("headsel")
    nchunk = 8 if k.wide else 1

    def v_slot(kt):
        return k.v[:, kt, :, 0:k.dv]

    with nc.Block() as block:

        @block.vector
        def _(dve):
            ch = Chain(dve, sem("dve_chain"))
            last = vector_layernorm(dve, ch, x_of(net, b), k.n.xn, k.n)
            if pre == "a3":
                ch.link(last)
                last = vector_layernorm(dve, ch, k.n.xn, k.n.xn, k.n)
                ch.link(last)
                ch.link(dve.tensor_tensor(k.n.xn[:], k.n.xn[:], over(w("a3_g"), 1, QT), ALU.mult))
                last = dve.tensor_tensor(k.n.xn[:], k.n.xn[:], over(w("a3_b"), 1, QT), ALU.add)
            last.then_inc(sem("xn_ready"), 1)
            vector_masks(net, dve, ch, k, b)
            if k.wide:
                for c in range(8):
                    dve.wait_ge(sem("q_done"), c + 1)
                    dve.tensor_scalar(k.qT[:, c, :], ps[c % 2][:], w("x3_bq")[:, c:c + 1], scale, ALU.add, ALU.mult).then_inc(sem("qT_ready"), 1)
                    dve.wait_ge(sem("k_done"), c + 1)
                    dve.scalar_tensor_tensor(k.kk[:, 2 * c:2 * c + 2, 0:S2], over(ps[2 + c % 2][:, 0:S2], 1, 2), w("x3_bk")[:, c:c + 1],
                                             over(headsel, 2, S2), ALU.add, ALU.mult).then_inc(sem("kk_ready"), 1)
            elif k.kind == "page":
                for name, direct, swapped in (("k", 0, 1), ("q", 2, 3)):
                    dve.wait_ge(sem(f"{name}_done"), 2)
                    s = scale if name == "q" else 1.0
                    dve.scalar_tensor_tensor(k.t1[:], ps[direct][:], s, w("cos"), ALU.mult, ALU.mult)
                    ch.link(dve.scalar_tensor_tensor(k.t2[:], ps[swapped][:], s, w("sin"), ALU.mult, ALU.mult))
                    if name == "q":
                        dve.tensor_tensor(k.qT[:, 0, :], k.t1[:], k.t2[:], ALU.add).then_inc(sem("qT_ready"), 1)
                    else:
                        ch.link(dve.tensor_tensor(k.kT[:], k.t1[:], k.t2[:], ALU.add))
                        dve.tensor_tensor(k.kk[:], over(k.kT[:], 1, HEADS), over(headsel, 2, S), ALU.mult).then_inc(sem("kk_ready"), 1)
            else:
                nk = S2 if k.ctx_keys else S
                dve.wait_ge(sem("q_done"), 1)
                if bias:
                    dve.tensor_scalar(k.qT[:, 0, :], ps[2][:], w(f"{pre}_bq"), scale, ALU.add, ALU.mult).then_inc(sem("qT_ready"), 1)
                else:
                    dve.tensor_scalar(k.qT[:, 0, :], ps[2][:], scale, None, ALU.mult).then_inc(sem("qT_ready"), 1)
                dve.wait_ge(sem("k_done"), 1)
                if bias:
                    dve.scalar_tensor_tensor(k.kk[:, :, 0:nk], over(ps[0][:, 0:nk], 1, HEADS), w(f"{pre}_bk"),
                                             over(headsel, 2, nk), ALU.add, ALU.mult).then_inc(sem("kk_ready"), 1)
                else:
                    dve.tensor_tensor(k.kk[:], over(ps[0][:], 1, HEADS), over(headsel, 2, nk), ALU.mult).then_inc(sem("kk_ready"), 1)
            for i, (t, h, n, nk) in enumerate(chunks):
                dve.wait_ge(sem("scores_done"), i + 1)
                dve.reduce_max(k.m[:, t, h:h + n], ps[3 + i % 2][:, 0:n * nk].rearrange("p (h k) -> p h k", h=n), AX).then_inc(sem("max_done"), 1)
            dve.wait_ge(sem("max_done"), len(chunks))
            ch.link(dve.tensor_scalar(k.mp[:, :, 0:HEADS], k.m[:], -1.0, None, ALU.mult))
            ch.link(dve.scalar_tensor_tensor(k.r[:], k.m[:], -1.0, k.mp[:, :, 0:HEADS], ALU.mult, ALU.subtract))
            ch.link(dve.tensor_copy(k.mp[:, :, 32:32 + HEADS], k.r[:]))
            dve.tensor_tensor(k.mp[:, :, 64:64 + HEADS], k.r[:], k.mp[:, :, 32:32 + HEADS], ALU.subtract).then_inc(sem("mp_ready"), 1)
            if k.wide:
                for h in range(HEADS):
                    dve.wait_ge(sem("pv_done"), h + 1)
                    o = ps[5 + h % 2][:, 0:QT * (XHD + 1)].rearrange("p (t d) -> p t d", t=QT)
                    ch.link(dve.reciprocal(k.rs[:, :, h], o[:, :, XHD]))
                    dve.tensor_tensor(k.o[:, :, h * XHD:(h + 1) * XHD], o[:, :, 0:XHD], over(k.rs[:, :, h], 2, XHD), ALU.mult).then_inc(sem("o_ready"), 1)
            else:
                dve.wait_ge(sem("pv_done"), len(mains))
                for i in range(2):
                    o = ps[5 + i][:, 0:2 * HEADS * (HD + 1)].rearrange("p (t h d) -> p t h d", t=2, h=HEADS)
                    ch.link(dve.reciprocal(k.rs[:, 2 * i:2 * i + 2, :], o[:, :, :, HD]))
                    dve.tensor_tensor(k.o[:, 2 * i:2 * i + 2, :].rearrange("p t (h d) -> p t h d", h=HEADS), o[:, :, :, 0:HD],
                                      over(k.rs[:, 2 * i:2 * i + 2, :], 3, HD), ALU.mult).then_inc(sem("o_ready"), 1)
            dve.wait_ge(sem("y_done"), 1)
            ch.link(dve.tensor_tensor(x_of(net, b), x_of(net, b), ps[3][:].rearrange("p (t d) -> p t d", t=QT), ALU.add))

        @block.gpsimd
        def _(pool):
            if k.ctx_keys:
                ctx = w("ctxT").rearrange("p (b k) -> p b k", b=B)
                nc.gpsimd.tensor_copy(k.src[:], ctx[:, b, :]).then_inc(sem("src_ready"), 1)

        @block.scalar
        def _(act):
            act.wait_ge(sem("xT_done"), 1)
            nc.scalar.copy(k.n.xnT[:], ps[7][:]).then_inc(sem("xnT_ready"), 1)
            if k.kind == "page":
                act.wait_ge(sem("lat_done"), 1)
                nc.scalar.copy(k.lat[:], ps[4][0:64, :]).then_inc(sem("lat_ready"), 1)
            if k.wide:
                for half in range(2):
                    act.wait_ge(sem("v_done"), half + 1)
                    nc.scalar.copy(k.v[:, 0, 8 * half:8 * half + 8, 0:XHD], ps[4][:].rearrange("p (h d) -> p h d", h=8)).then_inc(sem("v_ready"), 1)
                    for j in range(4):
                        rows = slice(32 * j, 32 * j + KREM)
                        nc.scalar.copy(k.vr[rows, 8 * half + j:8 * half + 8:4, 0:XHD],
                                       ps[5][rows, :].rearrange("p (h d) -> p h d", h=8)[:, j::4, :]).then_inc(sem("v_ready"), 1)
            else:
                act.wait_ge(sem("v_done"), 1)
                if k.ctx_keys:
                    nc.scalar.copy(v_slot(0), ps[4][:, 0:P].rearrange("p (h d) -> p h d", h=HEADS)).then_inc(sem("v_ready"), 1)
                    for j in range(4):
                        rows = slice(32 * j, 32 * j + KREM)
                        nc.scalar.copy(k.vr[rows, j::4, 0:HD], ps[4][rows, P:2 * P].rearrange("p (h d) -> p h d", h=HEADS)[:, j::4, :]).then_inc(sem("v_ready"), 1)
                else:
                    for c in range(QT):
                        nc.scalar.copy(v_slot(c), ps[4][:, c * P:(c + 1) * P].rearrange("p (h d) -> p h d", h=HEADS)).then_inc(sem("v_ready"), 1)
            act.wait_ge(sem("mT_done"), 1)
            nc.scalar.copy(k.negm[:], ps[7][:, 0:S // 2].bitcast(BF16)).then_inc(sem("negm_ready"), 1)
            m = 0
            for u, (what, h, kt, q0) in enumerate(units):
                act.wait_ge(sem("st_done"), u + 1)
                if what == "rest":
                    if h >= 2:
                        act.wait_ge(sem("pv_done"), 4 * (h - 1))
                    dst = k.pr[:, h % 2, :]
                else:
                    if m >= 3:
                        act.wait_ge(sem("pv_done"), m - 2)
                    dst = k.p[:, m % 3, q0:S]
                    m += 1
                nc.scalar.activation(dst, ps[u % 3][:, q0:S], ACT.Exp).then_inc(sem("exp_done"), 1)
            for c in range(nchunk):
                act.wait_ge(sem("oT_done"), c + 1)
                if c >= 2:
                    act.wait_ge(sem("oT_used"), c - 1)
                nc.scalar.copy(k.oT[:, c % 2, :], ps[c % 2][:]).then_inc(sem("oT_ready"), 1)

        @block.tensor
        def _(pe):
            pe.wait_ge(sem("xn_ready"), 1)
            tensor_transpose_tiles(pe, ps[7], k.n.xn, w("ident")).then_inc(sem("xT_done"), 1)
            if k.wide:
                pe.wait_ge(sem("src_ready"), 1)
                for half in range(2):
                    cols = slice(512 * half, 512 * half + 512)
                    if half:
                        pe.wait_ge(sem("v_ready"), 5)
                    pe.matmul(ps[4][:], k.src[:, 0:P], w("x3_wv")[:, cols], start=True, stop=False)
                    pe.matmul(ps[4][:], w("ones")[0:1, :], w("x3_bv")[0:1, cols], start=False, stop=True)
                    for j in range(4):
                        pe.matmul(ps[5][32 * j:32 * j + 32, :], k.src[:, P:KPAD], w("x3_wv")[:, cols], start=True, stop=False)
                        last = pe.matmul(ps[5][32 * j:32 * j + 32, :], w("ones")[0:1, 0:32], w("x3_bv")[0:1, cols], start=False, stop=True)
                    last.then_inc(sem("v_done"), 1)
                pe.wait_ge(sem("xnT_ready"), 1)
                for c in range(8):
                    if c >= 2:
                        pe.wait_ge(sem("qT_ready"), c - 1)
                    pe.matmul(ps[c % 2][:], w("x3_wq")[:, c * P:(c + 1) * P], k.n.xnT[:], start=True, stop=True).then_inc(sem("q_done"), 1)
                    if c >= 2:
                        pe.wait_ge(sem("kk_ready"), c - 1)
                    pe.matmul(ps[2 + c % 2][:, 0:KPAD], w("x3_wk")[:, c * P:(c + 1) * P], k.src[:], start=True, stop=True).then_inc(sem("k_done"), 1)
                pe.wait_ge(sem("qT_ready"), 8)
                pe.wait_ge(sem("kk_ready"), 8)
                pe.wait_ge(sem("v_ready"), 10)
            elif k.ctx_keys:
                pe.wait_ge(sem("src_ready"), 1)
                pe.matmul(ps[0][:, 0:KPAD], w(f"{pre}_wk"), k.src[:], start=True, stop=True).then_inc(sem("k_done"), 1)
                pe.matmul(ps[4][:, 0:P], k.src[:, 0:P], w(f"{pre}_wv"), start=True, stop=False)
                pe.matmul(ps[4][:, 0:P], w("ones")[0:1, :], w(f"{pre}_bv")[0:1, :], start=False, stop=True)
                for j in range(4):
                    pe.matmul(ps[4][32 * j:32 * j + 32, P:2 * P], k.src[:, P:KPAD], w(f"{pre}_wv"), start=True, stop=False)
                    last = pe.matmul(ps[4][32 * j:32 * j + 32, P:2 * P], w("ones")[0:1, 0:32], w(f"{pre}_bv")[0:1, :], start=False, stop=True)
                last.then_inc(sem("v_done"), 1)
                pe.wait_ge(sem("xnT_ready"), 1)
                pe.matmul(ps[2][:], w(f"{pre}_wq"), k.n.xnT[:], start=True, stop=True).then_inc(sem("q_done"), 1)
                pe.wait_ge(sem("v_ready"), 5)
            elif k.kind == "page":
                pe.wait_ge(sem("xnT_ready"), 1)
                pe.matmul(ps[4][0:64, :], w("a1_down"), k.n.xnT[:], start=True, stop=True).then_inc(sem("lat_done"), 1)
                pe.matmul(ps[2][:], w("a1_wq"), k.n.xnT[:], start=True, stop=True).then_inc(sem("q_done"), 1)
                pe.matmul(ps[3][:], w("a1_wqs"), k.n.xnT[:], start=True, stop=True).then_inc(sem("q_done"), 1)
                pe.wait_ge(sem("lat_ready"), 1)
                pe.matmul(ps[0][:], w("a1_wk")[0:64, :], k.lat[:], start=True, stop=True).then_inc(sem("k_done"), 1)
                pe.matmul(ps[1][:], w("a1_wks")[0:64, :], k.lat[:], start=True, stop=True).then_inc(sem("k_done"), 1)
                for c in range(QT):
                    last = pe.matmul(ps[4][:, c * P:(c + 1) * P], k.lat[:, c * P:(c + 1) * P], w("a1_wv")[0:64, :], start=True, stop=True)
                last.then_inc(sem("v_done"), 1)
                pe.wait_ge(sem("v_ready"), QT)
            else:
                pe.wait_ge(sem("xnT_ready"), 1)
                pe.matmul(ps[0][:], w(f"{pre}_wk"), k.n.xnT[:], start=True, stop=True).then_inc(sem("k_done"), 1)
                pe.matmul(ps[2][:], w(f"{pre}_wq"), k.n.xnT[:], start=True, stop=True).then_inc(sem("q_done"), 1)
                for c in range(QT):
                    last = pe.matmul(ps[4][:, c * P:(c + 1) * P], k.n.xnT[:, c * P:(c + 1) * P], w(f"{pre}_wv"), start=True, stop=True)
                last.then_inc(sem("v_done"), 1)
                pe.wait_ge(sem("v_ready"), QT)
            if not k.wide:
                pe.wait_ge(sem("qT_ready"), 1)
                pe.wait_ge(sem("kk_ready"), 1)

            for i, (t, h, n, nk) in enumerate(chunks):
                if i >= 2:
                    pe.wait_ge(sem("max_done"), i - 1)
                out = ps[3 + i % 2][:, 0:n * nk]
                masked = k.kind not in (None, "page")
                c = h // 2 if k.wide else 0
                last = pe.matmul(out.rearrange("p (h k) -> p h k", h=n), k.qT[:, c, t * P:(t + 1) * P], k.kk[:, h:h + n, 0:nk],
                                 start=True, stop=not masked)
                if k.kind in ("row", "add"):
                    last = pe.matmul(out.rearrange("p (h k) -> p h k", h=n), w("onesb")[:, 0:P], over(k.rowm[:, 0:nk], 1, n), start=False, stop=True)
                if k.kind in ("full", "len"):
                    last = pe.matmul(out.rearrange("p (h k) -> p h k", h=n), w("negi"), over(k.mq[:, t, 0:nk], 1, n), start=False, stop=True)
                if k.kind == "page":
                    last = pe.matmul(out[:, t * P:(t + 1) * P], w("negi"), w("pageq"), start=False, stop=True, skip_group_check=True)
                last.then_inc(sem("scores_done"), 1)

            pe.wait_ge(sem("mp_ready"), 1)
            mT = ps[7][:, 0:S // 2].bitcast(BF16)
            tensor_transpose_tiles(pe, mT, k.mp, w("identb")).then_inc(sem("mT_done"), 1)
            pe.wait_ge(sem("negm_ready"), 1)

            def second_scores(u):
                what, h, kt, q0 = units[u]
                if u >= 3:
                    pe.wait_ge(sem("exp_done"), u - 2)
                bank = ps[u % 3]
                heads = [(4 * h + j, slice(32 * j, 32 * j + 32), slice(KMAIN, KPAD), 32) for j in range(4)] if what == "rest" \
                    else [(h, slice(0, P), slice(kt * P, (kt + 1) * P), P)]
                for hh, rows, keys, width in heads:
                    out = bank[rows, q0:S]
                    pe.matmul(out, k.kk[:, hh, keys], k.qT[:, hh // 2 if k.wide else 0, q0:S], start=True, stop=False)
                    last = pe.matmul(out, w("sel")[:, hh * P:hh * P + width], k.negm[:, q0:S], start=False, stop=k.kind in (None, "page"))
                    if k.kind in ("row", "add"):
                        last = pe.matmul(out, k.rowm[:, keys], w("onesb")[:, q0:S], start=False, stop=True)
                    if k.kind in ("full", "len"):
                        last = pe.matmul(out, w("negi")[:, rows], (k.mr if what == "rest" else k.mt)[:, q0:S], start=False, stop=True)
                    if k.kind == "page":
                        last = pe.matmul(bank[:, kt * P:(kt + 1) * P], w("negi"), w("paget"), start=False, stop=True, skip_group_check=True)
                last.then_inc(sem("st_done"), 1)

            def products(m):
                u = mains[m]
                _, h, kt, q0 = units[u]
                pe.wait_ge(sem("exp_done"), u + 1)
                if k.wide and h >= 2:
                    pe.wait_ge(sem("o_ready"), h - 1)
                for t in range(q0 // P, QT):
                    if k.wide:
                        bank, at, first = ps[5 + h % 2], t * (XHD + 1), t == 0
                    else:
                        bank, at, first = ps[5 + t // 2], (t % 2) * HEADS * (HD + 1) + h * (HD + 1), m == 0 and t % 2 == 0
                    out = bank[:, at:at + k.dv + 1]
                    if k.ctx_keys:
                        pe.matmul(out, k.pr[:, h // 4 % 2, t * P:(t + 1) * P], k.vr[:, h, :],
                                  start=first, stop=False, skip_group_check=True)
                        first = False
                    last = pe.matmul(out, k.p[:, m % 3, t * P:(t + 1) * P], k.v[:, kt, h, :], start=first, stop=True, skip_group_check=True)
                last.then_inc(sem("pv_done"), 1)

            m = 0
            for u in range(len(units) + 2):
                if u < len(units):
                    second_scores(u)
                if m < len(mains) and mains[m] <= u - 2:
                    products(m)
                    m += 1

            pe.wait_ge(sem("o_ready"), HEADS if k.wide else 2)
            for c in range(nchunk + 1):
                if c < nchunk:
                    if c >= 2:
                        pe.wait_ge(sem("oT_ready"), c - 1)
                    for t in range(QT):
                        last = pe.transpose(ps[c % 2][:, t * P:(t + 1) * P], k.o[:, t, c * P:(c + 1) * P], w("ident"))
                    last.then_inc(sem("oT_done"), 1)
                if c >= 1:
                    pe.wait_ge(sem("oT_ready"), c)
                    for t in range(QT):
                        last = pe.matmul(ps[3][:, t * P:(t + 1) * P], k.oT[:, (c - 1) % 2, t * P:(t + 1) * P], w(f"{pre}_wo")[:, (c - 1) * P:c * P],
                                         start=(c == 1 and t == 0), stop=(c == nchunk), skip_group_check=True)
                    if c < nchunk or bias:
                        last.then_inc(sem("oT_used"), 1)
            if bias:
                for t in range(QT):
                    last = pe.matmul(ps[3][:, t * P:(t + 1) * P], w("ones")[0:1, :], w(f"{pre}_bo")[0:1, :], start=False, stop=True, skip_group_check=True)
            last.then_inc(sem("y_done"), 1)
    end_of_block(net)



class Narrow:

    def __init__(self, net, sb, kind, ctx_keys):
        self.kind, self.ctx_keys = kind, ctx_keys
        self.nk = KPAD if ctx_keys else S
        self.nkt = 1 if ctx_keys else QT
        self.q_hi, self.q_lo = sb("q_hi", [P, B * S], F32R), sb("q_lo", [P, B * S], F32R)
        self.k_hi, self.k_lo = sb("k_hi", [P, B * self.nk], F32R), sb("k_lo", [P, B * self.nk], F32R)
        self.values = sb("values", [P, B * self.nkt * P])
        self.rests = sb("rests", [P, B * P]) if ctx_keys else None

    def more_buffers(self, net, sb):
        self.rows = sb("rows", [P, self.nk], F32R)
        self.Q = sb("Q", [P, 2, S], F32R)
        self.K = sb("K", [P, 2, GROUP, self.nk], F32R)
        self.v = sb("v", [P, self.nkt, HEADS, 32])
        self.p = sb("p", [P, 3, S])
        self.m = sb("m", [P, QT, HEADS])
        self.mp = sb("mp", [P, 2, QT, P], F32R)
        self.o = sb("o", [P, 2, S])
        self.rs = sb("rs", [P, QT * GROUP])
        self.rx = sb("rx", [P, QT, P])
        if self.kind in ("row", "add"):
            self.ones = sb("ones", [P, S], F32R)
        if self.ctx_keys:
            self.kr = sb("kr", [P, 2, GROUP, KPAD - KMAIN], F32R)
            self.vr = sb("vr", [P, GROUPS, P])
            self.rf = sb("rf", [P, KPAD])
            self.rb = sb("rb", [P, 2, KPAD], F32R) if self.kind == "add" else None
        if self.kind == "full":
            self.mq = sb("mq", [P, QT, KPAD], BF16)
            self.mt = sb("mt", [P, S], BF16)
            self.mr = sb("mr", [P, S], BF16)
            self.kc = sb("kc", [P, 2])

    def chunks(self, g):
        if self.ctx_keys:
            return [(t, h, 2, S2) for t in range(QT) for h in (GROUP * g, GROUP * g + 2)]
        return [(t, h, 1, (t + 1) * P if self.kind == "page" else S) for t in range(QT) for h in range(GROUP * g, GROUP * (g + 1))]

    def units(self, g):
        if self.ctx_keys:
            return [("rest", g, 0, 0)] + [("main", h, 0, 0) for h in range(GROUP * g, GROUP * (g + 1))]
        return [("main", h, c, c * P if self.kind == "page" else 0) for h in range(GROUP * g, GROUP * (g + 1)) for c in range(QT)]


def narrow_project(net, k, pre, scale, sb):
    nc, sem, ps, w = net.nc, net.sem, net.ps, net.w
    n = Norm(net, sb, B * QT)
    full = sb("full", [P, 2, S])
    if k.kind == "page":
        lat, turned = sb("lat", [64, B * S]), sb("turned", [P, 2, S])
    bias = pre.startswith("x")
    xnT = net.xnT_all
    with nc.Block() as block:

        @block.vector
        def _(dve):
            ch = Chain(dve, sem("dve_chain"))
            if pre == "a3":
                ch.link(vector_layernorm(dve, ch, net.x, n.xn, n))
                ch.link(vector_layernorm(dve, ch, n.xn, n.xn, n))
                for b in range(B):
                    tiles = n.xn[:, b * QT:(b + 1) * QT, :]
                    ch.link(dve.tensor_tensor(tiles, tiles, over(w("a3_g"), 1, QT), ALU.mult))
                    dve.tensor_tensor(tiles, tiles, over(w("a3_b"), 1, QT), ALU.add).then_inc(sem("xn_ready"), 1)
            else:
                vector_layernorm(dve, ch, net.x, n.xn, n, sem("xn_ready"))
            for b in range(B):
                for i, (name, hi, lo, m) in enumerate((("k", k.k_hi, k.k_lo, k.nk), ("q", k.q_hi, k.q_lo, S))):
                    s = scale if name == "q" else 1.0
                    out, at = full[:, i, 0:m], slice(b * m, (b + 1) * m)
                    dve.wait_ge(sem(f"{name}_done"), b + 1)
                    if k.kind == "page":
                        dve.scalar_tensor_tensor(turned[:, 0, :], ps[2 * i][:], s, w("cos"), ALU.mult, ALU.mult)
                        ch.link(dve.scalar_tensor_tensor(turned[:, 1, :], ps[2 * i + 1][:], s, w("sin"), ALU.mult, ALU.mult))
                        ch.link(dve.tensor_tensor(out, turned[:, 0, :], turned[:, 1, :], ALU.add))
                    elif bias:
                        ch.link(dve.tensor_scalar(out, ps[2 * i][:, 0:m], w(f"{pre}_b{name}"), s, ALU.add, ALU.mult))
                    else:
                        ch.link(dve.tensor_scalar(out, ps[2 * i][:, 0:m], s, None, ALU.mult))
                    ch.link(dve.tensor_copy(hi[:, at], out))
                    dve.tensor_tensor(lo[:, at], out, hi[:, at].bitcast(F32), ALU.subtract).then_inc(sem(f"{name}_parts"), 1)

        @block.scalar
        def _(act):
            for b in range(B):
                act.wait_ge(sem("xT_done"), b + 1)
                nc.scalar.copy(xnT[:, b * S:(b + 1) * S], ps[6 + b % 2][:]).then_inc(sem("xnT_ready"), 1)
                if k.kind == "page":
                    act.wait_ge(sem("lat_done"), b + 1)
                    nc.scalar.copy(lat[:, b * S:(b + 1) * S], ps[6 + b % 2][0:64, :]).then_inc(sem("lat_ready"), 1)
                act.wait_ge(sem("v_done"), b + 1)
                if k.ctx_keys:
                    nc.scalar.copy(k.values[:, b * P:(b + 1) * P], ps[4 + b % 2][:, 0:P])
                    nc.scalar.copy(k.rests[:, b * P:(b + 1) * P], ps[4 + b % 2][:, P:2 * P]).then_inc(sem("v_kept"), 1)
                else:
                    nc.scalar.copy(k.values[:, b * S:(b + 1) * S], ps[4 + b % 2][:]).then_inc(sem("v_kept"), 1)

        @block.tensor
        def _(pe):
            ctx = w("ctxT").rearrange("p (b k) -> p b k", b=B)

            def values(b, at, src, bias):
                pe.matmul(ps[4 + b % 2][at], src, w(f"{pre}_wv")[0:src.shape[0], :], start=True, stop=not bias)

            for b in range(B):
                pe.wait_ge(sem("xn_ready"), b + 1)
                if b >= 2:
                    pe.wait_ge(sem("lat_ready" if k.kind == "page" else "xnT_ready"), b - 1)
                tensor_transpose_tiles(pe, ps[6 + b % 2], n.xn[:, b * QT:(b + 1) * QT, :], w("ident")).then_inc(sem("xT_done"), 1)
                pe.wait_ge(sem("xnT_ready"), b + 1)
                x = xnT[:, b * S:(b + 1) * S]
                if b >= 1:
                    pe.wait_ge(sem("q_parts"), b)
                if k.kind == "page":
                    pe.matmul(ps[6 + b % 2][0:64, :], w("a1_down"), x, start=True, stop=True).then_inc(sem("lat_done"), 1)
                    pe.matmul(ps[2][:], w("a1_wq"), x, start=True, stop=True)
                    pe.matmul(ps[3][:], w("a1_wqs"), x, start=True, stop=True).then_inc(sem("q_done"), 1)
                    pe.wait_ge(sem("lat_ready"), b + 1)
                    src = lat[:, b * S:(b + 1) * S]
                    pe.matmul(ps[0][:], w("a1_wk")[0:64, :], src, start=True, stop=True)
                    pe.matmul(ps[1][:], w("a1_wks")[0:64, :], src, start=True, stop=True).then_inc(sem("k_done"), 1)
                else:
                    pe.matmul(ps[0][:, 0:k.nk], w(f"{pre}_wk"), ctx[:, b, :] if k.ctx_keys else x, start=True, stop=True).then_inc(sem("k_done"), 1)
                    pe.matmul(ps[2][:], w(f"{pre}_wq"), x, start=True, stop=True).then_inc(sem("q_done"), 1)
                    src = x
                if b >= 2:
                    pe.wait_ge(sem("v_kept"), b - 1)
                out = ps[4 + b % 2]
                if k.ctx_keys:
                    pe.matmul(out[:, 0:P], ctx[:, b, 0:P], w(f"{pre}_wv"), start=True, stop=False)
                    pe.matmul(out[:, 0:P], w("ones")[0:1, :], w(f"{pre}_bv")[0:1, :], start=False, stop=True)
                    for j in range(GROUP):
                        rows = out[32 * j:32 * j + 32, P:2 * P]
                        pe.matmul(rows, ctx[:, b, P:KPAD], w(f"{pre}_wv"), start=True, stop=False)
                        last = pe.matmul(rows, w("ones")[0:1, 0:32], w(f"{pre}_bv")[0:1, :], start=False, stop=True)
                else:
                    for c in range(QT):
                        last = pe.matmul(out[:, c * P:(c + 1) * P], src[:, c * P:(c + 1) * P], w(f"{pre}_wv")[0:src.shape[0], :], start=True, stop=True)
                last.then_inc(sem("v_done"), 1)
    end_of_block(net)


def narrow_prepare(net, k):
    with net.nc.Block() as block:

        @block.vector
        def _(dve):
            ch = Chain(dve, net.sem("dve_chain"))
            dve.memset(k.mp[:].bitcast(F32), 0.0)
            dve.memset(k.rows[:].bitcast(F32), 0.0)
            if k.kind in ("row", "add"):
                dve.memset(k.ones[:].bitcast(F32), 0.0)
            if k.ctx_keys:
                dve.memset(k.vr[:], 0.0)
            ch.link(dve.memset(k.v[:], 0.0))
            dve.memset(k.v[:, :, :, HD:HD + 1], 1.0)
            dve.memset(k.rows[ONEROW:ONEROW + 1, :].bitcast(F32), 1.0)
            if k.kind in ("row", "add"):
                dve.memset(k.mp[:, :, :, MASKROW:MASKROW + 2].bitcast(F32), 1.0)
                dve.memset(k.ones[ONEROW:ONEROW + 1, :].bitcast(F32), 1.0)
            if k.ctx_keys:
                for j in range(GROUP):
                    dve.memset(k.vr[32 * j:32 * j + KREM, :, 32 * j + HD:32 * j + HD + 1], 1.0)
            last = dve.memset(k.m[:], 0.0)
            if k.kind in ("row", "add"):
                last = dve.memset(k.rows[0:1, S2:KPAD].bitcast(F32), NEG)
            ch.link(last)
    end_of_block(net)


def vector_narrow_masks(net, dve, ch, k, b):
    w = net.w
    if k.kind == "row":
        m0 = w("m0").rearrange("p (b k) -> p b k", b=B)
        ch.link(dve.tensor_copy(k.rf[:], m0[:, b, :]))
        dve.tensor_scalar(k.rows[0:1, 0:S2], k.rf[0:1, 0:S2], 0.0, NEG, ALU.is_equal, ALU.mult).then_inc(net.sem("masks_ready"), 1)
    if k.kind == "add":
        pad = w("x1_pad").rearrange("p (b k) -> p b k", b=B)
        ch.link(dve.tensor_scalar(k.rf[:], pad[:, b, :], -1e12, None, ALU.mult))
        ch.link(dve.tensor_copy(k.rb[:, 0, :], k.rf[:]))
        ch.link(dve.tensor_tensor(k.rb[:, 1, :], k.rf[:], k.rb[:, 0, :].bitcast(F32), ALU.subtract))
        for n in range(2):
            last = dve.tensor_copy(k.rows[32 * n:32 * n + 1, 0:S2], k.rb[32 * n:32 * n + 1, n, 0:S2].bitcast(F32))
        last.then_inc(net.sem("masks_ready"), 1)
    if k.kind == "full":
        kq = w("kq").rearrange("p (b k) -> p b k", b=B)
        aq = w("aq").rearrange("p (t k) -> p t k", t=QT)
        dve.tensor_scalar(k.rf[:], kq[:, b, :], 0, None, ALU.not_equal)
        dve.tensor_scalar(k.kc[:, 0:1], w("kt")[:, bass.ts(b, 1)], 0, None, ALU.not_equal)
        ch.link(dve.tensor_scalar(k.kc[:, 1:2], w("kr")[:, bass.ts(b, 1)], 0, None, ALU.not_equal))
        for t in range(QT):
            dve.scalar_tensor_tensor(k.mq[:, t, :], aq[:, t, :], 0.0, k.rf[:], ALU.not_equal, ALU.max)
        dve.tensor_scalar(k.mt[:], w("at"), 0.0, k.kc[:, 0:1], ALU.not_equal, ALU.max)
        dve.tensor_scalar(k.mr[:], w("ar"), 0.0, k.kc[:, 1:2], ALU.not_equal, ALU.max).then_inc(net.sem("masks_ready"), 1)



def narrow_block(net, b, k, pre):
    nc, sem, ps, w = net.nc, net.sem, net.ps, net.w
    bias = pre.startswith("x")
    nk = k.nk
    units = [u for g in range(GROUPS) for u in k.units(g)]
    per_group = len(units) // GROUPS
    nchunks = len(k.chunks(0))
    oT = net.xnT_all[:].rearrange("p (g q) -> p g q", g=GROUPS)

    with nc.Block() as block:

        @block.vector
        def _(dve):
            ch = Chain(dve, sem("dve_chain"))
            vector_narrow_masks(net, dve, ch, k, b)

            def stack_keys(g):
                if g >= 2:
                    dve.wait_ge(sem("st_done"), per_group * (g - 1))
                dve.wait_ge(sem("k_stacked"), g + 1)
                if k.ctx_keys:
                    dve.tensor_tensor(k.kr[:, g % 2], over(ps[7][:, KMAIN:KPAD], 1, GROUP), over(w("stackheads"), 2, KPAD - KMAIN), ALU.mult)
                dve.tensor_tensor(k.K[:, g % 2], over(ps[7][:, 0:nk], 1, GROUP), over(w("stackheads"), 2, nk), ALU.mult).then_inc(sem("K_ready"), 1)

            def normalise(g):
                dve.wait_ge(sem("sums_done"), g + 1)
                ch.link(dve.reciprocal(k.rs[:], ps[5 + g % 2][:, 0:QT * GROUP]))
                dve.tensor_copy(k.rx[:].rearrange("p t (j r) -> p (t j) r", j=GROUP), over(k.rs[:], 2, 32)).then_inc(sem("rx_ready"), 1)
                dve.wait_ge(sem("factors_done"), g + 1)
                dve.tensor_tensor(oT[:, g, :], k.o[:, g % 2, :], ps[5 + g % 2][:], ALU.mult).then_inc(sem("oT_ready"), 1)

            for g in range(GROUPS):
                stack_keys(g)
                for i, (t, h, n, keys) in enumerate(k.chunks(g), nchunks * g):
                    dve.wait_ge(sem("scores_done"), i + 1)
                    dve.reduce_max(k.m[:, t, h:h + n], ps[3 + i % 2][:, 0:n * keys].rearrange("p (h k) -> p h k", h=n), AX).then_inc(sem("max_done"), 1)
                dve.wait_ge(sem("max_done"), nchunks * (g + 1))
                if g >= 2:
                    dve.wait_ge(sem("mT_done"), g - 1)
                hi = k.mp[:, g % 2, :, MROW:MROW + 2 * GROUP:2]
                lo = k.mp[:, g % 2, :, MROW + 1:MROW + 2 * GROUP:2]
                top = k.m[:, :, GROUP * g:GROUP * (g + 1)]
                ch.link(dve.tensor_scalar(hi, top, -1.0, None, ALU.mult))
                dve.scalar_tensor_tensor(lo, top, -1.0, hi.bitcast(F32), ALU.mult, ALU.subtract).then_inc(sem("mp_ready"), 1)
                if g >= 2:
                    normalise(g - 2)
            normalise(GROUPS - 2)
            normalise(GROUPS - 1)
            dve.wait_ge(sem("y_done"), 1)
            ch.link(dve.tensor_tensor(x_of(net, b), x_of(net, b), ps[3][:].rearrange("p (t d) -> p t d", t=QT), ALU.add))

        @block.gpsimd
        def _(pool):
            values = k.values[:, bass.ts(b, k.nkt * P)].rearrange("p (c h d) -> p c h d", c=k.nkt, h=HEADS)
            nc.gpsimd.tensor_copy(k.v[:, :, :, 0:HD], values).then_inc(sem("v_ready"), 1)
            if k.ctx_keys:
                rests = k.rests[:, bass.ts(b, P)].rearrange("p (g j d) -> p g j d", g=GROUPS, j=GROUP)
                for j in range(GROUP):
                    pool.wait_ge(sem("v_ready"), j + 1)
                    rows = slice(32 * j, 32 * j + KREM)
                    nc.gpsimd.tensor_copy(k.vr[rows, :, 32 * j:32 * j + HD], rests[rows, :, j, :]).then_inc(sem("v_ready"), 1)

        @block.scalar
        def _(act):
            def copy_queries(g):
                act.wait_ge(sem("q_stacked"), g + 1)
                nc.scalar.copy(k.Q[:, g % 2, :], ps[2][:]).then_inc(sem("Q_ready"), 1)

            def copy_maxima(g):
                act.wait_ge(sem("mT_done"), g + 1)
                nc.scalar.copy(k.Q[MROW:P, g % 2, :], ps[7][MROW:P, :]).then_inc(sem("maxima_in"), 1)

            def copy_products(g):
                act.wait_ge(sem("pv_done"), per_group * (g + 1))
                if g >= 2:
                    act.wait_ge(sem("oT_ready"), g - 1)
                nc.scalar.copy(k.o[:, g % 2, :], ps[5 + g % 2][:]).then_inc(sem("o_ready"), 1)

            copy_queries(0)
            copy_maxima(0)
            for u, (what, h, kt, q0) in enumerate(units):
                g, at = divmod(u, per_group)
                act.wait_ge(sem("st_done"), u + 1)
                if u >= 3:
                    act.wait_ge(sem("pv_done"), u - 2)
                nc.scalar.activation(k.p[:, u % 3, q0:S], ps[u % 2][:, q0:S], ACT.Exp).then_inc(sem("exp_done"), 1)
                if at == 0 and g + 1 < GROUPS:
                    copy_queries(g + 1)
                if at == 2 and g >= 1:
                    copy_products(g - 1)
                if at == per_group - 1 and g + 1 < GROUPS:
                    copy_maxima(g + 1)
            copy_products(GROUPS - 1)

        @block.tensor
        def _(pe):
            q_at, k_at = bass.ts(b, S), bass.ts(b, nk)

            def stack_parts(g):
                if g == 0:
                    if k.ctx_keys:
                        pe.wait_ge(sem("masks_ready"), 1)
                else:
                    pe.wait_ge(sem("maxima_in"), g)
                pe.matmul(ps[7][:, 0:nk], w(f"k_hi{g}"), k.k_hi[:, k_at], start=True, stop=False)
                pe.matmul(ps[7][:, 0:nk], w(f"k_lo{g}"), k.k_lo[:, k_at], start=False, stop=False)
                pe.matmul(ps[7][:, 0:nk], w("key_rows"), k.rows[:], start=False, stop=True).then_inc(sem("k_stacked"), 1)
                if g >= 1:
                    pe.wait_ge(sem("Q_ready"), g)
                pe.matmul(ps[2][:], w(f"q_hi{g}"), k.q_hi[:, q_at], start=True, stop=False)
                masked = k.kind in ("row", "add")
                last = pe.matmul(ps[2][:], w(f"q_lo{g}"), k.q_lo[:, q_at], start=False, stop=not masked)
                if masked:
                    last = pe.matmul(ps[2][:], w("query_rows"), k.ones[:], start=False, stop=True)
                last.then_inc(sem("q_stacked"), 1)

            chunks = [(g, c) for g in range(GROUPS) for c in k.chunks(g)]

            def first_scores(i):
                g, (t, h, n, keys) = chunks[i]
                if i % nchunks == 0:
                    pe.wait_ge(sem("Q_ready"), g + 1)
                    pe.wait_ge(sem("K_ready"), g + 1)
                if i >= 2:
                    pe.wait_ge(sem("max_done"), i - 1)
                j = h % GROUP
                out = ps[3 + i % 2][:, 0:n * keys].rearrange("p (h k) -> p h k", h=n)
                last = pe.matmul(out, k.Q[:, g % 2, t * P:(t + 1) * P], k.K[:, g % 2, j:j + n, 0:keys], start=True, stop=k.kind != "full")
                if k.kind == "full":
                    last = pe.matmul(out, w("negi"), over(k.mq[:, t, 0:keys], 1, n), start=False, stop=True)
                if k.kind == "page":
                    last = pe.matmul(ps[3 + i % 2][:, t * P:(t + 1) * P], w("negi"), w("pageq"), start=False, stop=True, skip_group_check=True)
                last.then_inc(sem("scores_done"), 1)

            def turn_maxima(g):
                pe.wait_ge(sem("mp_ready"), g + 1)
                tensor_transpose_tiles(pe, ps[7], k.mp[:, g % 2].bitcast(F32), w("ident")).then_inc(sem("mT_done"), 1)

            def second_scores(u):
                what, h, kt, q0 = units[u]
                g = u // per_group
                if u % per_group == 0:
                    pe.wait_ge(sem("maxima_in"), g + 1)
                if u >= 2:
                    pe.wait_ge(sem("exp_done"), u - 1)
                out = ps[u % 2][:, q0:S]
                keys = k.kr[:, g % 2] if what == "rest" else k.K[:, g % 2, h % GROUP, kt * P:(kt + 1) * P]
                last = pe.matmul(out, keys, k.Q[:, g % 2, q0:S], start=True, stop=k.kind != "full")
                if k.kind == "full":
                    last = pe.matmul(out, w("negi"), (k.mr if what == "rest" else k.mt)[:, q0:S], start=False, stop=True)
                if k.kind == "page":
                    last = pe.matmul(ps[u % 2][:, kt * P:(kt + 1) * P], w("negi"), w("paget"), start=False, stop=True, skip_group_check=True)
                last.then_inc(sem("st_done"), 1)

            def products(u):
                what, h, kt, q0 = units[u]
                g, j = u // per_group, h % GROUP
                if u == 0:
                    pe.wait_ge(sem("v_ready"), 1 + GROUP if k.ctx_keys else 1)
                if u % per_group == 0 and g >= 2:
                    pe.wait_ge(sem("oT_ready"), g - 1)
                pe.wait_ge(sem("exp_done"), u + 1)
                if what == "rest":
                    last = pe.matmul(ps[5 + g % 2][:], k.vr[:, g, :], k.p[:, u % 3, :], start=True, stop=True, skip_group_check=True)
                else:
                    last = pe.matmul(ps[5 + g % 2][32 * j:32 * (j + 1), q0:S], k.v[:, kt, h, :], k.p[:, u % 3, q0:S],
                                     start=not k.ctx_keys and kt == 0, stop=True, skip_group_check=True)
                last.then_inc(sem("pv_done"), 1)

            def pick_sums(g):
                pe.wait_ge(sem("o_ready"), g + 1)
                for t in range(QT):
                    last = pe.matmul(ps[5 + g % 2][:, t * GROUP:(t + 1) * GROUP], k.o[:, g % 2, t * P:(t + 1) * P], w("sums"), start=True, stop=True)
                last.then_inc(sem("sums_done"), 1)

            def spread_factors(g):
                pe.wait_ge(sem("rx_ready"), g + 1)
                tensor_transpose_tiles(pe, ps[5 + g % 2], k.rx, w("ident")).then_inc(sem("factors_done"), 1)

            def output(g):
                pe.wait_ge(sem("oT_ready"), g + 1)
                if g == 0:
                    pe.wait_ge(sem("max_done"), len(chunks))
                for t in range(QT):
                    last = pe.matmul(ps[3][:, t * P:(t + 1) * P], oT[:, g, t * P:(t + 1) * P], w(f"{pre}_wo")[:, g * P:(g + 1) * P],
                                     start=(g == 0 and t == 0), stop=(g == GROUPS - 1), skip_group_check=True)
                return last

            stack_parts(0)
            for i in range(nchunks):
                first_scores(i)
            turn_maxima(0)
            i, used = nchunks, 0
            for u in range(len(units)):
                g, at = divmod(u, per_group)
                second_scores(u)
                upto = i
                if at == 0 and g >= 2:
                    spread_factors(g - 2)
                if g + 1 < GROUPS:
                    if at == 0:
                        stack_parts(g + 1)
                    else:
                        upto = nchunks * (g + 1) + min(nchunks, -(-nchunks * at // (per_group - 2)))
                middle = (i + upto + 1) // 2
                while i < middle:
                    first_scores(i)
                    i += 1
                behind = 1 if at == per_group - 1 else 2
                while used < u + 1 - behind:
                    products(used)
                    used += 1
                while i < upto:
                    first_scores(i)
                    i += 1
                if at == 3 and g >= 1:
                    pick_sums(g - 1)
                if at == per_group - 1 and g + 1 < GROUPS:
                    turn_maxima(g + 1)
            spread_factors(GROUPS - 2)
            while used < len(units):
                products(used)
                used += 1
            for g in range(GROUPS - 1):
                output(g)
            if bias:
                for t in range(QT):
                    pe.matmul(ps[3][:, t * P:(t + 1) * P], w("ones")[0:1, :], w(f"{pre}_bo")[0:1, :], start=False, stop=False, skip_group_check=True)
            pick_sums(GROUPS - 1)
            spread_factors(GROUPS - 1)
            output(GROUPS - 1).then_inc(sem("y_done"), 1)
    end_of_block(net)



def router_block(net, b, k, weight, keep_x=False):
    nc, sem, ps, w = net.nc, net.sem, net.ps, net.w
    with nc.Block() as block:

        @block.vector
        def _(dve):
            ch = Chain(dve, sem("dve_chain"))
            last = vector_layernorm(dve, ch, x_of(net, b), k.n.xn, k.n)
            last.then_inc(sem("xn_ready"), 1)
            if keep_x:
                dve.wait_ge(sem("xn_ready"), 1)
                ch.link(dve.tensor_tensor(x_of(net, b), x_of(net, b), k.n.xn[:], ALU.add))
            if weight is not None:
                dve.wait_ge(sem("logits_done"), 1)
                ch.link(dve.tensor_copy(net.logits[:, :, b, :], ps[0][:, 0:QT * E8].rearrange("p (t e) -> p t e", t=QT)))

        @block.scalar
        def _(act):
            act.wait_ge(sem("xT_done"), 1)
            nc.scalar.copy(k.n.xnT[:], ps[7][:]).then_inc(sem("xnT_ready"), 1)
            act.wait_ge(sem("xnT_ready"), 1)
            nc.scalar.copy(net.xnT_all[:, bass.ts(b, S)], k.n.xnT[:]).then_inc(sem("xnT_kept"), 1)

        @block.tensor
        def _(pe):
            pe.wait_ge(sem("xn_ready"), 1)
            tensor_transpose_tiles(pe, ps[7], k.n.xn, w("ident")).then_inc(sem("xT_done"), 1)
            if weight is not None:
                pe.wait_ge(sem("xnT_ready"), 1)
                for t in range(QT):
                    last = pe.matmul(ps[0][:, t * E8:(t + 1) * E8], k.n.xnT[:, t * P:(t + 1) * P], w(weight), start=True, stop=True)
                last.then_inc(sem("logits_done"), 1)
    end_of_block(net)


class Router:

    def __init__(self, net, sb):
        n = QT * B
        self.g = sb("g", [P, n, E8])
        self.t = sb("t", [P, n, E8])
        self.sel = [sb(f"sel{i}", [P, n, E8]) for i in range(2)]
        self.top = sb("top", [P, n, 2])
        self.rm = sb("rm", [P, n])
        self.sum = sb("sum", [P, n])
        self.pair = sb("pair", [P, 2, n, E8])
        self.tot = sb("tot", [P, 2, E8])
        self.one = sb("one", [P, E8])
        self.temp = sb("temp", [P, 1])
        self.u = sb("u", [32, S])
        self.ue = sb("ue", [32, S])
        self.um = sb("um", [32, 1])
        self.us = sb("us", [32, 1])
        self.ul = sb("ul", [32, 1])


def vector_top2(dve, ch, k, rank):
    n = QT * B
    src = k.g
    for i in range(2):
        ch.link(dve.reduce_max(k.top[:, :, i], src[:], AX))
        ch.link(dve.tensor_tensor(k.sel[i][:], src[:], over(k.top[:, :, i], 2, E8), ALU.is_equal))
        ch.link(dve.tensor_tensor(k.sel[i][:], k.sel[i][:], over(rank, 1, n), ALU.mult))
        ch.link(dve.reduce_max(k.rm[:], k.sel[i][:], AX))
        last = dve.tensor_tensor(k.sel[i][:], k.sel[i][:], over(k.rm[:], 2, E8), ALU.is_equal)
        if i == 0:
            ch.link(last)
            ch.link(dve.scalar_tensor_tensor(k.t[:], k.sel[0][:], NEG, k.g[:], ALU.mult, ALU.add))
            src = k.t
    return last


def flat(t):
    return t[:].rearrange("p t b e -> p (t b) e")


def route_mean(net, k):
    nc, sem, ps, w = net.nc, net.sem, net.ps, net.w
    n = QT * B
    with nc.Block() as block:

        @block.vector
        def _(dve):
            ch = Chain(dve, sem("dve_chain"))
            lg = flat(net.logits)
            ch.link(dve.reduce_max(k.rm[:], lg, AX))
            dve.tensor_tensor(k.g[:], lg, over(k.rm[:], 2, E8), ALU.subtract).then_inc(sem("centred"), 1)
            dve.wait_ge(sem("exp_done"), 1)
            ch.link(dve.reduce_sum(k.sum[:], k.t[:], AX))
            ch.link(dve.reciprocal(k.sum[:], k.sum[:]))
            ch.link(dve.tensor_tensor(k.g[:], k.t[:], over(k.sum[:], 2, E8), ALU.mult))
            ch.link(vector_top2(dve, ch, k, w("rank")))
            ch.link(dve.tensor_tensor(k.sum[:], k.top[:, :, 0], k.top[:, :, 1], ALU.add))
            ch.link(dve.reciprocal(k.sum[:], k.sum[:]))
            ch.link(dve.tensor_tensor(k.pair[:, 1], k.sel[0][:], k.sel[1][:], ALU.add))
            ch.link(dve.tensor_tensor(k.t[:], k.g[:], k.pair[:, 1], ALU.mult))
            dve.tensor_tensor(k.pair[:, 0], k.t[:], over(k.sum[:], 2, E8), ALU.mult).then_inc(sem("pair_ready"), 1)
            dve.wait_ge(sem("sums_done"), 1)
            ch.link(dve.reduce_sum(k.tot[:], ps[0][:, 0:2 * n * E8].rearrange("p (a n e) -> p a e n", a=2, n=n), AX))
            ch.link(dve.tensor_scalar(k.one[:], k.tot[:, 1], 1.0, None, ALU.max))
            ch.link(dve.reciprocal(k.one[:], k.one[:]))
            ch.link(dve.tensor_tensor(k.one[:], k.one[:], k.tot[:, 0], ALU.mult))
            ch.link(dve.tensor_tensor(flat(net.coef), k.pair[:, 1], over(k.one[:], 1, n), ALU.mult))

        @block.scalar
        def _(act):
            act.wait_ge(sem("centred"), 1)
            nc.scalar.activation(k.t[:], k.g[:], ACT.Exp).then_inc(sem("exp_done"), 1)

        @block.tensor
        def _(pe):
            pe.wait_ge(sem("pair_ready"), 1)
            pe.matmul(ps[0][:, 0:2 * n * E8], w("ones"), k.pair[:].rearrange("p a n e -> p (a n e)"), start=True, stop=True).then_inc(sem("sums_done"), 1)
    end_of_block(net)


SINKHORN = 3


def route_sinkhorn(net, k):
    nc, sem, ps, w = net.nc, net.sem, net.ps, net.w
    n = QT * B
    tok = k.g[:].rearrange("p (t b) e -> p t (b e)", t=QT)
    with nc.Block() as block:

        @block.vector
        def _(dve):
            ch = Chain(dve, sem("dve_chain"))
            lg = flat(net.logits)
            ch.link(dve.tensor_scalar(k.temp[:], w("f2_temp"), 0.1, None, ALU.max))
            ch.link(dve.reciprocal(k.temp[:], k.temp[:]))
            ch.link(dve.tensor_tensor(k.g[:], lg, over(w("f2_router_b"), 1, n), ALU.add))
            ch.link(dve.tensor_scalar(k.g[:], k.g[:], k.temp[:], None, ALU.mult))
            for i in range(SINKHORN):
                ch.link(dve.reduce_max(k.rm[:], k.g[:], AX))
                dve.tensor_tensor(k.g[:], k.g[:], over(k.rm[:], 2, E8), ALU.subtract).then_inc(sem("row_centred"), 1)
                dve.wait_ge(sem("row_exp"), i + 1)
                dve.reduce_sum(k.sum[:], k.t[:], AX).then_inc(sem("row_sum"), 1)
                dve.wait_ge(sem("row_log"), i + 1)
                dve.tensor_tensor(k.g[:], k.g[:], over(k.rm[:], 2, E8), ALU.subtract).then_inc(sem("row_ready"), 1)
                dve.wait_ge(sem("turned"), i + 1)
                ch.link(dve.reduce_max(k.um[:], ps[0][0:32, :], AX))
                dve.tensor_scalar(k.u[:], ps[0][0:32, :], k.um[:], None, ALU.subtract).then_inc(sem("col_centred"), 1)
                dve.wait_ge(sem("col_log"), i + 1)
                dve.tensor_scalar(k.u[:], k.u[:], k.ul[:], None, ALU.subtract).then_inc(sem("col_ready"), 1)
                dve.wait_ge(sem("turned_back"), i + 1)
                dve.tensor_copy(tok, ps[1][:, 0:QT * 32].rearrange("p (t c) -> p t c", t=QT)).then_inc(sem("log_gates"), 1)
                dve.wait_ge(sem("log_gates"), i + 1)
            dve.wait_ge(sem("gates_exp"), 1)
            ch.link(dve.reduce_sum(k.sum[:], k.t[:], AX))
            ch.link(dve.tensor_scalar(k.sum[:], k.sum[:], 1e-8, None, ALU.add))
            ch.link(dve.reciprocal(k.sum[:], k.sum[:]))
            ch.link(dve.tensor_tensor(k.g[:], k.t[:], over(k.sum[:], 2, E8), ALU.mult))
            ch.link(vector_top2(dve, ch, k, w("rank")))
            ch.link(dve.tensor_tensor(k.sum[:], k.top[:, :, 0], k.top[:, :, 1], ALU.add))
            ch.link(dve.tensor_scalar(k.sum[:], k.sum[:], 1e-8, None, ALU.add))
            ch.link(dve.reciprocal(k.sum[:], k.sum[:]))
            ch.link(dve.tensor_tensor(k.t[:], k.sel[0][:], k.sel[1][:], ALU.add))
            ch.link(dve.tensor_tensor(k.t[:], k.g[:], k.t[:], ALU.mult))
            ch.link(dve.tensor_tensor(flat(net.coef), k.t[:], over(k.sum[:], 2, E8), ALU.mult))

        @block.scalar
        def _(act):
            for i in range(SINKHORN):
                act.wait_ge(sem("row_centred"), i + 1)
                nc.scalar.activation(k.t[:], k.g[:], ACT.Exp).then_inc(sem("row_exp"), 1)
                act.wait_ge(sem("row_sum"), i + 1)
                nc.scalar.activation(k.rm[:], k.sum[:], ACT.Ln).then_inc(sem("row_log"), 1)
                act.wait_ge(sem("col_centred"), i + 1)
                nc.scalar.activation(k.ue[:], k.u[:], ACT.Exp, accum_out=k.us[:]).then_inc(sem("col_exp"), 1)
                act.wait_ge(sem("col_exp"), i + 1)
                nc.scalar.activation(k.ul[:], k.us[:], ACT.Ln).then_inc(sem("col_log"), 1)
            act.wait_ge(sem("log_gates"), SINKHORN)
            nc.scalar.activation(k.t[:], k.g[:], ACT.Exp).then_inc(sem("gates_exp"), 1)

        @block.tensor
        def _(pe):
            for i in range(SINKHORN):
                pe.wait_ge(sem("row_ready"), i + 1)
                for t in range(QT):
                    last = pe.transpose(ps[0][0:32, t * P:(t + 1) * P], tok[:, t, :], w("ident"))
                last.then_inc(sem("turned"), 1)
                pe.wait_ge(sem("col_ready"), i + 1)
                for t in range(QT):
                    last = pe.transpose(ps[1][:, t * 32:(t + 1) * 32], k.u[:, t * P:(t + 1) * P], w("ident")[0:32, 0:32])
                last.then_inc(sem("turned_back"), 1)
    end_of_block(net)


def route_tokens(net, k):
    nc, sem, ps, w = net.nc, net.sem, net.ps, net.w
    n = QT * B
    top = k.top[:].rearrange("p (t b) c -> p t (b c)", t=QT)
    nb = 2 * B
    with nc.Block() as block:

        @block.vector
        def _(dve):
            ch = Chain(dve, sem("dve_chain"))
            ch.link(dve.tensor_copy(k.g[:], flat(net.logits)))
            vector_top2(dve, ch, k, w("rank")).then_inc(sem("top_ready"), 1)
            dve.wait_ge(sem("top_ready"), 1)
            dve.wait_ge(sem("turned"), 1)
            ch.link(dve.reduce_max(k.um[0:nb], ps[0][0:nb, :], AX))
            dve.tensor_scalar(k.u[0:nb, :], ps[0][0:nb, :], k.um[0:nb], None, ALU.subtract).then_inc(sem("centred"), 1)
            dve.wait_ge(sem("exp_done"), 1)
            ch.link(dve.reciprocal(k.us[0:nb], k.us[0:nb]))
            dve.tensor_scalar(k.u[0:nb, :], k.ue[0:nb, :], k.us[0:nb], None, ALU.mult).then_inc(sem("weights_ready"), 1)
            dve.wait_ge(sem("turned_back"), 1)
            ch.link(dve.tensor_copy(top, ps[1][:, 0:QT * nb].rearrange("p (t c) -> p t c", t=QT)))
            ch.link(dve.tensor_tensor(k.g[:], k.sel[0][:], over(k.top[:, :, 0], 2, E8), ALU.mult))
            ch.link(dve.tensor_tensor(k.t[:], k.sel[1][:], over(k.top[:, :, 1], 2, E8), ALU.mult))
            ch.link(dve.tensor_tensor(flat(net.coef), k.g[:], k.t[:], ALU.add))

        @block.scalar
        def _(act):
            act.wait_ge(sem("centred"), 1)
            nc.scalar.activation(k.ue[0:nb, :], k.u[0:nb, :], ACT.Exp, accum_out=k.us[0:nb]).then_inc(sem("exp_done"), 1)

        @block.tensor
        def _(pe):
            pe.wait_ge(sem("top_ready"), 1)
            for t in range(QT):
                last = pe.transpose(ps[0][0:nb, t * P:(t + 1) * P], top[:, t, :], w("ident"))
            last.then_inc(sem("turned"), 1)
            pe.wait_ge(sem("weights_ready"), 1)
            for t in range(QT):
                last = pe.transpose(ps[1][:, t * nb:(t + 1) * nb], k.u[0:nb, t * P:(t + 1) * P], w("ident")[0:nb, 0:nb])
            last.then_inc(sem("turned_back"), 1)
    end_of_block(net)


class Experts:

    def __init__(self, net, sb):
        self.xT = sb("xT", [P, S])
        self.t = sb("et", [P, 2, S])
        self.a = sb("ea", [P, 2, S])
        self.h = sb("eh", [P, 2, S])
        self.y = sb("ey", [P, 2, QT, P])
        self.acc = sb("eacc", [P, QT, P])



def experts_block(net, b, k, act_kind, names, experts, tiles):
    nc, sem, ps, w = net.nc, net.sem, net.ps, net.w
    gate, up, down = names
    work = [(e, i) for e in range(experts) for i in range(tiles)]
    weighed = experts > 1
    with nc.Block() as block:

        @block.gpsimd
        def _(pool):
            nc.gpsimd.tensor_copy(k.xT[:], net.xnT_all[:, bass.ts(b, S)]).then_inc(sem("xT_ready"), 1)
            if weighed:
                nc.gpsimd.memset(k.acc[:], 0.0).then_inc(sem("acc_zero"), 1)
                pool.wait_ge(sem("acc_zero"), 1)
                for e in range(experts):
                    pool.wait_ge(sem("y_ready"), e + 1)
                    if e:
                        pool.wait_ge(sem("acc_done"), e)
                    nc.gpsimd.tensor_tensor(k.acc[:], k.acc[:], k.y[:, e % 2], ALU.add).then_inc(sem("acc_done"), 1)

        @block.vector
        def _(dve):
            ch = Chain(dve, sem("dve_chain"))

            def weigh(e):
                if act_kind == "bias":
                    dve.wait_ge(sem("out_done"), e + 1)
                else:
                    dve.wait_ge(sem("h_used"), tiles * (e + 1))
                if e >= 2:
                    dve.wait_ge(sem("acc_done"), e - 1)
                dve.tensor_tensor(k.y[:, e % 2], ps[4 + e % 2][:].rearrange("p (t d) -> p t d", t=QT), over(net.coef[:, :, b, e], 2, P),
                                  ALU.mult).then_inc(sem("y_ready"), 1)

            for n, (e, i) in enumerate(work):
                if act_kind == "bias":
                    if i == 1 and e >= 1:
                        weigh(e - 1)
                    continue
                dve.wait_ge(sem("act_done"), n + 1)
                if n >= 2:
                    dve.wait_ge(sem("h_used"), n - 1)
                dve.wait_ge(sem("up_done"), n + 1)
                if act_kind == "silu":
                    ch.link(dve.scalar_tensor_tensor(k.a[:, n % 2], k.t[:, n % 2], 1.0, ps[n % 2][:], ALU.add, ALU.mult))
                    dve.scalar_tensor_tensor(k.h[:, n % 2], ps[2 + n % 2][:], 0.5, k.a[:, n % 2], ALU.mult, ALU.mult).then_inc(sem("h_ready"), 1)
                else:
                    dve.tensor_tensor(k.h[:, n % 2], ps[2 + n % 2][:], k.t[:, n % 2], ALU.mult).then_inc(sem("h_ready"), 1)
                if i == 1 and e >= 1:
                    weigh(e - 1)
            if weighed:
                weigh(experts - 1)
                dve.wait_ge(sem("acc_done"), experts)
                ch.link(dve.tensor_tensor(x_of(net, b), x_of(net, b), k.acc[:], ALU.add))
            else:
                dve.wait_ge(sem("h_used"), tiles)
                ch.link(dve.tensor_tensor(x_of(net, b), x_of(net, b), ps[4][:].rearrange("p (t d) -> p t d", t=QT), ALU.add))

        @block.scalar
        def _(act):
            for n, (e, i) in enumerate(work):
                act.wait_ge(sem("gate_done"), n + 1)
                if act_kind == "bias":
                    if n >= 2:
                        act.wait_ge(sem("h_used"), n - 1)
                    nc.scalar.activation(k.h[:, n % 2], ps[n % 2][:], ACT.Relu, bias=w(f"b{e}")[:, i:i + 1]).then_inc(sem("h_ready"), 1)
                    continue
                if n >= 2:
                    act.wait_ge(sem("h_ready"), n - 1)
                if act_kind == "silu":
                    nc.scalar.activation(k.t[:, n % 2], ps[n % 2][:], ACT.Tanh, scale=0.5).then_inc(sem("act_done"), 1)
                else:
                    nc.scalar.activation(k.t[:, n % 2], ps[n % 2][:], ACT.Relu).then_inc(sem("act_done"), 1)

        @block.tensor
        def _(pe):
            pe.wait_ge(sem("xT_ready"), 1)

            def hidden(n):
                e, i = work[n]
                if n >= 2:
                    pe.wait_ge(sem("h_ready"), n - 1)
                cols = slice(i * P, (i + 1) * P)
                pe.matmul(ps[n % 2][:], w(gate.format(e))[:, cols], k.xT[:], start=True, stop=True).then_inc(sem("gate_done"), 1)
                if up:
                    pe.matmul(ps[2 + n % 2][:], w(up.format(e))[:, cols], k.xT[:], start=True, stop=True).then_inc(sem("up_done"), 1)

            def output(n):
                e, i = work[n]
                pe.wait_ge(sem("h_ready"), n + 1)
                if i == 0 and e >= 2:
                    pe.wait_ge(sem("y_ready"), e - 1)
                bank = ps[4 + e % 2]
                for t in range(QT):
                    last = pe.matmul(bank[:, t * P:(t + 1) * P], k.h[:, n % 2, t * P:(t + 1) * P], w(down.format(e))[:, i * P:(i + 1) * P],
                                     start=(i == 0 and t == 0), stop=(i == tiles - 1), skip_group_check=True)
                last.then_inc(sem("h_used"), 1)
                if i == tiles - 1:
                    if act_kind == "bias":
                        for t in range(QT):
                            last = pe.matmul(bank[:, t * P:(t + 1) * P], w("ones")[0:1, :], w("b2")[0:1, e * P:(e + 1) * P],
                                             start=False, stop=True, skip_group_check=True)
                        last.then_inc(sem("out_done"), 1)

            for n in range(len(work) + 1):
                if n < len(work):
                    hidden(n)
                if n >= 1:
                    output(n - 1)
    end_of_block(net)



NSTATE, NCONV = 16, 4


class Scan:

    def __init__(self, net, sb):
        self.n = Norm(net, sb)
        self.xp = sb("xp", [P, 2, NCONV - 1 + S])
        self.c = sb("c", [P, 2, S])
        self.z = sb("z", [P, 2, S])
        self.t = sb("st", [P, 2, S])
        self.xc = sb("xc", [P, 2, S])
        self.zs = sb("zs", [P, 2, S])
        self.A = sb("A", [P, 2 * NSTATE])
        self.bf = sb("bf", [32, S])
        self.bh = sb("bh", [32, S], BF16)
        self.bc = sb("bc", [P, S], BF16)
        self.raw = sb("raw", [P, S])
        self.e = sb("e", [P, S])
        self.ln = sb("ln", [P, S])
        self.d = sb("d", [P, S])
        self.iz = sb("iz", [P, S])
        self.dt = sb("dt", [P, S])
        self.dtx = sb("dtx", [P, 2, S])
        self.dA = sb("dA", [P, 2, 2, S])
        self.cb = sb("cb", [P, 2, S])
        self.dbx = sb("dbx", [P, 2, 2, S])
        self.h = sb("sh", [P, 2, 2, S])
        self.hc = sb("hc", [P, 2, 2, S])
        self.r = sb("sr", [P, QT, P])
        self.rn = sb("rn", [P, QT, P])


def scan_prepare(net, k):
    nc, sem, w = net.nc, net.sem, net.w
    with nc.Block() as block:

        @block.scalar
        def _(act):
            nc.scalar.activation(k.A[:], w("m_alog"), ACT.Exp).then_inc(sem("A_exp"), 1)

        @block.vector
        def _(dve):
            ch = Chain(dve, sem("dve_chain"))
            dve.memset(k.xp[:, :, 0:NCONV - 1], 0.0)
            ch.link(dve.memset(k.bc[:], 0.0))
            dve.wait_ge(sem("A_exp"), 1)
            ch.link(dve.tensor_scalar(k.A[:], k.A[:], -1.0, None, ALU.mult))
    end_of_block(net)



def scan_block(net, b, k):
    nc, sem, ps, w = net.nc, net.sem, net.ps, net.w
    with nc.Block() as block:

        @block.vector
        def _(dve):
            ch = Chain(dve, sem("dve_chain"))
            vector_layernorm(dve, ch, x_of(net, b), k.n.xn, k.n).then_inc(sem("xn_ready"), 1)
            for i in range(2):
                dve.wait_ge(sem("xm_ready"), i + 1)
                ch.link(dve.tensor_scalar(k.c[:, i], k.xp[:, i, 0:S], w("m_conv")[:, 4 * i:4 * i + 1], w("m_conv_b")[:, i:i + 1], ALU.mult, ALU.add))
                for j in range(1, NCONV):
                    last = dve.scalar_tensor_tensor(k.c[:, i], k.xp[:, i, j:j + S], w("m_conv")[:, 4 * i + j:4 * i + j + 1], k.c[:, i], ALU.mult, ALU.add)
                    if j < NCONV - 1:
                        ch.link(last)
                last.then_inc(sem("conv_ready"), 1)
            dve.wait_ge(sem("tanh_c"), 1)
            ch.link(dve.scalar_tensor_tensor(k.t[:], k.t[:], 1.0, k.c[:], ALU.add, ALU.mult))
            dve.tensor_scalar(k.xc[:], k.t[:], 0.5, None, ALU.mult).then_inc(sem("xc_ready"), 1)
            dve.wait_ge(sem("tanh_z"), 1)
            ch.link(dve.scalar_tensor_tensor(k.zs[:], k.zs[:], 1.0, k.z[:], ALU.add, ALU.mult))
            dve.wait_ge(sem("dt_done"), 1)
            ch.link(dve.tensor_scalar(k.raw[:], ps[5][:], w("m_dt_b"), None, ALU.add))
            dve.scalar_tensor_tensor(k.e[:], k.raw[:], -1.0, k.raw[:], ALU.mult, ALU.max).then_inc(sem("abs_ready"), 1)
            dve.wait_ge(sem("bc_done"), 1)
            ch.link(dve.tensor_scalar(k.bf[:], ps[4][0:32, :], w("m_xp_b")[0:32, :], None, ALU.add))
            ch.link(dve.tensor_copy(k.bh[:], k.bf[:]))
            dve.tensor_copy(k.bc[0:32, :], k.bh[:])
            ch.link(dve.tensor_tensor(k.bf[:], k.bf[:], k.bh[:], ALU.subtract))
            ch.link(dve.tensor_copy(k.bh[:], k.bf[:]))
            dve.tensor_copy(k.bc[32:64, :], k.bh[:])
            ch.link(dve.tensor_tensor(k.bf[:], k.bf[:], k.bh[:], ALU.subtract))
            dve.tensor_copy(k.bc[64:96, :], k.bf[:]).then_inc(sem("bc_ready"), 1)
            dve.wait_ge(sem("log_ready"), 1)
            ch.link(dve.tensor_scalar(k.iz[:], k.d[:], -1.0, 0.0, ALU.add, ALU.is_equal))
            ch.link(dve.scalar_tensor_tensor(k.d[:], k.d[:], -1.0, k.iz[:], ALU.add, ALU.add))
            ch.link(dve.reciprocal(k.d[:], k.d[:]))
            dve.tensor_tensor(k.ln[:], k.ln[:], k.iz[:], ALU.add)
            ch.link(dve.tensor_tensor(k.d[:], k.d[:], k.e[:], ALU.mult))
            ch.link(dve.tensor_tensor(k.d[:], k.d[:], k.ln[:], ALU.mult))
            dve.scalar_tensor_tensor(k.dt[:], k.raw[:], 0.0, k.d[:], ALU.max, ALU.add).then_inc(sem("dt_ready"), 1)
            dve.wait_ge(sem("dt_ready"), 1)
            ch.link(dve.tensor_tensor(k.dtx[:], k.xc[:], over(k.dt[:], 1, 2), ALU.mult))
            for s in range(NSTATE):
                dve.wait_ge(sem("B_done"), s + 1)
                dve.tensor_tensor(k.dbx[:, s % 2], k.dtx[:], over(ps[s % 2][:], 1, 2), ALU.mult).then_inc(sem("dbx_ready"), 1)
                dve.wait_ge(sem("dbx_ready"), s + 1)
                for i in range(2):
                    dve.wait_ge(sem("dA_ready"), 2 * s + i + 1)
                    if s >= 2 and i == 0:
                        dve.wait_ge(sem("hc_ready"), s - 1)
                    dve.tensor_tensor_scan(k.h[:, s % 2, i], k.dA[:, s % 2, i], k.dbx[:, s % 2, i], 0.0, ALU.mult, ALU.add).then_inc(sem("h_ready"), 1)
            dve.wait_ge(sem("y_done"), 1)
            for i in range(2):
                ch.link(dve.scalar_tensor_tensor(k.c[:, i], k.xc[:, i], w("m_d")[:, i:i + 1], ps[4 + i][:], ALU.mult, ALU.add))
            dve.scalar_tensor_tensor(k.c[:], k.c[:], 0.5, k.zs[:], ALU.mult, ALU.mult).then_inc(sem("gated_ready"), 1)
            dve.wait_ge(sem("out_done"), 1)
            ch.link(dve.tensor_tensor(k.r[:], ps[6][:].rearrange("p (t d) -> p t d", t=QT), k.n.xn[:], ALU.add))
            ch.link(vector_layernorm(dve, ch, k.r, k.rn, k.n))
            ch.link(dve.tensor_tensor(k.rn[:], k.rn[:], over(w("m_gamma"), 1, QT), ALU.mult))
            ch.link(dve.tensor_tensor(k.rn[:], k.rn[:], over(w("m_beta"), 1, QT), ALU.add))
            ch.link(dve.tensor_tensor(x_of(net, b), x_of(net, b), k.rn[:], ALU.add))

        @block.gpsimd
        def _(pool):
            for s in range(NSTATE):
                pool.wait_ge(sem("C_ready"), s + 1)
                pool.wait_ge(sem("h_ready"), 2 * s + 2)
                if s >= 2:
                    pool.wait_ge(sem("hc_used"), s - 1)
                nc.gpsimd.tensor_tensor(k.hc[:, s % 2], k.h[:, s % 2], over(k.cb[:, s % 2], 1, 2), ALU.mult).then_inc(sem("hc_ready"), 1)

        @block.scalar
        def _(act):
            act.wait_ge(sem("xT_done"), 1)
            nc.scalar.copy(k.n.xnT[:], ps[7][:]).then_inc(sem("xnT_ready"), 1)
            for i in range(2):
                act.wait_ge(sem("in_done"), i + 1)
                nc.scalar.activation(k.xp[:, i, NCONV - 1:NCONV - 1 + S], ps[i][:], ACT.Identity, bias=w("m_in_b")[:, i:i + 1]).then_inc(sem("xm_ready"), 1)
            for i in range(2):
                act.wait_ge(sem("in_done"), i + 3)
                nc.scalar.activation(k.z[:, i], ps[2 + i][:], ACT.Identity, bias=w("m_in_b")[:, 2 + i:3 + i]).then_inc(sem("z_ready"), 1)
            act.wait_ge(sem("z_ready"), 2)
            nc.scalar.activation(k.zs[:], k.z[:], ACT.Tanh, scale=0.5).then_inc(sem("tanh_z"), 1)
            act.wait_ge(sem("conv_ready"), 2)
            nc.scalar.activation(k.t[:], k.c[:], ACT.Tanh, scale=0.5).then_inc(sem("tanh_c"), 1)
            act.wait_ge(sem("abs_ready"), 1)
            nc.scalar.activation(k.e[:], k.e[:], ACT.Exp, scale=-1.0).then_inc(sem("e_ready"), 1)
            act.wait_ge(sem("e_ready"), 1)
            nc.scalar.activation(k.d[:], k.e[:], ACT.Identity, bias=1.0).then_inc(sem("e1_ready"), 1)
            act.wait_ge(sem("e1_ready"), 1)
            nc.scalar.activation(k.ln[:], k.d[:], ACT.Ln).then_inc(sem("log_ready"), 1)
            act.wait_ge(sem("dt_ready"), 1)
            for s in range(NSTATE):
                for i in range(2):
                    if s >= 2:
                        act.wait_ge(sem("h_ready"), 2 * (s - 2) + i + 1)
                    nc.scalar.activation(k.dA[:, s % 2, i], k.dt[:], ACT.Exp, scale=k.A[:, i * NSTATE + s:i * NSTATE + s + 1]).then_inc(sem("dA_ready"), 1)
                act.wait_ge(sem("C_done"), s + 1)
                if s >= 2:
                    act.wait_ge(sem("hc_ready"), s - 1)
                nc.scalar.copy(k.cb[:, s % 2], ps[2 + s % 2][:]).then_inc(sem("C_ready"), 1)

        @block.tensor
        def _(pe):
            pe.wait_ge(sem("xn_ready"), 1)
            tensor_transpose_tiles(pe, ps[7], k.n.xn, w("ident")).then_inc(sem("xT_done"), 1)
            pe.wait_ge(sem("xnT_ready"), 1)
            for i in range(4):
                pe.matmul(ps[i][:], w("m_in")[:, i * P:(i + 1) * P], k.n.xnT[:], start=True, stop=True).then_inc(sem("in_done"), 1)
            pe.wait_ge(sem("xc_ready"), 1)
            for i in range(2):
                last = pe.matmul(ps[5][:], w("m_dt")[:, i * P:(i + 1) * P], k.xc[:, i], start=(i == 0), stop=(i == 1))
            last.then_inc(sem("dt_done"), 1)
            for i in range(2):
                last = pe.matmul(ps[4][0:32, :], w("m_xp")[:, i * 32:(i + 1) * 32], k.xc[:, i], start=(i == 0), stop=(i == 1))
            last.then_inc(sem("bc_done"), 1)
            pe.wait_ge(sem("bc_ready"), 1)
            pe.wait_ge(sem("z_ready"), 2)

            def spread(s):
                if s >= 2:
                    pe.wait_ge(sem("dbx_ready"), s - 1)
                pe.matmul(ps[s % 2][:], w("sel")[:, s * P:(s + 1) * P], k.bc[:], start=True, stop=True).then_inc(sem("B_done"), 1)
                if s >= 2:
                    pe.wait_ge(sem("C_ready"), s - 1)
                pe.matmul(ps[2 + s % 2][:], w("sel")[:, (NSTATE + s) * P:(NSTATE + s + 1) * P], k.bc[:], start=True, stop=True).then_inc(sem("C_done"), 1)

            spread(0)
            spread(1)
            pe.wait_ge(sem("dt_ready"), 1)
            for s in range(NSTATE):
                pe.wait_ge(sem("hc_ready"), s + 1)
                for i in range(2):
                    last = pe.matmul(ps[4 + i][:], w("ident"), k.hc[:, s % 2, i], start=(s == 0), stop=(s == NSTATE - 1))
                if s == NSTATE - 1:
                    last.then_inc(sem("y_done"), 1)
                else:
                    last.then_inc(sem("hc_used"), 1)
                if s + 2 < NSTATE:
                    spread(s + 2)
            pe.wait_ge(sem("gated_ready"), 1)
            for t in range(QT):
                for i in range(2):
                    pe.matmul(ps[6][:, t * P:(t + 1) * P], k.c[:, i, t * P:(t + 1) * P], w("m_out")[:, i * P:(i + 1) * P], start=(i == 0), stop=False)
                last = pe.matmul(ps[6][:, t * P:(t + 1) * P], w("ones")[0:1, :], w("m_out_b")[0:1, :], start=False, stop=True)
            last.then_inc(sem("out_done"), 1)
    end_of_block(net)



def program(nc, x_dram, packs, out_dram, upto=12, after=0):
    with ExitStack() as ctx:
        net = Net(nc, ctx)
        loads = {}
        loaded = {name: nc.alloc_semaphore(f"loaded_{name}") for name in packs if name != "x"}
        x_loaded = nc.alloc_semaphore("x_loaded")
        stored = nc.alloc_semaphore("stored")

        def place(stack, name, table, dt=F32):
            offs, n = offsets(table)
            t = stack.enter_context(nc.sbuf_tensor(f"w_{name}", [P, n], dt))
            for key, at in offs.items():
                net.weights[key] = (t, at)
            loads[name] = (t, packs[name], loaded[name])

        for name, table, dt in (("constf", CONSTF, F32), ("constb", CONSTB, BF16), ("attn", ATTN, F32), ("ints", INTS, I32)):
            place(ctx, name, table, dt)
        offs, n = offsets(PLACE)
        placers = net.sb("placers", [P, n], F32R)
        for key, at in offs.items():
            net.weights[key] = (placers, at)
        xv = x_dram.rearrange("b (t p) d -> p (b t) d", p=P)
        ov = out_dram.rearrange("b (t p) d -> p (b t) d", p=P)

        ffn1_room, ffn0_room, first_room = ExitStack(), ExitStack(), ExitStack()
        place(ffn1_room, "ffn1", FFN1, I32)
        place(ffn0_room, "ffn0", FFN0)
        ffn1 = loads["ffn1"][0]
        l1w = ffn1[:, :].bitcast(F32)
        for key in FFN1:
            net.weights[key] = (l1w, net.weights[key][1])
        place_f = first_room.enter_context(nc.sbuf_tensor("place_f", [P, n], F32))
        with nc.Block() as block:

            @block.sync
            def _(sp):
                sp.dma_start(net.x[:], xv).then_inc(x_loaded, 16)
                sp.dma_start(place_f[:, 0:n], packs["place"]).then_inc(loaded["place"], 16)
                for name in ("constf", "attn", "ints", "ffn1"):
                    t, src, s = loads[name]
                    sp.dma_start(t[:, :], src).then_inc(s, 16)

            @block.scalar
            def _(act):
                for name in ("constb", "ffn0"):
                    t, src, s = loads[name]
                    act.dma_start(t[:, :], src).then_inc(s, 16)

            @block.vector
            def _(dve):
                dve.wait_ge(x_loaded, 16)
                for name in ("constf", "constb", "attn", "ints", "ffn1"):
                    dve.wait_ge(loads[name][2], 16)
                dve.wait_ge(loaded["place"], 16)
                dve.tensor_scalar(l1w, ffn1[:, :], 1.0 / 127.0, None, ALU.mult).then_inc(net.sem("dve_chain"), 1)
                dve.tensor_copy(placers[:], place_f[:, 0:n]).then_inc(net.sem("dve_chain"), 1)
                dve.wait_ge(net.sem("dve_chain"), 2)
        end_of_block(net)
        first_room.close()

        def scope():
            stack = ExitStack()

            def sb(name, shape, dt=F32):
                net.names += 1
                return stack.enter_context(nc.sbuf_tensor(f"{name}_{net.names}", shape, dt))
            return stack, sb

        def wait_loaded(name):
            with nc.Block() as block:

                @block.vector
                def _(dve):
                    dve.wait_ge(loads[name][2], 16)

        def narrow_attention(pre, kind, ctx_keys):
            stack, sb = scope()
            with stack:
                k = Narrow(net, sb, kind, ctx_keys)
                inner, inner_sb = scope()
                with inner:
                    narrow_project(net, k, pre, 1.0 / float(np.sqrt(np.float32(HD))), inner_sb)
                k.more_buffers(net, sb)
                narrow_prepare(net, k)
                with nc.Fori(0, B, 1) as b:
                    narrow_block(net, b, k, pre)

        def attention(pre, kind, ctx_keys, scale, wide=False):
            stack, sb = scope()
            with stack:
                k = Heads(net, sb, kind, ctx_keys, wide)
                heads_prepare(net, k)
                with nc.Fori(0, B, 1) as b:
                    heads_block(net, b, k, pre, scale)

        class One:
            pass

        def experts(weight, route, act_kind, names, n, tiles, keep_x=False):
            stack, sb = scope()
            with stack:
                k = One()
                k.n = Norm(net, sb)
                r = Router(net, sb) if route else None
                e = Experts(net, sb)
                with nc.Fori(0, B, 1) as b:
                    router_block(net, b, k, weight, keep_x)
                if route:
                    route(net, r)
                with nc.Fori(0, B, 1) as b:
                    experts_block(net, b, e, act_kind, names, n, tiles)

        done = 0

        def more():
            nonlocal done
            done += 1
            return after < done <= upto

        if more():
            stack, sb = scope()
            with stack:
                k = One()
                k.n = Norm(net, sb)
                k.qT, k.kT = sb("qT", [P, S]), sb("kT", [P, S])
                k.s, k.p = sb("s", [P, QT, S]), sb("p", [P, QT, S])
                k.mx, k.negm, k.sum, k.rs = sb("mx", [P, QT]), sb("negm", [P, QT]), sb("sum", [P, QT]), sb("rs", [P, QT])
                with nc.Fori(0, B, 1) as b:
                    single_head_block(net, b, k)
        if more():
            narrow_attention("x0", "row", True)
        wait_loaded("ffn0")
        if more():
            experts("f0_router", route_mean, "silu", ("g{}", "u{}", "d{}"), E8, 4)
        ffn0_room.close()
        if more():
            narrow_attention("a1", "page", False)
        if more():
            narrow_attention("x1", "add", True)
        if more():
            experts(None, None, "silu", ("L1_g", "L1_u", "L1_d"), 1, 3)
        ffn1_room.close()
        if more():
            stack, sb = scope()
            with stack:
                k = Scan(net, sb)
                scan_prepare(net, k)
                with nc.Fori(0, B, 1) as b:
                    scan_block(net, b, k)
        def load(room, name, table):
            place(room, name, table)
            with nc.Block() as block:

                @block.sync
                def _(sp):
                    t, src, s = loads[name]
                    sp.dma_start(t[:, :], src).then_inc(s, 16)

        late_room, ffn2_room = ExitStack(), ExitStack()
        load(ffn2_room, "ffn2", FFN2)
        if more():
            narrow_attention("x2", "full", True)
        wait_loaded("ffn2")
        if more():
            experts("f2_router", route_sinkhorn, "relu", ("g{}", "u{}", "d{}"), E8, 2, keep_x=True)
        ffn2_room.close()
        load(late_room, "wide", WIDE)
        if more():
            narrow_attention("a3", None, False)
        load(late_room, "ffn3", FFN3)
        wait_loaded("wide")
        if more():
            attention("x3", "len", True, 0.125, wide=True)
        wait_loaded("ffn3")
        if more():
            experts("f3_router", route_tokens, "bias", ("w{}", None, "o{}"), E8, 2)

        with nc.Block() as block:

            @block.sync
            def _(sp):
                for name in ("wide", "ffn2", "ffn3", "ffn0"):
                    sp.wait_ge(loads[name][2], 16)
                sp.dma_start(ov, net.x[:]).then_inc(stored, 16)
                sp.wait_ge(stored, 16)
        late_room.close()



def pack(table, inputs, dtype):
    offs, n = offsets(table)
    out = np.zeros((P, n), dtype)
    for name, (_, f) in table.items():
        a = f(inputs) if inputs is not None else f()
        at, cols = offs[name]
        assert a.shape[1] == cols, (name, a.shape, cols)
        out[0:a.shape[0], at:at + cols] = a
    return out


PACKS = (("attn", ATTN, "f"), ("wide", WIDE, "f"), ("ffn0", FFN0, "f"), ("ffn2", FFN2, "f"), ("ffn3", FFN3, "f"), ("ffn1", FFN1, "i"), ("ints", INTS, "i"))


def arrays_of(inputs):
    inputs = {n: np.asarray(a) for n, a in inputs.items()}
    out = {"x_dram": np.ascontiguousarray(inputs["x"])}
    for name, table, kind in PACKS:
        out[f"{name}_dram"] = pack(table, inputs, np.float32 if kind == "f" else np.int32)
    out["constf_dram"] = pack(CONSTF, None, np.float32)
    out["place_dram"] = pack(PLACE, None, np.float32)
    out["constb_dram"] = (pack(CONSTB, None, np.float32).view(np.uint32) >> 16).astype(np.uint16)
    return out


def build(nc, arrays, upto=12, after=0):
    aps = {n: nc.dram_tensor(n, a.shape, mybir.dt.from_np(a.dtype), kind="ExternalInput").ap() for n, a in arrays.items()}
    out = nc.dram_tensor("out_dram", (B, S, P), F32, kind="ExternalOutput").ap()
    packs = {n[:-5]: ap for n, ap in aps.items()}
    packs["constb"] = packs["constb"].bitcast(BF16)
    program(nc, aps["x_dram"], packs, out, upto, after)


def kernel(**inputs):
    import concourse.bacc as bacc
    from concourse.bass_utils import run_bass_kernel_spmd as run

    nc = bacc.Bacc("TRN2", target_bir_lowering=False, num_devices=1)
    arrays = arrays_of(inputs)
    build(nc, arrays)
    r = run(nc, [arrays], core_ids=[0])
    return r.results[0]["out_dram"]
```

```python
from contextlib import ExitStack

import numpy as np

import concourse.bass as bass
from concourse import mybir

F32 = mybir.dt.float32
F32R = mybir.dt.float32r
BF16 = mybir.dt.bfloat16
I32 = mybir.dt.int32
ALU = mybir.AluOpType
ACT = mybir.ActivationFunctionType
AX = mybir.AxisListType.X

P = 128
B, S, S2 = 4, 512, 154
QT = S // P
HEADS = 16
HD = P // HEADS
XHD = 64
KMAIN, KREM = P, S2 - P
KPAD = KMAIN + 32
E8 = 8
EPS = 1e-5
NEG = -1e30
PAGE = 32
LN_BN = 6
BODY = 2
GROUP = 4
GROUPS = HEADS // GROUP
MROW, MASKROW = 96, 104
ONEROW = 64



def chunked(a, n):
    return a.reshape(n, P, a.shape[-1]).transpose(1, 0, 2).reshape(P, -1)


def col(a):
    return a.reshape(-1, P).T


def row(a):
    return a.reshape(1, -1)


def swap_pairs(w):
    return w.reshape(w.shape[0], -1, 2)[:, :, ::-1].reshape(w.shape[0], -1)


def quads(a):
    out = np.ones((P, a.shape[1]), a.dtype)
    for j in range(4):
        out[32 * j:32 * j + KREM] = a[KMAIN:]
    return out


def context(i):
    return np.pad(i["ctx_1024"].transpose(2, 0, 1), ((0, 0), (0, 0), (0, KPAD - S2))).reshape(P, -1)


def by_group(a):
    out = np.zeros((P, GROUPS, P), a.dtype)
    for h in range(HEADS):
        out[32 * (h % GROUP):32 * (h % GROUP) + HD, h // GROUP] = a[HD * h:HD * (h + 1)]
    return out.reshape(P, -1)


START = {
    "a0_wq": (P, lambda i: i["L0_attn_Wq"]), "a0_wk": (P, lambda i: i["L0_attn_Wk"]), "a0_wv": (P, lambda i: i["L0_attn_Wv"]),
    "a0_bq": (1, lambda i: col(i["L0_attn_bq"])), "a0_bk": (1, lambda i: col(i["L0_attn_bk"])), "a0_bv": (P, lambda i: row(i["L0_attn_bv"])),
    "ident": (P, lambda i: np.eye(P)), "ones": (P, lambda i: np.ones((P, P))),
}
ATTN = {
    "ctxT": (B * KPAD, lambda i: context(i)), "restT": (B * P, lambda i: np.repeat(context(i).reshape(P, B, 1, KPAD)[..., KMAIN:], 4, axis=2).reshape(P, -1)),
    "x0_wq": (P, lambda i: i["L0_xattn_wq"].T), "x0_wk": (P, lambda i: i["L0_xattn_wk"].T),
    "x0_wv": (P, lambda i: i["L0_xattn_wv"].T), "x0_wo": (GROUPS * P, lambda i: by_group(i["L0_xattn_wo"].T)),
    "x0_bq": (1, lambda i: col(i["L0_xattn_bq"])), "x0_bk": (1, lambda i: col(i["L0_xattn_bk"])),
    "x0_bv": (P, lambda i: row(i["L0_xattn_bv"])), "x0_bo": (P, lambda i: row(i["L0_xattn_bo"])),
    "f0_router": (E8, lambda i: i["L0_ffn_router_w"].T),
    "a1_wq": (P, lambda i: i["L1_attn_wq"]), "a1_wqs": (P, lambda i: swap_pairs(i["L1_attn_wq"])),
    "a1_down": (64, lambda i: i["L1_attn_w_down"]),
    "a1_wk": (P, lambda i: i["L1_attn_wk_up"]), "a1_wks": (P, lambda i: swap_pairs(i["L1_attn_wk_up"])),
    "a1_wv": (P, lambda i: i["L1_attn_wv_up"]), "a1_wo": (GROUPS * P, lambda i: by_group(i["L1_attn_wo"])),
    "x1_wq": (P, lambda i: i["L1_xattn_Wq"]), "x1_wk": (P, lambda i: i["L1_xattn_Wk"]),
    "x1_wv": (P, lambda i: i["L1_xattn_Wv"]), "x1_wo": (GROUPS * P, lambda i: by_group(i["L1_xattn_Wo"])),
    "x1_bq": (1, lambda i: col(i["L1_xattn_bq"])), "x1_bk": (1, lambda i: col(i["L1_xattn_bk"])),
    "x1_bv": (P, lambda i: row(i["L1_xattn_bv"])), "x1_bo": (P, lambda i: row(i["L1_xattn_bo"])),
    "x1_pad": (B * KPAD, lambda i: np.broadcast_to(np.pad(i["mask_Bx1x1xS2_ff0"].reshape(B, S2), ((0, 0), (0, KPAD - S2))).reshape(1, -1), (P, B * KPAD))),
    "m_in": (4 * P, lambda i: i["L2_attn_in_proj_w"].T), "m_in_b": (4, lambda i: col(i["L2_attn_in_proj_b"])),
    "m_conv": (8, lambda i: chunked(i["L2_attn_conv_w"].reshape(2 * P, 4), 2)), "m_conv_b": (2, lambda i: col(i["L2_attn_conv_b"])),
    "m_xp": (2 * 32, lambda i: chunked(i["L2_attn_x_proj_w"].T[:, 0:32], 2)),
    "m_xp_b": (1, lambda i: i["L2_attn_x_proj_b"][0:32].reshape(32, 1)),
    "m_dt": (2 * P, lambda i: np.repeat(chunked(i["L2_attn_x_proj_w"].T[:, 32:33], 2), P, axis=1)),
    "m_dt_b": (1, lambda i: np.broadcast_to(i["L2_attn_x_proj_b"][32:33].reshape(1, 1), (P, 1))),
    "m_alog": (32, lambda i: chunked(i["L2_attn_A_log"], 2)), "m_d": (2, lambda i: col(i["L2_attn_D"])),
    "m_out": (2 * P, lambda i: chunked(i["L2_attn_out_proj_w"].T, 2)), "m_out_b": (P, lambda i: row(i["L2_attn_out_proj_b"])),
    "m_gamma": (P, lambda i: np.broadcast_to(row(i["L2_attn_ln_gamma"]), (P, P))), "m_beta": (P, lambda i: np.broadcast_to(row(i["L2_attn_ln_beta"]), (P, P))),
    "x2_wq": (P, lambda i: i["L2_xattn_Wq"].T), "x2_wk": (P, lambda i: i["L2_xattn_Wk"].T),
    "x2_wv": (P, lambda i: i["L2_xattn_Wv"].T), "x2_wo": (GROUPS * P, lambda i: by_group(i["L2_xattn_Wo"].T)),
    "x2_bq": (1, lambda i: col(i["L2_xattn_bq"])), "x2_bk": (1, lambda i: col(i["L2_xattn_bk"])),
    "x2_bv": (P, lambda i: row(i["L2_xattn_bv"])), "x2_bo": (P, lambda i: row(i["L2_xattn_bo"])),
    "f2_router": (E8, lambda i: i["L2_ffn_router_w"].T), "f2_router_b": (E8, lambda i: np.broadcast_to(row(i["L2_ffn_router_b"]), (P, E8))),
    "f2_temp": (1, lambda i: np.broadcast_to(i["L2_ffn_temperature"].reshape(1, 1), (P, 1))),
    "a3_g": (P, lambda i: np.broadcast_to(row(i["L3_attn_ln_gamma"]), (P, P))), "a3_b": (P, lambda i: np.broadcast_to(row(i["L3_attn_ln_beta"]), (P, P))),
    "a3_wq": (P, lambda i: i["L3_attn_w_qkv"][:, 0:P]), "a3_wk": (P, lambda i: i["L3_attn_w_qkv"][:, P:2 * P]),
    "a3_wv": (P, lambda i: i["L3_attn_w_qkv"][:, 2 * P:3 * P]), "a3_wo": (GROUPS * P, lambda i: by_group(i["L3_attn_w_out"])),
    "f3_router": (E8, lambda i: i["L3_ffn_gate_w"]),
}
WIDE = {
    "x3_wq": (8 * P, lambda i: i["L3_xattn_WQ"].transpose(1, 0, 2).reshape(P, -1)), "x3_wk": (8 * P, lambda i: i["L3_xattn_WK"].transpose(1, 0, 2).reshape(P, -1)),
    "x3_wv": (8 * P, lambda i: i["L3_xattn_WV"].transpose(1, 0, 2).reshape(P, -1)),
    "x3_bq": (8, lambda i: col(i["L3_xattn_bQ"])), "x3_bk": (8, lambda i: col(i["L3_xattn_bK"])), "x3_bv": (8 * P, lambda i: np.broadcast_to(row(i["L3_xattn_bV"]), (P, 8 * P))),
    "x3_wo": (8 * P, lambda i: chunked(i["L3_xattn_WO"], 8)), "x3_bo": (P, lambda i: row(i["L3_xattn_bO"])),
}
FFN0 = {}
for _e in range(E8):
    FFN0[f"g{_e}"] = (512, lambda i, e=_e: i["L0_ffn_gate_w"][e].T)
    FFN0[f"u{_e}"] = (512, lambda i, e=_e: i["L0_ffn_up_w"][e].T)
    FFN0[f"d{_e}"] = (512, lambda i, e=_e: chunked(i["L0_ffn_down_w"][e].T, 4))
FFN2, FFN3 = {}, {}
for _e in range(E8):
    FFN2[f"g{_e}"] = (256, lambda i, e=_e: i["L2_ffn_wg"][e])
    FFN2[f"u{_e}"] = (256, lambda i, e=_e: i["L2_ffn_wp"][e])
    FFN2[f"d{_e}"] = (256, lambda i, e=_e: chunked(i["L2_ffn_wo"][e], 2))
for _e in range(E8):
    FFN3[f"w{_e}"] = (256, lambda i, e=_e: i["L3_ffn_w1"][e])
    FFN3[f"o{_e}"] = (256, lambda i, e=_e: chunked(i["L3_ffn_w2"][e], 2))
    FFN3[f"b{_e}"] = (2, lambda i, e=_e: col(i["L3_ffn_b1"][e]))
FFN3["b2"] = (E8 * P, lambda i: row(i["L3_ffn_b2"]))
FFN1 = {
    "L1_g": (384, lambda i: i["L1_ffn_w_gate"].T), "L1_u": (384, lambda i: i["L1_ffn_w_up"].T), "L1_d": (384, lambda i: chunked(i["L1_ffn_w_down"].T, 3)),
}
INTS = {
    "m0": (B * KPAD, lambda i: np.broadcast_to(np.pad(i["mask_Bx1x1xS2_ik0"].reshape(B, S2), ((0, 0), (0, KPAD - S2))).reshape(1, -1), (P, B * KPAD))),
    "kq": (B * KPAD, lambda i: np.broadcast_to(np.pad(i["mask_BxS2_ik0"], ((0, 0), (0, KPAD - S2))).reshape(1, -1), (P, B * KPAD))),
    "kt": (B, lambda i: i["mask_BxS2_ik0"].T[0:KMAIN]), "kr": (B, lambda i: quads(i["mask_BxS2_ik0"].T)),
    "aq": (QT * KPAD, lambda i: chunked(np.pad(i["mask_SxS2_ik1"], ((0, 0), (0, KPAD - S2))), QT)),
    "at": (S, lambda i: i["mask_SxS2_ik1"].T[0:KMAIN]), "ar": (S, lambda i: quads(i["mask_SxS2_ik1"].T)),
    "len": (B, lambda i: np.broadcast_to(i["_lenS2"].reshape(1, B), (P, B))),
}


def rope():
    inv = 1.0 / 10000.0 ** (np.arange(0, HD, 2, dtype=np.float32) / HD)
    ang = np.outer(np.arange(S, dtype=np.float32), inv)
    cos, sin = np.cos(ang), np.sin(ang)
    c = np.repeat(cos.T, 2, axis=0)
    s = np.stack([-sin.T, sin.T], axis=1).reshape(HD, S)
    return np.tile(c, (HEADS, 1)).astype(np.float32), np.tile(s, (HEADS, 1)).astype(np.float32)


def keys_of_rest():
    return KMAIN + np.arange(P) % 32


CONSTF = {
    "cos": (S, lambda: rope()[0]), "sin": (S, lambda: rope()[1]),
    "headsel": (HEADS, lambda: np.arange(P)[:, None] // HD == np.arange(HEADS)), "halfsel": (2, lambda: np.arange(P)[:, None] // XHD == np.arange(2)),
    "sums": (GROUP, lambda: np.arange(P)[:, None] == 32 * np.arange(GROUP) + HD), "stackheads": (GROUP, lambda: stack_heads()), "rank": (E8, lambda: np.broadcast_to(E8 - np.arange(E8), (P, E8))),
    "kidx": (KPAD, lambda: np.broadcast_to(np.arange(KPAD), (P, KPAD))), "kcol": (1, lambda: np.arange(P)[:, None]), "krem": (1, lambda: keys_of_rest()[:, None]),
}
TRIL = {"tril": (QT * S, lambda: chunked(np.tril(np.ones((S, S))), QT))}
CONSTB = {
    "identb": (P, lambda: np.eye(P)), "negi": (P, lambda: NEG * np.eye(P)), "onesb": (S, lambda: np.ones((P, S))),
    "sel": (32 * P, lambda: np.repeat((np.arange(P)[:, None] % 32 == np.arange(32)) & (np.arange(P)[:, None] < 96), P, axis=1)),
    "pageq": (P, lambda: np.arange(P)[None] // PAGE > np.arange(P)[:, None] // PAGE),
    "paget": (P, lambda: np.arange(P)[:, None] // PAGE > np.arange(P)[None] // PAGE),
    "cq": (QT * KPAD, lambda: chunked(np.arange(KPAD)[None] > np.arange(S)[:, None], QT)),
    "ct": (S, lambda: np.arange(P)[:, None] > np.arange(S)[None]),
    "cr": (S, lambda: keys_of_rest()[:, None] > np.arange(S)[None]),
}




def placer(group, targets):
    out = np.zeros((P, P))
    for t in targets:
        out[32 * group + np.arange(32), 32 * t + np.arange(32)] = 1
    return out


def key_rows():
    out = np.zeros((P, P))
    out[0, MASKROW] = out[32, MASKROW + 1] = 1
    out[ONEROW, MROW:MROW + 2 * GROUP] = 1
    return out


def query_rows():
    out = np.zeros((P, P))
    out[ONEROW, MASKROW:MASKROW + 2] = 1
    return out


def stack_heads():
    out = np.zeros((P, GROUP))
    for j in range(GROUP):
        for t in range(3):
            out[32 * t + HD * j:32 * t + HD * (j + 1), j] = 1
        out[MROW + 2 * j:MROW + 2 * j + 2, j] = 1
    out[MASKROW:MASKROW + 2] = 1
    return out


PLACE = {}
for _g in range(GROUPS):
    PLACE[f"q_hi{_g}"] = (P, lambda g=_g: placer(g, (0, 1)))
    PLACE[f"q_lo{_g}"] = (P, lambda g=_g: placer(g, (2,)))
    PLACE[f"k_hi{_g}"] = (P, lambda g=_g: placer(g, (0, 2)))
    PLACE[f"k_lo{_g}"] = (P, lambda g=_g: placer(g, (1,)))
PLACE["identr"] = (3 * P, lambda: np.pad(np.eye(P), ((0, 0), (P, P))))
PLACE["key_rows"] = (P, key_rows)
PLACE["query_rows"] = (P, query_rows)


def offsets(table):
    at, out = 0, {}
    for name, (n, _) in table.items():
        out[name] = (at, n)
        at += n
    return out, at



class Sems:

    def __init__(self, nc):
        self.nc, self.by = nc, {}

    def __call__(self, name):
        if name not in self.by:
            self.by[name] = self.nc.alloc_semaphore(name)
        return self.by[name]


class Chain:

    def __init__(self, eng, sem):
        self.eng, self.sem, self.n = eng, sem, 0

    def link(self, ins):
        self.n += 1
        ins.then_inc(self.sem, 1)
        self.eng.wait_ge(self.sem, self.n)


def over(ap, axis, n):
    v = ap.unsqueeze(axis)
    shape = list(v.shape)
    shape[axis] = n
    return v.to_broadcast(shape)


class Net:

    def __init__(self, nc, ctx):
        self.nc, self.ctx = nc, ctx
        self.sem = Sems(nc)
        self.names = 0
        self.x = self.sb("x", [P, B * QT, P])
        self.xnT_all = self.sb("xnT_all", [P, B * S])
        self.logits = self.sb("logits", [P, QT, B, E8])
        self.coef = self.sb("coef", [P, QT, B, E8])
        self.ps = [ctx.enter_context(nc.psum_tensor(f"bank{n}", [P, 512], F32)) for n in range(8)]
        self.weights = {}

    def sb(self, name, shape, dt=F32):
        return self.ctx.enter_context(self.nc.sbuf_tensor(name, shape, dt))

    def table(self, name, table, dt=F32, tile=None):
        offs, n = offsets(table)
        t = self.sb(name, [P, n], dt) if tile is None else tile
        return t, offs, n

    def w(self, name):
        t, (at, n) = self.weights[name]
        return t[:, at:at + n]


def end_of_block(net):
    nums = sorted(s.num for s in net.sem.by.values())
    assert nums[-1] - nums[0] + 1 == len(nums)
    net.nc.vector.sem_clear(range(nums[0], nums[-1] + 1))
    net.nc.all_engine_barrier()



def vector_layernorm(dve, ch, xin, xn, n, done=None):
    for t in range(n.tiles):
        last = dve.bn_stats(n.stats[:, t, :], xin[:, t, :])
    ch.link(last)
    for t in range(n.tiles):
        last = dve.bn_aggr(n.aggr[:, t, :], n.stats[:, t, :])
    ch.link(last)
    ch.link(dve.tensor_scalar(n.var[:], n.aggr[:, :, 1], EPS, None, ALU.add))
    dve.tensor_scalar(n.vh[:], n.var[:], -0.5, None, ALU.mult)
    ch.link(dve.tensor_scalar(n.bits[:], n.var[:].bitcast(I32), 1, None, ALU.logical_shift_right))
    ch.link(dve.tensor_scalar(n.rstd[:].bitcast(I32), n.bits[:], -1.0, float(0x5F3759DF), ALU.mult, ALU.add))
    for _ in range(3):
        ch.link(dve.tensor_tensor(n.sq[:], n.rstd[:], n.rstd[:], ALU.mult))
        ch.link(dve.tensor_tensor(n.sq[:], n.sq[:], n.vh[:], ALU.mult))
        ch.link(dve.scalar_tensor_tensor(n.rstd[:], n.sq[:], 1.5, n.rstd[:], ALU.add, ALU.mult))
    for t in range(n.tiles):
        last = dve.tensor_scalar(xn[:, t, :], xin[:, t, :], n.aggr[:, t, 0:1], n.rstd[:, t:t + 1], ALU.subtract, ALU.mult)
        if done is not None and t % QT == QT - 1:
            last.then_inc(done, 1)
    return last


def tensor_transpose_tiles(pe, out, tiles, ident):
    for t in range(QT):
        last = pe.transpose(out[:, t * P:(t + 1) * P], tiles[:, t, :], ident)
    return last


class Norm:

    def __init__(self, net, sb, tiles=QT):
        self.tiles = tiles
        self.xn = sb("xn", [P, tiles, P])
        self.stats = sb("stats", [P, tiles, LN_BN])
        self.aggr = sb("aggr", [P, tiles, 2])
        self.rstd = sb("rstd", [P, tiles])
        self.var, self.vh, self.sq = sb("var", [P, tiles]), sb("vh", [P, tiles]), sb("sq", [P, tiles])
        self.bits = sb("bits", [P, tiles], I32)
        if tiles == QT:
            self.xnT = sb("xnT", [P, S])


def x_of(net, b):
    return net.x[:, bass.ts(b, QT), :]



def single_head_block(net, b, k):
    nc, sem, ps, w = net.nc, net.sem, net.ps, net.w
    scale = 1.0 / float(np.sqrt(np.float32(P)))
    with nc.Block() as block:

        @block.vector
        def _(dve):
            ch = Chain(dve, sem("dve_chain"))
            vector_layernorm(dve, ch, x_of(net, b), k.n.xn, k.n).then_inc(sem("xn_ready"), 1)
            dve.wait_ge(sem("q_done"), 1)
            dve.tensor_scalar(k.qT[:], ps[0][:], w("a0_bq"), None, ALU.add).then_inc(sem("qT_ready"), 1)
            dve.wait_ge(sem("k_done"), 1)
            dve.tensor_scalar(k.kT[:], ps[1][:], w("a0_bk"), None, ALU.add).then_inc(sem("kT_ready"), 1)
            tril = w("tril").rearrange("p (t k) -> p t k", t=QT)
            for t in range(QT):
                dve.wait_ge(sem("scores_done"), t + 1)
                ch.link(dve.scalar_tensor_tensor(k.s[:, t, :], ps[t][:], scale, tril[:, t, :], ALU.mult, ALU.mult))
                ch.link(dve.reduce_max(k.mx[:, t:t + 1], k.s[:, t, :], AX))
                dve.tensor_scalar(k.negm[:, t:t + 1], k.mx[:, t:t + 1], -1.0, None, ALU.mult).then_inc(sem("negm_ready"), 1)
            dve.wait_ge(sem("exp_done"), QT)
            dve.wait_ge(sem("v_done"), 1)
            ch.link(dve.reciprocal(k.rs[:], k.sum[:]))
            ch.link(dve.tensor_tensor(k.rs[:], k.rs[:], k.sum[:], ALU.mult))
            for t in range(QT):
                last = dve.scalar_tensor_tensor(x_of(net, b)[:, t, :], ps[4][:, t * P:(t + 1) * P], k.rs[:, t:t + 1],
                                                x_of(net, b)[:, t, :], ALU.mult, ALU.add)
            ch.link(last)

        @block.scalar
        def _(act):
            act.wait_ge(sem("xT_done"), 1)
            nc.scalar.copy(k.n.xnT[:], ps[7][:]).then_inc(sem("xnT_ready"), 1)
            for t in range(QT):
                act.wait_ge(sem("negm_ready"), t + 1)
                nc.scalar.activation(k.p[:, t, :], k.s[:, t, :], ACT.Exp, bias=k.negm[:, t:t + 1],
                                     accum_out=k.sum[:, t:t + 1]).then_inc(sem("exp_done"), 1)

        @block.tensor
        def _(pe):
            pe.wait_ge(sem("xn_ready"), 1)
            tensor_transpose_tiles(pe, ps[7], k.n.xn, w("ident")).then_inc(sem("xT_done"), 1)
            pe.wait_ge(sem("xnT_ready"), 1)
            pe.matmul(ps[0][:], w("a0_wq"), k.n.xnT[:], start=True, stop=True).then_inc(sem("q_done"), 1)
            pe.matmul(ps[1][:], w("a0_wk"), k.n.xnT[:], start=True, stop=True).then_inc(sem("k_done"), 1)
            for t in range(QT):
                pe.matmul(ps[4][:, t * P:(t + 1) * P], k.n.xnT[:, t * P:(t + 1) * P], w("a0_wv"), start=True, stop=False)
                last = pe.matmul(ps[4][:, t * P:(t + 1) * P], w("ones")[0:1, :], w("a0_bv")[0:1, :], start=False, stop=True)
            last.then_inc(sem("v_done"), 1)
            pe.wait_ge(sem("qT_ready"), 1)
            pe.wait_ge(sem("kT_ready"), 1)
            for t in range(QT):
                pe.matmul(ps[t][:], k.qT[:, t * P:(t + 1) * P], k.kT[:], start=True, stop=True).then_inc(sem("scores_done"), 1)
    end_of_block(net)





class Narrow:

    def __init__(self, net, sb, kind, ctx_keys):
        self.kind, self.ctx_keys = kind, ctx_keys
        self.nk = KPAD if ctx_keys else S
        self.nkt = 1 if ctx_keys else QT
        self.q_hi, self.q_lo = sb("q_hi", [P, B * S], F32R), sb("q_lo", [P, B * S], F32R)
        self.k_hi, self.k_lo = sb("k_hi", [P, B * self.nk], F32R), sb("k_lo", [P, B * self.nk], F32R)
        self.values = sb("values", [P, B * self.nkt * P])
        self.rests = sb("rests", [P, B * P]) if ctx_keys else None

    def more_buffers(self, net, sb):
        masks = BODY if self.kind in ("row", "add") else 1
        self.rows = sb("rows", [P, masks, self.nk], F32R)
        self.Q = sb("Q", [P, 2, S], F32R)
        self.K = sb("K", [P, 2, GROUP, self.nk], F32R)
        self.v = sb("v", [P, 2, self.nkt, GROUP, 32])
        self.p = sb("p", [P, 3, S])
        self.m = sb("m", [P, QT, HEADS])
        self.mp = sb("mp", [P, 2, QT, P], F32R)
        self.o = sb("o", [P, 2, S])
        self.rs = sb("rs", [P, QT * GROUP])
        self.rx = sb("rx", [P, QT, P])
        if self.kind in ("row", "add"):
            self.ones = sb("ones", [P, S], F32R)
        if self.ctx_keys:
            self.kr = sb("kr", [P, 2, GROUP, KPAD - KMAIN], F32R)
            self.vr = sb("vr", [P, 2, P])
            self.rf = sb("rf", [P, KPAD])
            self.rb = sb("rb", [P, 2, KPAD], F32R) if self.kind == "add" else None
        if self.kind == "full":
            self.mq = sb("mq", [P, BODY, QT, KPAD], BF16)
            self.mt = sb("mt", [P, BODY, S], BF16)
            self.mr = sb("mr", [P, BODY, S], BF16)
            self.kc = sb("kc", [P, 2])

    def chunks(self, g):
        if self.ctx_keys:
            return [(t, h, 2, S2) for t in range(QT) for h in (GROUP * g, GROUP * g + 2)]
        return [(t, h, 1, (t + 1) * P if self.kind == "page" else S) for t in range(QT) for h in range(GROUP * g, GROUP * (g + 1))]

    def units(self, g):
        if self.ctx_keys:
            return [("rest", g, 0, 0)] + [("main", h, 0, 0) for h in range(GROUP * g, GROUP * (g + 1))]
        return [("main", h, c, c * P if self.kind == "page" else 0) for h in range(GROUP * g, GROUP * (g + 1)) for c in range(QT)]


def narrow_project(net, k, pre, scale, sb):
    nc, sem, ps, w = net.nc, net.sem, net.ps, net.w
    n = Norm(net, sb, B * QT)
    full = sb("full", [P, 2, S])
    if k.kind == "page":
        lat, turned = sb("lat", [64, B * S]), sb("turned", [P, 2, S])
    bias = pre.startswith("x")
    xnT = net.xnT_all
    with nc.Block() as block:

        @block.vector
        def _(dve):
            ch = Chain(dve, sem("dve_chain"))
            if pre == "a3":
                ch.link(vector_layernorm(dve, ch, net.x, n.xn, n))
                ch.link(vector_layernorm(dve, ch, n.xn, n.xn, n))
                for b in range(B):
                    tiles = n.xn[:, b * QT:(b + 1) * QT, :]
                    ch.link(dve.tensor_tensor(tiles, tiles, over(w("a3_g"), 1, QT), ALU.mult))
                    dve.tensor_tensor(tiles, tiles, over(w("a3_b"), 1, QT), ALU.add).then_inc(sem("xn_ready"), 1)
            else:
                vector_layernorm(dve, ch, net.x, n.xn, n, sem("xn_ready"))
            for b in range(B):
                for i, (name, hi, lo, m) in enumerate((("k", k.k_hi, k.k_lo, k.nk), ("q", k.q_hi, k.q_lo, S))):
                    s = scale if name == "q" else 1.0
                    out, at = full[:, i, 0:m], slice(b * m, (b + 1) * m)
                    dve.wait_ge(sem(f"{name}_done"), b + 1)
                    if k.kind == "page":
                        dve.scalar_tensor_tensor(turned[:, 0, :], ps[2 * i][:], s, w("cos"), ALU.mult, ALU.mult)
                        ch.link(dve.scalar_tensor_tensor(turned[:, 1, :], ps[2 * i + 1][:], s, w("sin"), ALU.mult, ALU.mult))
                        ch.link(dve.tensor_tensor(out, turned[:, 0, :], turned[:, 1, :], ALU.add))
                    elif bias:
                        ch.link(dve.tensor_scalar(out, ps[2 * i][:, 0:m], w(f"{pre}_b{name}"), s, ALU.add, ALU.mult))
                    else:
                        ch.link(dve.tensor_scalar(out, ps[2 * i][:, 0:m], s, None, ALU.mult))
                    ch.link(dve.tensor_copy(hi[:, at], out))
                    dve.tensor_tensor(lo[:, at], out, hi[:, at].bitcast(F32), ALU.subtract).then_inc(sem(f"{name}_parts"), 1)

        @block.scalar
        def _(act):
            for b in range(B):
                act.wait_ge(sem("xT_done"), b + 1)
                nc.scalar.copy(xnT[:, b * S:(b + 1) * S], ps[6 + b % 2][:]).then_inc(sem("xnT_ready"), 1)
                if k.kind == "page":
                    act.wait_ge(sem("lat_done"), b + 1)
                    nc.scalar.copy(lat[:, b * S:(b + 1) * S], ps[6 + b % 2][0:64, :]).then_inc(sem("lat_ready"), 1)
                act.wait_ge(sem("v_done"), b + 1)
                if k.ctx_keys:
                    nc.scalar.copy(k.values[:, b * P:(b + 1) * P], ps[4 + b % 2][:, 0:P])
                    nc.scalar.copy(k.rests[:, b * P:(b + 1) * P], ps[4 + b % 2][:, P:2 * P]).then_inc(sem("v_kept"), 1)
                else:
                    nc.scalar.copy(k.values[:, b * S:(b + 1) * S], ps[4 + b % 2][:]).then_inc(sem("v_kept"), 1)

        @block.tensor
        def _(pe):
            ctx = w("ctxT").rearrange("p (b k) -> p b k", b=B)

            for b in range(B):
                pe.wait_ge(sem("xn_ready"), b + 1)
                if b >= 2:
                    pe.wait_ge(sem("lat_ready" if k.kind == "page" else "xnT_ready"), b - 1)
                tensor_transpose_tiles(pe, ps[6 + b % 2], n.xn[:, b * QT:(b + 1) * QT, :], w("ident")).then_inc(sem("xT_done"), 1)
                pe.wait_ge(sem("xnT_ready"), b + 1)
                x = xnT[:, b * S:(b + 1) * S]
                if b >= 1:
                    pe.wait_ge(sem("q_parts"), b)
                if k.kind == "page":
                    pe.matmul(ps[6 + b % 2][0:64, :], w("a1_down"), x, start=True, stop=True).then_inc(sem("lat_done"), 1)
                    pe.matmul(ps[2][:], w("a1_wq"), x, start=True, stop=True)
                    pe.matmul(ps[3][:], w("a1_wqs"), x, start=True, stop=True).then_inc(sem("q_done"), 1)
                    pe.wait_ge(sem("lat_ready"), b + 1)
                    src = lat[:, b * S:(b + 1) * S]
                    pe.matmul(ps[0][:], w("a1_wk")[0:64, :], src, start=True, stop=True)
                    pe.matmul(ps[1][:], w("a1_wks")[0:64, :], src, start=True, stop=True).then_inc(sem("k_done"), 1)
                else:
                    pe.matmul(ps[0][:, 0:k.nk], w(f"{pre}_wk"), ctx[:, b, :] if k.ctx_keys else x, start=True, stop=True).then_inc(sem("k_done"), 1)
                    pe.matmul(ps[2][:], w(f"{pre}_wq"), x, start=True, stop=True).then_inc(sem("q_done"), 1)
                    src = x
                if b >= 2:
                    pe.wait_ge(sem("v_kept"), b - 1)
                out = ps[4 + b % 2]
                if k.ctx_keys:
                    pe.matmul(out[:, 0:P], ctx[:, b, 0:P], w(f"{pre}_wv"), start=True, stop=False)
                    pe.matmul(out[:, 0:P], w("ones")[0:1, :], w(f"{pre}_bv")[0:1, :], start=False, stop=True)
                    pe.matmul(out[:, P:2 * P], w("restT")[:, b * P:(b + 1) * P], w(f"{pre}_wv"), start=True, stop=False)
                    last = pe.matmul(out[:, P:2 * P], w("ones")[0:1, :], w(f"{pre}_bv")[0:1, :], start=False, stop=True)
                else:
                    for c in range(QT):
                        last = pe.matmul(out[:, c * P:(c + 1) * P], src[:, c * P:(c + 1) * P], w(f"{pre}_wv")[0:src.shape[0], :], start=True, stop=True)
                last.then_inc(sem("v_done"), 1)
    end_of_block(net)


def narrow_prepare(net, k):
    with net.nc.Block() as block:

        @block.vector
        def _(dve):
            ch = Chain(dve, net.sem("dve_chain"))
            dve.memset(k.mp[:].bitcast(F32), 0.0)
            dve.memset(k.rows[:].bitcast(F32), 0.0)
            if k.kind in ("row", "add"):
                dve.memset(k.ones[:].bitcast(F32), 0.0)
            if k.ctx_keys:
                dve.memset(k.vr[:], 0.0)
            ch.link(dve.memset(k.v[:], 0.0))
            dve.memset(k.v[:, :, :, :, HD:HD + 1], 1.0)
            dve.memset(k.rows[ONEROW:ONEROW + 1].bitcast(F32), 1.0)
            if k.kind in ("row", "add"):
                dve.memset(k.mp[:, :, :, MASKROW:MASKROW + 2].bitcast(F32), 1.0)
                dve.memset(k.ones[ONEROW:ONEROW + 1, :].bitcast(F32), 1.0)
            if k.ctx_keys:
                for j in range(GROUP):
                    dve.memset(k.vr[32 * j:32 * j + KREM, :, 32 * j + HD:32 * j + HD + 1], 1.0)
            last = dve.memset(k.m[:], 0.0)
            if k.kind in ("row", "add"):
                last = dve.memset(k.rows[0:1, :, S2:KPAD].bitcast(F32), NEG)
            ch.link(last)
    end_of_block(net)


def vector_narrow_masks(net, dve, ch, k, b, e):
    w = net.w
    if k.kind == "row":
        m0 = w("m0").rearrange("p (b k) -> p b k", b=B)
        ch.link(dve.tensor_copy(k.rf[:], m0[:, b, :]))
        ch.link(dve.tensor_scalar(k.rows[0:1, e, 0:S2], k.rf[0:1, 0:S2], 0.0, NEG, ALU.is_equal, ALU.mult))
    if k.kind == "add":
        pad = w("x1_pad").rearrange("p (b k) -> p b k", b=B)
        ch.link(dve.tensor_scalar(k.rf[:], pad[:, b, :], -1e12, None, ALU.mult))
        ch.link(dve.tensor_copy(k.rb[:, 0, :], k.rf[:]))
        ch.link(dve.tensor_tensor(k.rb[:, 1, :], k.rf[:], k.rb[:, 0, :].bitcast(F32), ALU.subtract))
        for n in range(2):
            last = dve.tensor_copy(k.rows[32 * n:32 * n + 1, e, 0:S2], k.rb[32 * n:32 * n + 1, n, 0:S2].bitcast(F32))
        ch.link(last)
    if k.kind == "full":
        kq = w("kq").rearrange("p (b k) -> p b k", b=B)
        aq = w("aq").rearrange("p (t k) -> p t k", t=QT)
        dve.tensor_scalar(k.rf[:], kq[:, b, :], 0, None, ALU.not_equal)
        dve.tensor_scalar(k.kc[:, 0:1], w("kt")[:, bass.ts(b, 1)], 0, None, ALU.not_equal)
        ch.link(dve.tensor_scalar(k.kc[:, 1:2], w("kr")[:, bass.ts(b, 1)], 0, None, ALU.not_equal))
        for t in range(QT):
            dve.scalar_tensor_tensor(k.mq[:, e, t, :], aq[:, t, :], 0.0, k.rf[:], ALU.not_equal, ALU.max)
        dve.tensor_scalar(k.mt[:, e], w("at"), 0.0, k.kc[:, 0:1], ALU.not_equal, ALU.max)
        ch.link(dve.tensor_scalar(k.mr[:, e], w("ar"), 0.0, k.kc[:, 1:2], ALU.not_equal, ALU.max))



def narrow_block(net, b0, k, pre):
    nc, sem, ps, w = net.nc, net.sem, net.ps, net.w
    bias = pre.startswith("x")
    nk = k.nk
    groups = BODY * GROUPS
    units = [(n,) + u for n in range(groups) for u in k.units(n % GROUPS)]
    chunks = [(n,) + c for n in range(groups) for c in k.chunks(n % GROUPS)]
    per_group, nchunks = len(units) // groups, len(chunks) // groups
    oT = net.xnT_all[:].rearrange("p (g q) -> p g q", g=GROUPS)

    def ends(n):
        return n % GROUPS == GROUPS - 1

    with nc.Block() as block:

        @block.vector
        def _(dve):
            ch = Chain(dve, sem("dve_chain"))

            def masks(e):
                if k.kind in ("row", "add", "full"):
                    vector_narrow_masks(net, dve, ch, k, b0 + e, e)
                    dve.sem_inc(sem("masks_ready"), 1)

            def stack_keys(n):
                if n >= 2:
                    dve.wait_ge(sem("st_done"), per_group * (n - 1))
                dve.wait_ge(sem("k_stacked"), n + 1)
                if k.ctx_keys:
                    dve.tensor_tensor(k.kr[:, n % 2], over(ps[7][:, KMAIN:KPAD], 1, GROUP), over(w("stackheads"), 2, KPAD - KMAIN), ALU.mult)
                dve.tensor_tensor(k.K[:, n % 2], over(ps[7][:, 0:nk], 1, GROUP), over(w("stackheads"), 2, nk), ALU.mult).then_inc(sem("K_ready"), 1)

            def maxima(n):
                for i in range(nchunks * n, nchunks * (n + 1)):
                    _, t, h, m, keys = chunks[i]
                    dve.wait_ge(sem("scores_done"), i + 1)
                    dve.reduce_max(k.m[:, t, h:h + m], ps[3 + i % 2][:, 0:m * keys].rearrange("p (h k) -> p h k", h=m), AX).then_inc(sem("max_done"), 1)
                dve.wait_ge(sem("max_done"), nchunks * (n + 1))
                if n >= 2:
                    dve.wait_ge(sem("mT_done"), n - 1)
                g = n % GROUPS
                hi = k.mp[:, n % 2, :, MROW:MROW + 2 * GROUP:2]
                lo = k.mp[:, n % 2, :, MROW + 1:MROW + 2 * GROUP:2]
                top = k.m[:, :, GROUP * g:GROUP * (g + 1)]
                ch.link(dve.tensor_scalar(hi, top, -1.0, None, ALU.mult))
                dve.scalar_tensor_tensor(lo, top, -1.0, hi.bitcast(F32), ALU.mult, ALU.subtract).then_inc(sem("mp_ready"), 1)

            def normalise(n):
                dve.wait_ge(sem("sums_done"), n + 1)
                ch.link(dve.reciprocal(k.rs[:], ps[5 + n % 2][:, 0:QT * GROUP]))
                dve.tensor_copy(k.rx[:].rearrange("p t (j r) -> p (t j) r", j=GROUP), over(k.rs[:], 2, 32)).then_inc(sem("rx_ready"), 1)
                dve.wait_ge(sem("factors_done"), n + 1)
                if n >= GROUPS:
                    dve.wait_ge(sem("y_done"), n // GROUPS)
                dve.tensor_tensor(oT[:, n % GROUPS, :], k.o[:, n % 2, :], ps[5 + n % 2][:], ALU.mult).then_inc(sem("oT_ready"), 1)

            def add_output(e):
                x = x_of(net, b0 + e)
                dve.wait_ge(sem("y_done"), e + 1)
                dve.tensor_tensor(x, x, ps[2][:].rearrange("p (t d) -> p t d", t=QT), ALU.add).then_inc(sem("x_added"), 1)

            masks(0)
            for n in range(groups):
                stack_keys(n)
                if n + 1 < BODY:
                    masks(n + 1)
                maxima(n)
                if n >= 2:
                    normalise(n - 2)
                if n >= 3 and ends(n - 3):
                    add_output((n - 3) // GROUPS)
            normalise(groups - 2)
            normalise(groups - 1)
            add_output(BODY - 1)
            dve.wait_ge(sem("x_added"), BODY)

        @block.gpsimd
        def _(pool):
            def values(n):
                e, g = divmod(n, GROUPS)
                if n >= 2:
                    pool.wait_ge(sem("pv_done"), per_group * (n - 1))
                all_heads = k.values[:, bass.ts(b0 + e, k.nkt * P)].rearrange("p (c h d) -> p c h d", c=k.nkt, h=HEADS)
                nc.gpsimd.tensor_copy(k.v[:, n % 2, :, :, 0:HD], all_heads[:, :, GROUP * g:GROUP * (g + 1), :]).then_inc(sem("v_ready"), 1)
                if k.ctx_keys:
                    rests = k.rests[:, bass.ts(b0 + e, P)].rearrange("p (h d) -> p h d", h=HEADS)
                    for j in range(GROUP):
                        pool.wait_ge(sem("v_ready"), (GROUP + 1) * n + j + 1)
                        rows = slice(32 * j, 32 * j + KREM)
                        nc.gpsimd.tensor_copy(k.vr[rows, n % 2, 32 * j:32 * j + HD], rests[rows, GROUP * g + j, :]).then_inc(sem("v_ready"), 1)
                    pool.wait_ge(sem("v_ready"), (GROUP + 1) * (n + 1))
                else:
                    pool.wait_ge(sem("v_ready"), n + 1)

            for n in range(groups):
                values(n)

        @block.scalar
        def _(act):
            def copy_queries(n):
                act.wait_ge(sem("q_stacked"), n + 1)
                nc.scalar.copy(k.Q[:, n % 2, :], ps[2][:]).then_inc(sem("Q_ready"), 1)

            def copy_maxima(n):
                act.wait_ge(sem("mT_done"), n + 1)
                nc.scalar.copy(k.Q[MROW:P, n % 2, :], ps[7][MROW:P, :]).then_inc(sem("maxima_in"), 1)

            def copy_products(n):
                act.wait_ge(sem("pv_done"), per_group * (n + 1))
                if n >= 2:
                    act.wait_ge(sem("oT_ready"), n - 1)
                nc.scalar.copy(k.o[:, n % 2, :], ps[5 + n % 2][:]).then_inc(sem("o_ready"), 1)

            copy_queries(0)
            copy_maxima(0)
            for u, (n, what, h, kt, q0) in enumerate(units):
                at = u % per_group
                act.wait_ge(sem("st_done"), u + 1)
                if u >= 3:
                    act.wait_ge(sem("pv_done"), u - 2)
                nc.scalar.activation(k.p[:, u % 3, q0:S], ps[u % 2][:, q0:S], ACT.Exp).then_inc(sem("exp_done"), 1)
                if at == 0 and n + 1 < groups:
                    copy_queries(n + 1)
                if at == 2 and n >= 1:
                    copy_products(n - 1)
                if at == per_group - 1 and n + 1 < groups:
                    copy_maxima(n + 1)
            copy_products(groups - 1)

        @block.tensor
        def _(pe):
            def stack_parts(n):
                e, g = divmod(n, GROUPS)
                q_at, k_at = bass.ts(b0 + e, S), bass.ts(b0 + e, nk)
                rowmask = k.kind in ("row", "add")
                if g == 0 and k.ctx_keys:
                    pe.wait_ge(sem("masks_ready"), e + 1)
                if n >= 1:
                    pe.wait_ge(sem("maxima_in"), n)
                keys = ps[7][:, 0:nk]
                pe.matmul(keys, w(f"k_hi{g}"), k.k_hi[:, k_at], start=True, stop=False)
                pe.matmul(keys, w(f"k_lo{g}"), k.k_lo[:, k_at], start=False, stop=False)
                pe.matmul(keys, w("key_rows"), k.rows[:, e if rowmask else 0], start=False, stop=True).then_inc(sem("k_stacked"), 1)
                if n >= 1:
                    pe.wait_ge(sem("Q_ready"), n)
                if n >= 4 and ends(n - 4):
                    pe.wait_ge(sem("x_added"), (n - 4) // GROUPS + 1)
                pe.matmul(ps[2][:], w(f"q_hi{g}"), k.q_hi[:, q_at], start=True, stop=False)
                last = pe.matmul(ps[2][:], w(f"q_lo{g}"), k.q_lo[:, q_at], start=False, stop=not rowmask)
                if rowmask:
                    last = pe.matmul(ps[2][:], w("query_rows"), k.ones[:], start=False, stop=True)
                last.then_inc(sem("q_stacked"), 1)

            def first_scores(i):
                n, t, h, m, keys = chunks[i]
                if i % nchunks == 0:
                    pe.wait_ge(sem("Q_ready"), n + 1)
                    pe.wait_ge(sem("K_ready"), n + 1)
                if i >= 2:
                    pe.wait_ge(sem("max_done"), i - 1)
                j = h % GROUP
                out = ps[3 + i % 2][:, 0:m * keys].rearrange("p (h k) -> p h k", h=m)
                last = pe.matmul(out, k.Q[:, n % 2, t * P:(t + 1) * P], k.K[:, n % 2, j:j + m, 0:keys], start=True, stop=k.kind != "full")
                if k.kind == "full":
                    last = pe.matmul(out, w("negi"), over(k.mq[:, n // GROUPS, t, 0:keys], 1, m), start=False, stop=True)
                if k.kind == "page":
                    last = pe.matmul(ps[3 + i % 2][:, t * P:(t + 1) * P], w("negi"), w("pageq"), start=False, stop=True, skip_group_check=True)
                last.then_inc(sem("scores_done"), 1)

            def turn_maxima(n):
                pe.wait_ge(sem("mp_ready"), n + 1)
                for t in range(QT):
                    half, first = ps[7][:, (t // 2) * 2 * P:(t // 2 + 1) * 2 * P], t % 2 == 0
                    last = pe.matmul(half, k.mp[:, n % 2, t, :], w("identr")[:, P if first else 0:3 * P if first else 2 * P], start=first, stop=not first)
                last.then_inc(sem("mT_done"), 1)

            def second_scores(u):
                n, what, h, kt, q0 = units[u]
                if u % per_group == 0:
                    pe.wait_ge(sem("maxima_in"), n + 1)
                if u >= 2:
                    pe.wait_ge(sem("exp_done"), u - 1)
                out = ps[u % 2][:, q0:S]
                keys = k.kr[:, n % 2] if what == "rest" else k.K[:, n % 2, h % GROUP, kt * P:(kt + 1) * P]
                last = pe.matmul(out, keys, k.Q[:, n % 2, q0:S], start=True, stop=k.kind != "full")
                if k.kind == "full":
                    last = pe.matmul(out, w("negi"), (k.mr if what == "rest" else k.mt)[:, n // GROUPS, q0:S], start=False, stop=True)
                if k.kind == "page":
                    last = pe.matmul(ps[u % 2][:, kt * P:(kt + 1) * P], w("negi"), w("paget"), start=False, stop=True, skip_group_check=True)
                last.then_inc(sem("st_done"), 1)

            def products(u):
                n, what, h, kt, q0 = units[u]
                j = h % GROUP
                if u % per_group == 0:
                    pe.wait_ge(sem("v_ready"), (n + 1) * (1 + GROUP if k.ctx_keys else 1))
                    if n >= 2:
                        pe.wait_ge(sem("oT_ready"), n - 1)
                pe.wait_ge(sem("exp_done"), u + 1)
                if what == "rest":
                    last = pe.matmul(ps[5 + n % 2][:], k.vr[:, n % 2, :], k.p[:, u % 3, :], start=True, stop=True, skip_group_check=True)
                else:
                    last = pe.matmul(ps[5 + n % 2][32 * j:32 * (j + 1), q0:S], k.v[:, n % 2, kt, j, :], k.p[:, u % 3, q0:S],
                                     start=not k.ctx_keys and kt == 0, stop=True, skip_group_check=True)
                last.then_inc(sem("pv_done"), 1)

            def pick_sums(n):
                pe.wait_ge(sem("o_ready"), n + 1)
                for t in range(QT):
                    last = pe.matmul(ps[5 + n % 2][:, t * GROUP:(t + 1) * GROUP], k.o[:, n % 2, t * P:(t + 1) * P], w("sums"), start=True, stop=True)
                last.then_inc(sem("sums_done"), 1)

            def spread_factors(n):
                pe.wait_ge(sem("rx_ready"), n + 1)
                tensor_transpose_tiles(pe, ps[5 + n % 2], k.rx, w("ident")).then_inc(sem("factors_done"), 1)

            def output(e, g):
                pe.wait_ge(sem("oT_ready"), GROUPS * e + g + 1)
                if g == 0:
                    pe.wait_ge(sem("Q_ready"), min(groups, GROUPS * (e + 1) + 3))
                for t in range(QT):
                    last = pe.matmul(ps[2][:, t * P:(t + 1) * P], oT[:, g, t * P:(t + 1) * P], w(f"{pre}_wo")[:, g * P:(g + 1) * P],
                                     start=(g == 0 and t == 0), stop=(g == GROUPS - 1), skip_group_check=True)
                    if bias and g == 0:
                        pe.matmul(ps[2][:, t * P:(t + 1) * P], w("ones")[0:1, :], w(f"{pre}_bo")[0:1, :], start=False, stop=False, skip_group_check=True)
                if g == GROUPS - 1:
                    last.then_inc(sem("y_done"), 1)

            stack_parts(0)
            for i in range(nchunks):
                first_scores(i)
            turn_maxima(0)
            i, used = nchunks, 0
            for u in range(len(units)):
                n, at = divmod(u, per_group)
                second_scores(u)
                upto = i
                if at == 0 and n >= 2:
                    spread_factors(n - 2)
                if n + 1 < groups:
                    if at == 0:
                        stack_parts(n + 1)
                    else:
                        upto = nchunks * (n + 1) + min(nchunks, -(-nchunks * at // (per_group - 2)))
                middle = (i + upto + 1) // 2
                while i < middle:
                    first_scores(i)
                    i += 1
                behind = 1 if at == per_group - 1 else 2
                while used < u + 1 - behind:
                    products(used)
                    used += 1
                while i < upto:
                    first_scores(i)
                    i += 1
                if at == 2 and n >= 2 and ends(n - 2):
                    for g in range(GROUPS):
                        output((n - 2) // GROUPS, g)
                if at == 3 and n >= 1:
                    pick_sums(n - 1)
                if at == per_group - 1 and n + 1 < groups:
                    turn_maxima(n + 1)
            spread_factors(groups - 2)
            while used < len(units):
                products(used)
                used += 1
            for g in range(GROUPS - 1):
                output(BODY - 1, g)
            pick_sums(groups - 1)
            spread_factors(groups - 1)
            output(BODY - 1, GROUPS - 1)
    end_of_block(net)



class Wide:

    def __init__(self, net, sb):
        self.src = sb("src", [P, KPAD + P])
        self.qT = sb("qT", [P, HEADS // 2, S])
        self.kk = sb("kk", [P, HEADS, KPAD])
        self.v = sb("v", [P, HEADS, XHD])
        self.vr = sb("vr", [P, HEADS, XHD])
        self.p = sb("p", [P, 2, GROUP, KPAD])
        self.pr = sb("pr", [P, 2, P])
        self.pT = sb("pT", [P, 2, GROUP, P])
        self.prT = sb("prT", [P, 2, P])
        self.m = sb("m", [P, 2, GROUP])
        self.negm = sb("negm", [P, 2, GROUP])
        self.sum = sb("sum", [P, 4, GROUP])
        self.rs = sb("rs", [P, 2, GROUP])
        self.o = sb("o", [P, 2, HEADS * XHD])
        self.oT = sb("oT", [P, 2, 4, P])
        self.mq = sb("mq", [P, QT, KPAD], BF16)
        self.kf = sb("kf", [P, KPAD])
        self.lf = sb("lf", [P, 1])
        self.bq = sb("bq", [P, HEADS // 2])


def wide_prepare(net, k, scale):
    with net.nc.Block() as block:

        @block.vector
        def _(dve):
            ch = Chain(dve, net.sem("dve_chain"))
            dve.memset(k.kk[:], 0.0)
            dve.memset(k.vr[:], 0.0)
            dve.tensor_scalar(k.bq[:], net.w("x3_bq"), scale, None, ALU.mult)
            ch.link(dve.memset(k.p[:], 0.0))
    end_of_block(net)



def wide_block(net, b, k, scale):
    nc, sem, ps, w = net.nc, net.sem, net.ps, net.w
    steps, pairs = QT * GROUPS, HEADS // 2
    rest_cols = slice(3 * P, 4 * P)

    with nc.Block() as block:

        @block.vector
        def _(dve):
            ch = Chain(dve, sem("dve_chain"))
            cq = w("cq").rearrange("p (t k) -> p t k", t=QT)
            ch.link(dve.tensor_copy(k.lf[:], w("len")[:, bass.ts(b, 1)]))
            ch.link(dve.tensor_scalar(k.kf[:], w("kidx"), k.lf[:], None, ALU.is_ge))
            for t in range(QT):
                last = dve.tensor_tensor(k.mq[:, t, :], cq[:, t, :], k.kf[:], ALU.max)
            last.then_inc(sem("mask_ready"), 1)
            for c in range(pairs):
                if c % 4 == 0:
                    heads = slice(2 * c, 2 * c + 8)
                    bias = w("x3_bv").rearrange("p (h d) -> p h d", h=HEADS)
                    dve.wait_ge(sem("v_done"), c // 4 + 1)
                    dve.tensor_tensor(k.v[:, heads, :], ps[4][:].rearrange("p (h d) -> p h d", h=8), bias[:, heads, :], ALU.add).then_inc(sem("v_ready"), 1)
                    for j in range(GROUP):
                        rows, own = slice(32 * j, 32 * j + KREM), slice(2 * c + j, 2 * c + 8, GROUP)
                        dve.tensor_tensor(k.vr[rows, own, :], ps[5][rows, :].rearrange("p (h d) -> p h d", h=8)[:, j::GROUP, :],
                                          bias[rows, own, :], ALU.add).then_inc(sem("v_ready"), 1)
                dve.wait_ge(sem("k_done"), c + 1)
                dve.scalar_tensor_tensor(k.kk[:, 2 * c:2 * c + 2, 0:S2], over(ps[2 + c % 2][:, 0:S2], 1, 2), w("x3_bk")[:, c:c + 1],
                                         over(w("halfsel"), 2, S2), ALU.add, ALU.mult).then_inc(sem("kk_ready"), 1)

            def maxima(n):
                for i in range(2):
                    dve.wait_ge(sem("scores_done"), 2 * n + i + 1)
                    last = dve.reduce_max(k.m[:, n % 2, 2 * i:2 * i + 2], ps[2 * (n % 2) + i][:, 0:2 * S2].rearrange("p (h k) -> p h k", h=2), AX)
                ch.link(last)
                if n >= 2:
                    dve.wait_ge(sem("exp_done"), GROUP * (n - 1))
                dve.tensor_scalar(k.negm[:, n % 2, :], k.m[:, n % 2, :], -1.0, None, ALU.mult).then_inc(sem("negm_ready"), 1)

            def copy_turned(n):
                dve.wait_ge(sem("tr_done"), n + 1)
                if n >= 2:
                    dve.wait_ge(sem("pv_done"), n - 1)
                dve.tensor_copy(k.pT[:, n % 2], ps[4 + n % 2][:].rearrange("p (h q) -> p h q", h=GROUP)).then_inc(sem("pT_ready"), 1)
                dve.wait_ge(sem("rest_done"), n + 1)
                dve.tensor_copy(k.prT[:, n % 2, :], ps[2 * (n % 2)][:, rest_cols]).then_inc(sem("prT_ready"), 1)

            def normalise(n):
                t, g = divmod(n, GROUPS)
                dve.wait_ge(sem("pv_done"), n + 1)
                ch.link(dve.reciprocal(k.rs[:, n % 2, :], k.sum[:, n % 4, :]))
                if g == 0 and t >= 2:
                    dve.wait_ge(sem("oT_done"), 2 * (t - 1))
                width = GROUP * XHD
                dve.tensor_tensor(k.o[:, t % 2, g * width:(g + 1) * width].rearrange("p (h d) -> p h d", h=GROUP),
                                  ps[6 + n % 2][:, 0:width].rearrange("p (h d) -> p h d", h=GROUP), over(k.rs[:, n % 2, :], 2, XHD), ALU.mult).then_inc(sem("o_ready"), 1)

            def add_output(t):
                x = x_of(net, b)[:, t, :]
                dve.wait_ge(sem("y_done"), t + 1)
                dve.tensor_tensor(x, x, ps[1][:, 0:P], ALU.add).then_inc(sem("x_added"), 1)

            maxima(0)
            for n in range(steps):
                if n + 1 < steps:
                    maxima(n + 1)
                copy_turned(n)
                if n >= 1:
                    normalise(n - 1)
                if n >= 6 and n % GROUPS == 2:
                    add_output((n - 6) // GROUPS)
            normalise(steps - 1)
            add_output(QT - 1)
            dve.wait_ge(sem("x_added"), QT)

        @block.gpsimd
        def _(pool):
            nc.gpsimd.tensor_copy(k.src[:, 0:KPAD], w("ctxT")[:, bass.ts(b, KPAD)]).then_inc(sem("src_ready"), 1)
            pool.wait_ge(sem("src_ready"), 1)
            nc.gpsimd.tensor_copy(k.src[:, KPAD:KPAD + P], w("restT")[:, bass.ts(b, P)]).then_inc(sem("src_ready"), 1)
            pool.wait_ge(sem("src_ready"), 2)
            for n in range(steps):
                pool.wait_ge(sem("exp_done"), GROUP * (n + 1))
                if n >= 2:
                    pool.wait_ge(sem("tr_done"), n - 1)
                nc.gpsimd.tensor_copy(k.pr[:, n % 2, :].rearrange("p (h k) -> p h k", h=GROUP), k.p[:, n % 2, :, KMAIN:KPAD]).then_inc(sem("pr_ready"), 1)

        @block.scalar
        def _(act):
            for c in range(pairs):
                act.wait_ge(sem("q_done"), c + 1)
                nc.scalar.activation(k.qT[:, c, :], ps[c % 2][:], ACT.Identity, scale=scale, bias=k.bq[:, c:c + 1]).then_inc(sem("qT_ready"), 1)

            def exponentials(n):
                act.wait_ge(sem("negm_ready"), n + 1)
                if n >= 2:
                    act.wait_ge(sem("tr_done"), n - 1)
                    act.wait_ge(sem("pr_ready"), n - 1)
                if n >= 4:
                    act.wait_ge(sem("o_ready"), n - 3)
                for j in range(GROUP):
                    nc.scalar.activation(k.p[:, n % 2, j, 0:S2], ps[2 * (n % 2) + j // 2][:, j % 2 * S2:(j % 2 + 1) * S2], ACT.Exp,
                                         bias=k.negm[:, n % 2, j:j + 1], accum_out=k.sum[:, n % 4, j:j + 1]).then_inc(sem("exp_done"), 1)

            def copy_outputs(t):
                for i in range(2):
                    act.wait_ge(sem("oT_done"), 2 * t + i + 1)
                    if t >= 1:
                        act.wait_ge(sem("y_done"), t)
                    nc.scalar.copy(k.oT[:, i], ps[4 + i][:].rearrange("p (c q) -> p c q", c=4)).then_inc(sem("oT_ready"), 1)

            exponentials(0)
            for n in range(steps):
                if n + 1 < steps:
                    exponentials(n + 1)
                if n >= 5 and n % GROUPS == 1:
                    copy_outputs((n - 5) // GROUPS)
            copy_outputs(QT - 1)

        @block.tensor
        def _(pe):
            ones = w("ones")[0:1, :]
            x = net.xnT_all[:, bass.ts(b, S)]
            pe.wait_ge(sem("src_ready"), 2)
            for half in range(2):
                cols = slice(512 * half, 512 * half + 512)
                if half:
                    pe.wait_ge(sem("v_ready"), 1 + GROUP)
                pe.matmul(ps[4][:], k.src[:, 0:P], w("x3_wv")[:, cols], start=True, stop=True)
                pe.matmul(ps[5][:], k.src[:, KPAD:KPAD + P], w("x3_wv")[:, cols], start=True, stop=True).then_inc(sem("v_done"), 1)
                for c in range(4 * half, 4 * half + 4):
                    if c >= 2:
                        pe.wait_ge(sem("qT_ready"), c - 1)
                    pe.matmul(ps[c % 2][:], w("x3_wq")[:, c * P:(c + 1) * P], x, start=True, stop=True).then_inc(sem("q_done"), 1)
                    if c >= 2:
                        pe.wait_ge(sem("kk_ready"), c - 1)
                    pe.matmul(ps[2 + c % 2][:, 0:KPAD], w("x3_wk")[:, c * P:(c + 1) * P], k.src[:, 0:KPAD], start=True, stop=True).then_inc(sem("k_done"), 1)
            pe.wait_ge(sem("mask_ready"), 1)
            pe.wait_ge(sem("qT_ready"), pairs)
            pe.wait_ge(sem("kk_ready"), pairs)
            pe.wait_ge(sem("v_ready"), 2 * (1 + GROUP))

            def scores(n):
                t, g = divmod(n, GROUPS)
                if n >= 2:
                    pe.wait_ge(sem("exp_done"), GROUP * (n - 1))
                    pe.wait_ge(sem("prT_ready"), n - 1)
                if n >= 8 and g == 0:
                    pe.wait_ge(sem("x_added"), t - 1)
                for i in range(2):
                    c = 2 * g + i
                    out = ps[2 * (n % 2) + i][:, 0:2 * S2].rearrange("p (h k) -> p h k", h=2)
                    pe.matmul(out, k.qT[:, c, t * P:(t + 1) * P], k.kk[:, 2 * c:2 * c + 2, 0:S2], start=True, stop=False)
                    pe.matmul(out, w("negi"), over(k.mq[:, t, 0:S2], 1, 2), start=False, stop=True).then_inc(sem("scores_done"), 1)

            def turn(n):
                t, g = divmod(n, GROUPS)
                pe.wait_ge(sem("exp_done"), GROUP * (n + 1))
                if n >= 6 and g >= 2:
                    pe.wait_ge(sem("oT_ready"), 2 * ((n - 6) // GROUPS) + n % 2 + 1)
                elif n >= 2:
                    pe.wait_ge(sem("pT_ready"), n - 1)
                for j in range(GROUP):
                    last = pe.transpose(ps[4 + n % 2][:, j * P:(j + 1) * P], k.p[:, n % 2, j, 0:KMAIN], w("ident"))
                last.then_inc(sem("tr_done"), 1)
                pe.wait_ge(sem("pr_ready"), n + 1)
                pe.transpose(ps[2 * (n % 2)][:, rest_cols], k.pr[:, n % 2, :], w("ident")).then_inc(sem("rest_done"), 1)

            def products(n):
                g = n % GROUPS
                pe.wait_ge(sem("prT_ready"), n + 1)
                pe.wait_ge(sem("pT_ready"), n + 1)
                if n >= 2:
                    pe.wait_ge(sem("o_ready"), n - 1)
                out = ps[6 + n % 2]
                heads = slice(GROUP * g, GROUP * (g + 1))
                pe.matmul(out[:, 0:GROUP * XHD], k.prT[:, n % 2, :], k.vr[:, heads, :].rearrange("p h d -> p (h d)"), start=True, stop=False, skip_group_check=True)
                for j in range(GROUP):
                    last = pe.matmul(out[:, j * XHD:(j + 1) * XHD], k.pT[:, n % 2, j, :], k.v[:, GROUP * g + j, :], start=False, stop=True, skip_group_check=True)
                last.then_inc(sem("pv_done"), 1)

            def turn_outputs(t):
                pe.wait_ge(sem("o_ready"), GROUPS * (t + 1))
                for i in range(2):
                    pe.wait_ge(sem("pT_ready"), min(steps - 1 + i, GROUPS * t + 5 + i))
                    for c in range(4):
                        at = (4 * i + c) * P
                        last = pe.transpose(ps[4 + i][:, c * P:(c + 1) * P], k.o[:, t % 2, at:at + P], w("ident"))
                    last.then_inc(sem("oT_done"), 1)

            def output(t):
                pe.wait_ge(sem("oT_ready"), 2 * t + 2)
                out = ps[1][:, 0:P]
                for c in range(pairs):
                    pe.matmul(out, k.oT[:, c // 4, c % 4, :], w("x3_wo")[:, c * P:(c + 1) * P], start=(c == 0), stop=False, skip_group_check=True)
                pe.matmul(out, ones, w("x3_bo")[0:1, :], start=False, stop=True, skip_group_check=True).then_inc(sem("y_done"), 1)

            scores(0)
            for n in range(steps):
                if n + 1 < steps:
                    scores(n + 1)
                turn(n)
                if n >= 1:
                    products(n - 1)
                if n >= 5 and n % GROUPS == 1:
                    turn_outputs((n - 5) // GROUPS)
                if n >= 6 and n % GROUPS == 2:
                    output((n - 6) // GROUPS)
            products(steps - 1)
            turn_outputs(QT - 1)
            output(QT - 1)
    end_of_block(net)



def router_block(net, k, weight, keep_x=False):
    nc, sem, ps, w = net.nc, net.sem, net.ps, net.w
    n = k.n
    with nc.Block() as block:

        @block.vector
        def _(dve):
            ch = Chain(dve, sem("dve_chain"))
            vector_layernorm(dve, ch, net.x, n.xn, n, sem("xn_ready"))
            if keep_x:
                dve.wait_ge(sem("xn_ready"), B)
                ch.link(dve.tensor_tensor(net.x[:], net.x[:], n.xn[:], ALU.add))
            if weight is not None:
                for b in range(B):
                    dve.wait_ge(sem("logits_done"), b + 1)
                    ch.link(dve.tensor_copy(net.logits[:, :, b, :], ps[b][:, 0:QT * E8].rearrange("p (t e) -> p t e", t=QT)))

        @block.scalar
        def _(act):
            for b in range(B):
                act.wait_ge(sem("xT_done"), b + 1)
                nc.scalar.copy(net.xnT_all[:, b * S:(b + 1) * S], ps[6 + b % 2][:]).then_inc(sem("xnT_ready"), 1)

        @block.tensor
        def _(pe):
            def scores(b):
                pe.wait_ge(sem("xnT_ready"), b + 1)
                for t in range(QT):
                    at = b * S + t * P
                    last = pe.matmul(ps[b][:, t * E8:(t + 1) * E8], net.xnT_all[:, at:at + P], w(weight), start=True, stop=True)
                last.then_inc(sem("logits_done"), 1)

            for b in range(B):
                pe.wait_ge(sem("xn_ready"), b + 1)
                if b >= 2:
                    pe.wait_ge(sem("xnT_ready"), b - 1)
                tensor_transpose_tiles(pe, ps[6 + b % 2], n.xn[:, b * QT:(b + 1) * QT, :], w("ident")).then_inc(sem("xT_done"), 1)
                if weight is not None and b >= 1:
                    scores(b - 1)
            if weight is not None:
                scores(B - 1)
    end_of_block(net)


class Router:

    def __init__(self, net, sb):
        n = QT * B
        self.g = sb("g", [P, n, E8])
        self.t = sb("t", [P, n, E8])
        self.sel = [sb(f"sel{i}", [P, n, E8]) for i in range(2)]
        self.top = sb("top", [P, n, 2])
        self.rm = sb("rm", [P, n])
        self.sum = sb("sum", [P, n])
        self.pair = sb("pair", [P, 2, n, E8])
        self.tot = sb("tot", [P, 2, E8])
        self.one = sb("one", [P, E8])
        self.temp = sb("temp", [P, 1])
        self.u = sb("u", [32, S])
        self.ue = sb("ue", [32, S])
        self.um = sb("um", [32, 1])
        self.us = sb("us", [32, 1])
        self.ul = sb("ul", [32, 1])


def vector_top2(dve, ch, k, rank):
    n = QT * B
    src = k.g
    for i in range(2):
        ch.link(dve.reduce_max(k.top[:, :, i], src[:], AX))
        ch.link(dve.tensor_tensor(k.sel[i][:], src[:], over(k.top[:, :, i], 2, E8), ALU.is_equal))
        ch.link(dve.tensor_tensor(k.sel[i][:], k.sel[i][:], over(rank, 1, n), ALU.mult))
        ch.link(dve.reduce_max(k.rm[:], k.sel[i][:], AX))
        last = dve.tensor_tensor(k.sel[i][:], k.sel[i][:], over(k.rm[:], 2, E8), ALU.is_equal)
        if i == 0:
            ch.link(last)
            ch.link(dve.scalar_tensor_tensor(k.t[:], k.sel[0][:], NEG, k.g[:], ALU.mult, ALU.add))
            src = k.t
    return last


def flat(t):
    return t[:].rearrange("p t b e -> p (t b) e")


def route_mean(net, k):
    nc, sem, ps, w = net.nc, net.sem, net.ps, net.w
    n = QT * B
    with nc.Block() as block:

        @block.vector
        def _(dve):
            ch = Chain(dve, sem("dve_chain"))
            lg = flat(net.logits)
            ch.link(dve.reduce_max(k.rm[:], lg, AX))
            dve.tensor_tensor(k.g[:], lg, over(k.rm[:], 2, E8), ALU.subtract).then_inc(sem("centred"), 1)
            dve.wait_ge(sem("exp_done"), 1)
            ch.link(dve.reduce_sum(k.sum[:], k.t[:], AX))
            ch.link(dve.reciprocal(k.sum[:], k.sum[:]))
            ch.link(dve.tensor_tensor(k.g[:], k.t[:], over(k.sum[:], 2, E8), ALU.mult))
            ch.link(vector_top2(dve, ch, k, w("rank")))
            ch.link(dve.tensor_tensor(k.sum[:], k.top[:, :, 0], k.top[:, :, 1], ALU.add))
            ch.link(dve.reciprocal(k.sum[:], k.sum[:]))
            ch.link(dve.tensor_tensor(k.pair[:, 1], k.sel[0][:], k.sel[1][:], ALU.add))
            ch.link(dve.tensor_tensor(k.t[:], k.g[:], k.pair[:, 1], ALU.mult))
            dve.tensor_tensor(k.pair[:, 0], k.t[:], over(k.sum[:], 2, E8), ALU.mult).then_inc(sem("pair_ready"), 1)
            dve.wait_ge(sem("sums_done"), 1)
            ch.link(dve.reduce_sum(k.tot[:], ps[0][:, 0:2 * n * E8].rearrange("p (a n e) -> p a e n", a=2, n=n), AX))
            ch.link(dve.tensor_scalar(k.one[:], k.tot[:, 1], 1.0, None, ALU.max))
            ch.link(dve.reciprocal(k.one[:], k.one[:]))
            ch.link(dve.tensor_tensor(k.one[:], k.one[:], k.tot[:, 0], ALU.mult))
            ch.link(dve.tensor_tensor(flat(net.coef), k.pair[:, 1], over(k.one[:], 1, n), ALU.mult))

        @block.scalar
        def _(act):
            act.wait_ge(sem("centred"), 1)
            nc.scalar.activation(k.t[:], k.g[:], ACT.Exp).then_inc(sem("exp_done"), 1)

        @block.tensor
        def _(pe):
            pe.wait_ge(sem("pair_ready"), 1)
            pe.matmul(ps[0][:, 0:2 * n * E8], w("ones"), k.pair[:].rearrange("p a n e -> p (a n e)"), start=True, stop=True).then_inc(sem("sums_done"), 1)
    end_of_block(net)


SINKHORN = 3


def route_sinkhorn(net, k):
    nc, sem, ps, w = net.nc, net.sem, net.ps, net.w
    n = QT * B
    tok = k.g[:].rearrange("p (t b) e -> p t (b e)", t=QT)
    with nc.Block() as block:

        @block.vector
        def _(dve):
            ch = Chain(dve, sem("dve_chain"))
            lg = flat(net.logits)
            ch.link(dve.tensor_scalar(k.temp[:], w("f2_temp"), 0.1, None, ALU.max))
            ch.link(dve.reciprocal(k.temp[:], k.temp[:]))
            ch.link(dve.tensor_tensor(k.g[:], lg, over(w("f2_router_b"), 1, n), ALU.add))
            ch.link(dve.tensor_scalar(k.g[:], k.g[:], k.temp[:], None, ALU.mult))
            for i in range(SINKHORN):
                ch.link(dve.reduce_max(k.rm[:], k.g[:], AX))
                dve.tensor_tensor(k.g[:], k.g[:], over(k.rm[:], 2, E8), ALU.subtract).then_inc(sem("row_centred"), 1)
                dve.wait_ge(sem("row_exp"), i + 1)
                dve.reduce_sum(k.sum[:], k.t[:], AX).then_inc(sem("row_sum"), 1)
                dve.wait_ge(sem("row_log"), i + 1)
                dve.tensor_tensor(k.g[:], k.g[:], over(k.rm[:], 2, E8), ALU.subtract).then_inc(sem("row_ready"), 1)
                dve.wait_ge(sem("turned"), i + 1)
                ch.link(dve.reduce_max(k.um[:], ps[0][0:32, :], AX))
                dve.tensor_scalar(k.u[:], ps[0][0:32, :], k.um[:], None, ALU.subtract).then_inc(sem("col_centred"), 1)
                dve.wait_ge(sem("col_log"), i + 1)
                dve.tensor_scalar(k.u[:], k.u[:], k.ul[:], None, ALU.subtract).then_inc(sem("col_ready"), 1)
                dve.wait_ge(sem("turned_back"), i + 1)
                dve.tensor_copy(tok, ps[1][:, 0:QT * 32].rearrange("p (t c) -> p t c", t=QT)).then_inc(sem("log_gates"), 1)
                dve.wait_ge(sem("log_gates"), i + 1)
            dve.wait_ge(sem("gates_exp"), 1)
            ch.link(dve.reduce_sum(k.sum[:], k.t[:], AX))
            ch.link(dve.tensor_scalar(k.sum[:], k.sum[:], 1e-8, None, ALU.add))
            ch.link(dve.reciprocal(k.sum[:], k.sum[:]))
            ch.link(dve.tensor_tensor(k.g[:], k.t[:], over(k.sum[:], 2, E8), ALU.mult))
            ch.link(vector_top2(dve, ch, k, w("rank")))
            ch.link(dve.tensor_tensor(k.sum[:], k.top[:, :, 0], k.top[:, :, 1], ALU.add))
            ch.link(dve.tensor_scalar(k.sum[:], k.sum[:], 1e-8, None, ALU.add))
            ch.link(dve.reciprocal(k.sum[:], k.sum[:]))
            ch.link(dve.tensor_tensor(k.t[:], k.sel[0][:], k.sel[1][:], ALU.add))
            ch.link(dve.tensor_tensor(k.t[:], k.g[:], k.t[:], ALU.mult))
            ch.link(dve.tensor_tensor(flat(net.coef), k.t[:], over(k.sum[:], 2, E8), ALU.mult))

        @block.scalar
        def _(act):
            for i in range(SINKHORN):
                act.wait_ge(sem("row_centred"), i + 1)
                nc.scalar.activation(k.t[:], k.g[:], ACT.Exp).then_inc(sem("row_exp"), 1)
                act.wait_ge(sem("row_sum"), i + 1)
                nc.scalar.activation(k.rm[:], k.sum[:], ACT.Ln).then_inc(sem("row_log"), 1)
                act.wait_ge(sem("col_centred"), i + 1)
                nc.scalar.activation(k.ue[:], k.u[:], ACT.Exp, accum_out=k.us[:]).then_inc(sem("col_exp"), 1)
                act.wait_ge(sem("col_exp"), i + 1)
                nc.scalar.activation(k.ul[:], k.us[:], ACT.Ln).then_inc(sem("col_log"), 1)
            act.wait_ge(sem("log_gates"), SINKHORN)
            nc.scalar.activation(k.t[:], k.g[:], ACT.Exp).then_inc(sem("gates_exp"), 1)

        @block.tensor
        def _(pe):
            for i in range(SINKHORN):
                pe.wait_ge(sem("row_ready"), i + 1)
                for t in range(QT):
                    last = pe.transpose(ps[0][0:32, t * P:(t + 1) * P], tok[:, t, :], w("ident"))
                last.then_inc(sem("turned"), 1)
                pe.wait_ge(sem("col_ready"), i + 1)
                for t in range(QT):
                    last = pe.transpose(ps[1][:, t * 32:(t + 1) * 32], k.u[:, t * P:(t + 1) * P], w("ident")[0:32, 0:32])
                last.then_inc(sem("turned_back"), 1)
    end_of_block(net)


def route_tokens(net, k):
    nc, sem, ps, w = net.nc, net.sem, net.ps, net.w
    n = QT * B
    top = k.top[:].rearrange("p (t b) c -> p t (b c)", t=QT)
    nb = 2 * B
    with nc.Block() as block:

        @block.vector
        def _(dve):
            ch = Chain(dve, sem("dve_chain"))
            ch.link(dve.tensor_copy(k.g[:], flat(net.logits)))
            vector_top2(dve, ch, k, w("rank")).then_inc(sem("top_ready"), 1)
            dve.wait_ge(sem("top_ready"), 1)
            dve.wait_ge(sem("turned"), 1)
            ch.link(dve.reduce_max(k.um[0:nb], ps[0][0:nb, :], AX))
            dve.tensor_scalar(k.u[0:nb, :], ps[0][0:nb, :], k.um[0:nb], None, ALU.subtract).then_inc(sem("centred"), 1)
            dve.wait_ge(sem("exp_done"), 1)
            ch.link(dve.reciprocal(k.us[0:nb], k.us[0:nb]))
            dve.tensor_scalar(k.u[0:nb, :], k.ue[0:nb, :], k.us[0:nb], None, ALU.mult).then_inc(sem("weights_ready"), 1)
            dve.wait_ge(sem("turned_back"), 1)
            ch.link(dve.tensor_copy(top, ps[1][:, 0:QT * nb].rearrange("p (t c) -> p t c", t=QT)))
            ch.link(dve.tensor_tensor(k.g[:], k.sel[0][:], over(k.top[:, :, 0], 2, E8), ALU.mult))
            ch.link(dve.tensor_tensor(k.t[:], k.sel[1][:], over(k.top[:, :, 1], 2, E8), ALU.mult))
            ch.link(dve.tensor_tensor(flat(net.coef), k.g[:], k.t[:], ALU.add))

        @block.scalar
        def _(act):
            act.wait_ge(sem("centred"), 1)
            nc.scalar.activation(k.ue[0:nb, :], k.u[0:nb, :], ACT.Exp, accum_out=k.us[0:nb]).then_inc(sem("exp_done"), 1)

        @block.tensor
        def _(pe):
            pe.wait_ge(sem("top_ready"), 1)
            for t in range(QT):
                last = pe.transpose(ps[0][0:nb, t * P:(t + 1) * P], top[:, t, :], w("ident"))
            last.then_inc(sem("turned"), 1)
            pe.wait_ge(sem("weights_ready"), 1)
            for t in range(QT):
                last = pe.transpose(ps[1][:, t * nb:(t + 1) * nb], k.u[0:nb, t * P:(t + 1) * P], w("ident")[0:nb, 0:nb])
            last.then_inc(sem("turned_back"), 1)
    end_of_block(net)


RING = 3


class Experts:

    def __init__(self, net, sb):
        self.t = sb("et", [P, 2, S])
        self.a = sb("ea", [P, 2, S])
        self.h = sb("eh", [P, RING, S])



def experts_block(net, b, k, act_kind, names, experts, tiles):
    nc, sem, ps, w = net.nc, net.sem, net.ps, net.w
    gate, up, down = names
    work = [(e, i) for e in range(experts) for i in range(tiles)]
    weighed = experts > 1
    with nc.Block() as block:

        @block.vector
        def _(dve):
            ch = Chain(dve, sem("dve_chain"))
            x = x_of(net, b)

            def add_expert(e):
                if act_kind == "bias":
                    dve.wait_ge(sem("out_done"), e + 1)
                else:
                    dve.wait_ge(sem("h_used"), tiles * (e + 1))
                if e >= 1:
                    dve.wait_ge(sem("x_added"), e)
                y = ps[6 + e % 2][:].rearrange("p (t d) -> p t d", t=QT)
                if weighed:
                    for t in range(QT):
                        last = dve.scalar_tensor_tensor(x[:, t, :], y[:, t, :], net.coef[:, t, b, e:e + 1], x[:, t, :], ALU.mult, ALU.add)
                else:
                    last = dve.tensor_tensor(x, x, y, ALU.add)
                last.then_inc(sem("x_added"), 1)

            for n, (e, i) in enumerate(work):
                if act_kind != "bias":
                    g, u = ps[n % RING], ps[3 + n % RING]
                    dve.wait_ge(sem("act_done"), n + 1)
                    if n >= RING:
                        dve.wait_ge(sem("h_used"), n - RING + 1)
                    dve.wait_ge(sem("up_done"), n + 1)
                    if act_kind == "silu":
                        ch.link(dve.scalar_tensor_tensor(k.a[:, n % 2], k.t[:, n % 2], 1.0, g[:], ALU.add, ALU.mult))
                        dve.scalar_tensor_tensor(k.h[:, n % RING], u[:], 0.5, k.a[:, n % 2], ALU.mult, ALU.mult).then_inc(sem("h_ready"), 1)
                    else:
                        dve.tensor_tensor(k.h[:, n % RING], u[:], k.t[:, n % 2], ALU.mult).then_inc(sem("h_ready"), 1)
                if i == 1 and e >= 1:
                    add_expert(e - 1)
            add_expert(experts - 1)
            dve.wait_ge(sem("x_added"), experts)

        @block.scalar
        def _(act):
            for n, (e, i) in enumerate(work):
                act.wait_ge(sem("gate_done"), n + 1)
                if act_kind == "bias":
                    if n >= RING:
                        act.wait_ge(sem("h_used"), n - RING + 1)
                    nc.scalar.activation(k.h[:, n % RING], ps[n % RING][:], ACT.Relu, bias=w(f"b{e}")[:, i:i + 1]).then_inc(sem("h_ready"), 1)
                    continue
                if n >= 2:
                    act.wait_ge(sem("h_ready"), n - 1)
                if act_kind == "silu":
                    nc.scalar.activation(k.t[:, n % 2], ps[n % RING][:], ACT.Tanh, scale=0.5).then_inc(sem("act_done"), 1)
                else:
                    nc.scalar.activation(k.t[:, n % 2], ps[n % RING][:], ACT.Relu).then_inc(sem("act_done"), 1)

        @block.tensor
        def _(pe):
            x = net.xnT_all[:, bass.ts(b, S)]

            def hidden(n):
                e, i = work[n]
                if n >= RING:
                    pe.wait_ge(sem("h_ready"), n - RING + 1)
                cols = slice(i * P, (i + 1) * P)
                pe.matmul(ps[n % RING][:], w(gate.format(e))[:, cols], x, start=True, stop=True).then_inc(sem("gate_done"), 1)
                if up:
                    pe.matmul(ps[3 + n % RING][:], w(up.format(e))[:, cols], x, start=True, stop=True).then_inc(sem("up_done"), 1)

            def output(n):
                e, i = work[n]
                pe.wait_ge(sem("h_ready"), n + 1)
                if i == 0 and e >= 2:
                    pe.wait_ge(sem("x_added"), e - 1)
                bank = ps[6 + e % 2]
                for t in range(QT):
                    last = pe.matmul(bank[:, t * P:(t + 1) * P], k.h[:, n % RING, t * P:(t + 1) * P], w(down.format(e))[:, i * P:(i + 1) * P],
                                     start=(i == 0 and t == 0), stop=(i == tiles - 1), skip_group_check=True)
                last.then_inc(sem("h_used"), 1)
                if i == tiles - 1 and act_kind == "bias":
                    for t in range(QT):
                        last = pe.matmul(bank[:, t * P:(t + 1) * P], w("ones")[0:1, :], w("b2")[0:1, e * P:(e + 1) * P],
                                         start=False, stop=True, skip_group_check=True)
                    last.then_inc(sem("out_done"), 1)

            for n in range(len(work) + 2):
                if n < len(work):
                    hidden(n)
                if n >= 2:
                    output(n - 2)
    end_of_block(net)



NSTATE, NCONV = 16, 4


class Scan:

    def __init__(self, net, sb):
        self.n = Norm(net, sb)
        self.xp = sb("xp", [P, 2, NCONV - 1 + S])
        self.c = sb("c", [P, 2, S])
        self.z = sb("z", [P, 2, S])
        self.t = sb("st", [P, 2, S])
        self.xc = sb("xc", [P, 2, S])
        self.zs = sb("zs", [P, 2, S])
        self.A = sb("A", [P, 2 * NSTATE])
        self.bf = sb("bf", [32, S])
        self.bh = sb("bh", [32, S], BF16)
        self.bc = sb("bc", [P, S], BF16)
        self.raw = sb("raw", [P, S])
        self.e = sb("e", [P, S])
        self.ln = sb("ln", [P, S])
        self.d = sb("d", [P, S])
        self.iz = sb("iz", [P, S])
        self.dt = sb("dt", [P, S])
        self.dtx = sb("dtx", [P, 2, S])
        self.dA = sb("dA", [P, 2, 2, S])
        self.cb = sb("cb", [P, 2, S])
        self.dbx = sb("dbx", [P, 2, 2, S])
        self.h = sb("sh", [P, 2, 2, S])
        self.hc = sb("hc", [P, 2, 2, S])
        self.r = sb("sr", [P, QT, P])
        self.rn = sb("rn", [P, QT, P])


def scan_prepare(net, k):
    nc, sem, w = net.nc, net.sem, net.w
    with nc.Block() as block:

        @block.scalar
        def _(act):
            nc.scalar.activation(k.A[:], w("m_alog"), ACT.Exp).then_inc(sem("A_exp"), 1)

        @block.vector
        def _(dve):
            ch = Chain(dve, sem("dve_chain"))
            dve.memset(k.xp[:, :, 0:NCONV - 1], 0.0)
            ch.link(dve.memset(k.bc[:], 0.0))
            dve.wait_ge(sem("A_exp"), 1)
            ch.link(dve.tensor_scalar(k.A[:], k.A[:], -1.0, None, ALU.mult))
    end_of_block(net)



def scan_block(net, b, k):
    nc, sem, ps, w = net.nc, net.sem, net.ps, net.w
    with nc.Block() as block:

        @block.vector
        def _(dve):
            ch = Chain(dve, sem("dve_chain"))
            vector_layernorm(dve, ch, x_of(net, b), k.n.xn, k.n).then_inc(sem("xn_ready"), 1)
            for i in range(2):
                dve.wait_ge(sem("xm_ready"), i + 1)
                ch.link(dve.tensor_scalar(k.c[:, i], k.xp[:, i, 0:S], w("m_conv")[:, 4 * i:4 * i + 1], w("m_conv_b")[:, i:i + 1], ALU.mult, ALU.add))
                for j in range(1, NCONV):
                    last = dve.scalar_tensor_tensor(k.c[:, i], k.xp[:, i, j:j + S], w("m_conv")[:, 4 * i + j:4 * i + j + 1], k.c[:, i], ALU.mult, ALU.add)
                    if j < NCONV - 1:
                        ch.link(last)
                last.then_inc(sem("conv_ready"), 1)
            dve.wait_ge(sem("tanh_c"), 1)
            ch.link(dve.scalar_tensor_tensor(k.t[:], k.t[:], 1.0, k.c[:], ALU.add, ALU.mult))
            dve.tensor_scalar(k.xc[:], k.t[:], 0.5, None, ALU.mult).then_inc(sem("xc_ready"), 1)
            dve.wait_ge(sem("tanh_z"), 1)
            ch.link(dve.scalar_tensor_tensor(k.zs[:], k.zs[:], 1.0, k.z[:], ALU.add, ALU.mult))
            dve.wait_ge(sem("dt_done"), 1)
            ch.link(dve.tensor_scalar(k.raw[:], ps[5][:], w("m_dt_b"), None, ALU.add))
            dve.scalar_tensor_tensor(k.e[:], k.raw[:], -1.0, k.raw[:], ALU.mult, ALU.max).then_inc(sem("abs_ready"), 1)
            dve.wait_ge(sem("bc_done"), 1)
            ch.link(dve.tensor_scalar(k.bf[:], ps[4][0:32, :], w("m_xp_b")[0:32, :], None, ALU.add))
            ch.link(dve.tensor_copy(k.bh[:], k.bf[:]))
            dve.tensor_copy(k.bc[0:32, :], k.bh[:])
            ch.link(dve.tensor_tensor(k.bf[:], k.bf[:], k.bh[:], ALU.subtract))
            ch.link(dve.tensor_copy(k.bh[:], k.bf[:]))
            dve.tensor_copy(k.bc[32:64, :], k.bh[:])
            ch.link(dve.tensor_tensor(k.bf[:], k.bf[:], k.bh[:], ALU.subtract))
            dve.tensor_copy(k.bc[64:96, :], k.bf[:]).then_inc(sem("bc_ready"), 1)
            dve.wait_ge(sem("log_ready"), 1)
            ch.link(dve.tensor_scalar(k.iz[:], k.d[:], -1.0, 0.0, ALU.add, ALU.is_equal))
            ch.link(dve.scalar_tensor_tensor(k.d[:], k.d[:], -1.0, k.iz[:], ALU.add, ALU.add))
            ch.link(dve.reciprocal(k.d[:], k.d[:]))
            dve.tensor_tensor(k.ln[:], k.ln[:], k.iz[:], ALU.add)
            ch.link(dve.tensor_tensor(k.d[:], k.d[:], k.e[:], ALU.mult))
            ch.link(dve.tensor_tensor(k.d[:], k.d[:], k.ln[:], ALU.mult))
            dve.scalar_tensor_tensor(k.dt[:], k.raw[:], 0.0, k.d[:], ALU.max, ALU.add).then_inc(sem("dt_ready"), 1)
            dve.wait_ge(sem("dt_ready"), 1)
            ch.link(dve.tensor_tensor(k.dtx[:], k.xc[:], over(k.dt[:], 1, 2), ALU.mult))
            for s in range(NSTATE):
                dve.wait_ge(sem("B_done"), s + 1)
                dve.tensor_tensor(k.dbx[:, s % 2], k.dtx[:], over(ps[s % 2][:], 1, 2), ALU.mult).then_inc(sem("dbx_ready"), 1)
                dve.wait_ge(sem("dbx_ready"), s + 1)
                for i in range(2):
                    dve.wait_ge(sem("dA_ready"), 2 * s + i + 1)
                    if s >= 2 and i == 0:
                        dve.wait_ge(sem("hc_ready"), s - 1)
                    dve.tensor_tensor_scan(k.h[:, s % 2, i], k.dA[:, s % 2, i], k.dbx[:, s % 2, i], 0.0, ALU.mult, ALU.add).then_inc(sem("h_ready"), 1)
            dve.wait_ge(sem("y_done"), 1)
            for i in range(2):
                ch.link(dve.scalar_tensor_tensor(k.c[:, i], k.xc[:, i], w("m_d")[:, i:i + 1], ps[4 + i][:], ALU.mult, ALU.add))
            dve.scalar_tensor_tensor(k.c[:], k.c[:], 0.5, k.zs[:], ALU.mult, ALU.mult).then_inc(sem("gated_ready"), 1)
            dve.wait_ge(sem("out_done"), 1)
            ch.link(dve.tensor_tensor(k.r[:], ps[6][:].rearrange("p (t d) -> p t d", t=QT), k.n.xn[:], ALU.add))
            ch.link(vector_layernorm(dve, ch, k.r, k.rn, k.n))
            ch.link(dve.tensor_tensor(k.rn[:], k.rn[:], over(w("m_gamma"), 1, QT), ALU.mult))
            ch.link(dve.tensor_tensor(k.rn[:], k.rn[:], over(w("m_beta"), 1, QT), ALU.add))
            ch.link(dve.tensor_tensor(x_of(net, b), x_of(net, b), k.rn[:], ALU.add))

        @block.gpsimd
        def _(pool):
            for s in range(NSTATE):
                pool.wait_ge(sem("C_ready"), s + 1)
                pool.wait_ge(sem("h_ready"), 2 * s + 2)
                if s >= 2:
                    pool.wait_ge(sem("hc_used"), s - 1)
                nc.gpsimd.tensor_tensor(k.hc[:, s % 2], k.h[:, s % 2], over(k.cb[:, s % 2], 1, 2), ALU.mult).then_inc(sem("hc_ready"), 1)

        @block.scalar
        def _(act):
            act.wait_ge(sem("xT_done"), 1)
            nc.scalar.copy(k.n.xnT[:], ps[7][:]).then_inc(sem("xnT_ready"), 1)
            for i in range(2):
                act.wait_ge(sem("in_done"), i + 1)
                nc.scalar.activation(k.xp[:, i, NCONV - 1:NCONV - 1 + S], ps[i][:], ACT.Identity, bias=w("m_in_b")[:, i:i + 1]).then_inc(sem("xm_ready"), 1)
            for i in range(2):
                act.wait_ge(sem("in_done"), i + 3)
                nc.scalar.activation(k.z[:, i], ps[2 + i][:], ACT.Identity, bias=w("m_in_b")[:, 2 + i:3 + i]).then_inc(sem("z_ready"), 1)
            act.wait_ge(sem("z_ready"), 2)
            nc.scalar.activation(k.zs[:], k.z[:], ACT.Tanh, scale=0.5).then_inc(sem("tanh_z"), 1)
            act.wait_ge(sem("conv_ready"), 2)
            nc.scalar.activation(k.t[:], k.c[:], ACT.Tanh, scale=0.5).then_inc(sem("tanh_c"), 1)
            act.wait_ge(sem("abs_ready"), 1)
            nc.scalar.activation(k.e[:], k.e[:], ACT.Exp, scale=-1.0).then_inc(sem("e_ready"), 1)
            act.wait_ge(sem("e_ready"), 1)
            nc.scalar.activation(k.d[:], k.e[:], ACT.Identity, bias=1.0).then_inc(sem("e1_ready"), 1)
            act.wait_ge(sem("e1_ready"), 1)
            nc.scalar.activation(k.ln[:], k.d[:], ACT.Ln).then_inc(sem("log_ready"), 1)
            act.wait_ge(sem("dt_ready"), 1)
            for s in range(NSTATE):
                for i in range(2):
                    if s >= 2:
                        act.wait_ge(sem("h_ready"), 2 * (s - 2) + i + 1)
                    nc.scalar.activation(k.dA[:, s % 2, i], k.dt[:], ACT.Exp, scale=k.A[:, i * NSTATE + s:i * NSTATE + s + 1]).then_inc(sem("dA_ready"), 1)
                act.wait_ge(sem("C_done"), s + 1)
                if s >= 2:
                    act.wait_ge(sem("hc_ready"), s - 1)
                nc.scalar.copy(k.cb[:, s % 2], ps[2 + s % 2][:]).then_inc(sem("C_ready"), 1)

        @block.tensor
        def _(pe):
            pe.wait_ge(sem("xn_ready"), 1)
            tensor_transpose_tiles(pe, ps[7], k.n.xn, w("ident")).then_inc(sem("xT_done"), 1)
            pe.wait_ge(sem("xnT_ready"), 1)
            for i in range(4):
                pe.matmul(ps[i][:], w("m_in")[:, i * P:(i + 1) * P], k.n.xnT[:], start=True, stop=True).then_inc(sem("in_done"), 1)
            pe.wait_ge(sem("xc_ready"), 1)
            for i in range(2):
                last = pe.matmul(ps[5][:], w("m_dt")[:, i * P:(i + 1) * P], k.xc[:, i], start=(i == 0), stop=(i == 1))
            last.then_inc(sem("dt_done"), 1)
            for i in range(2):
                last = pe.matmul(ps[4][0:32, :], w("m_xp")[:, i * 32:(i + 1) * 32], k.xc[:, i], start=(i == 0), stop=(i == 1))
            last.then_inc(sem("bc_done"), 1)
            pe.wait_ge(sem("bc_ready"), 1)
            pe.wait_ge(sem("z_ready"), 2)

            def spread(s):
                if s >= 2:
                    pe.wait_ge(sem("dbx_ready"), s - 1)
                pe.matmul(ps[s % 2][:], w("sel")[:, s * P:(s + 1) * P], k.bc[:], start=True, stop=True).then_inc(sem("B_done"), 1)
                if s >= 2:
                    pe.wait_ge(sem("C_ready"), s - 1)
                pe.matmul(ps[2 + s % 2][:], w("sel")[:, (NSTATE + s) * P:(NSTATE + s + 1) * P], k.bc[:], start=True, stop=True).then_inc(sem("C_done"), 1)

            spread(0)
            spread(1)
            pe.wait_ge(sem("dt_ready"), 1)
            for s in range(NSTATE):
                if s + 2 < NSTATE:
                    spread(s + 2)
                pe.wait_ge(sem("hc_ready"), s + 1)
                for i in range(2):
                    last = pe.matmul(ps[4 + i][:], w("ident"), k.hc[:, s % 2, i], start=(s == 0), stop=(s == NSTATE - 1))
                if s == NSTATE - 1:
                    last.then_inc(sem("y_done"), 1)
                else:
                    last.then_inc(sem("hc_used"), 1)
            pe.wait_ge(sem("gated_ready"), 1)
            for t in range(QT):
                for i in range(2):
                    pe.matmul(ps[6][:, t * P:(t + 1) * P], k.c[:, i, t * P:(t + 1) * P], w("m_out")[:, i * P:(i + 1) * P], start=(i == 0), stop=False)
                last = pe.matmul(ps[6][:, t * P:(t + 1) * P], w("ones")[0:1, :], w("m_out_b")[0:1, :], start=False, stop=True)
            last.then_inc(sem("out_done"), 1)
    end_of_block(net)



def program(nc, x_dram, packs, out_dram, upto=12, after=0):
    with ExitStack() as ctx:
        net = Net(nc, ctx)
        loads = {}
        loaded = {name: nc.alloc_semaphore(f"loaded_{name}") for name in packs if name != "x"}
        x_loaded = nc.alloc_semaphore("x_loaded")
        stored = nc.alloc_semaphore("stored")

        def place(stack, name, table, dt=F32):
            offs, n = offsets(table)
            t = stack.enter_context(nc.sbuf_tensor(f"w_{name}", [P, n], dt))
            for key, at in offs.items():
                net.weights[key] = (t, at)
            loads[name] = (t, packs[name], loaded[name])

        for name, table, dt in (("start", START, F32), ("constf", CONSTF, F32), ("constb", CONSTB, BF16), ("attn", ATTN, F32), ("ints", INTS, I32)):
            place(ctx, name, table, dt)
        offs, n = offsets(PLACE)
        placers = net.sb("placers", [P, n], F32R)
        for key, at in offs.items():
            net.weights[key] = (placers, at)
        xv = x_dram.rearrange("b (t p) d -> p (b t) d", p=P)
        ov = out_dram.rearrange("b (t p) d -> p (b t) d", p=P)

        ffn1_room, ffn0_room, first_room = ExitStack(), ExitStack(), ExitStack()
        place(ffn1_room, "ffn1", FFN1, I32)
        place(ffn0_room, "ffn0", FFN0)
        ffn1 = loads["ffn1"][0]
        l1w = ffn1[:, :].bitcast(F32)
        for key in FFN1:
            net.weights[key] = (l1w, net.weights[key][1])
        place(first_room, "tril", TRIL, BF16)
        place_f = first_room.enter_context(nc.sbuf_tensor("place_f", [P, n], F32))

        def load(queue, name):
            t, src, s = loads[name]
            queue.dma_start(t[:, :], src).then_inc(s, 16)

        with nc.Block() as block:

            @block.sync
            def _(sp):
                sp.dma_start(net.x[:], xv).then_inc(x_loaded, 16)
                for name in ("tril", "constf", "attn"):
                    load(sp, name)

            @block.scalar
            def _(act):
                load(act, "start")
                act.dma_start(place_f[:, :], packs["place"]).then_inc(loaded["place"], 16)
                for name in ("constb", "ints", "ffn1", "ffn0"):
                    load(act, name)

            @block.vector
            def _(dve):
                dve.wait_ge(x_loaded, 16)
                dve.wait_ge(loads["start"][2], 16)
                dve.wait_ge(loads["tril"][2], 16)

        def scope():
            stack = ExitStack()

            def sb(name, shape, dt=F32):
                net.names += 1
                return stack.enter_context(nc.sbuf_tensor(f"{name}_{net.names}", shape, dt))
            return stack, sb

        def wait_loaded(name):
            with nc.Block() as block:

                @block.vector
                def _(dve):
                    dve.wait_ge(loads[name][2], 16)

        def narrow_attention(pre, kind, ctx_keys):
            stack, sb = scope()
            with stack:
                k = Narrow(net, sb, kind, ctx_keys)
                inner, inner_sb = scope()
                with inner:
                    narrow_project(net, k, pre, 1.0 / float(np.sqrt(np.float32(HD))), inner_sb)
                k.more_buffers(net, sb)
                narrow_prepare(net, k)
                with nc.Fori(0, B // BODY, 1) as i:
                    narrow_block(net, i * BODY, k, pre)

        class One:
            pass

        def experts(weight, route, act_kind, names, n, tiles, keep_x=False):
            stack, sb = scope()
            with stack:
                k = One()
                k.n = Norm(net, sb, B * QT)
                r = Router(net, sb) if route else None
                e = Experts(net, sb)
                router_block(net, k, weight, keep_x)
                if route:
                    route(net, r)
                with nc.Fori(0, B, 1) as b:
                    experts_block(net, b, e, act_kind, names, n, tiles)

        done = 0

        def more():
            nonlocal done
            done += 1
            return after < done <= upto

        if more():
            stack, sb = scope()
            with stack:
                k = One()
                k.n = Norm(net, sb)
                k.qT, k.kT = sb("qT", [P, S]), sb("kT", [P, S])
                k.s, k.p = sb("s", [P, QT, S]), sb("p", [P, QT, S])
                k.mx, k.negm, k.sum, k.rs = sb("mx", [P, QT]), sb("negm", [P, QT]), sb("sum", [P, QT]), sb("rs", [P, QT])
                with nc.Fori(0, B, 1) as b:
                    single_head_block(net, b, k)
        with nc.Block() as block:

            @block.vector
            def _(dve):
                for name in ("constf", "attn", "constb", "ints"):
                    dve.wait_ge(loads[name][2], 16)
                dve.wait_ge(loaded["place"], 16)
                dve.tensor_copy(placers[:], place_f[:, :]).then_inc(net.sem("placers_ready"), 1)
                dve.wait_ge(net.sem("placers_ready"), 1)
        end_of_block(net)
        first_room.close()
        if more():
            narrow_attention("x0", "row", True)
        wait_loaded("ffn0")
        if more():
            experts("f0_router", route_mean, "silu", ("g{}", "u{}", "d{}"), E8, 4)
        ffn0_room.close()
        if more():
            narrow_attention("a1", "page", False)
        if more():
            narrow_attention("x1", "add", True)
        with nc.Block() as block:

            @block.vector
            def _(dve):
                dve.wait_ge(loads["ffn1"][2], 16)
                dve.tensor_scalar(l1w, ffn1[:, :], 1.0 / 127.0, None, ALU.mult).then_inc(net.sem("weights_scaled"), 1)
                dve.wait_ge(net.sem("weights_scaled"), 1)
        end_of_block(net)
        if more():
            experts(None, None, "silu", ("L1_g", "L1_u", "L1_d"), 1, 3)
        ffn1_room.close()
        if more():
            stack, sb = scope()
            with stack:
                k = Scan(net, sb)
                scan_prepare(net, k)
                with nc.Fori(0, B, 1) as b:
                    scan_block(net, b, k)
        def place_and_load(room, name, table):
            place(room, name, table)
            with nc.Block() as block:

                @block.sync
                def _(sp):
                    load(sp, name)

        late_room, ffn2_room = ExitStack(), ExitStack()
        place_and_load(ffn2_room, "ffn2", FFN2)
        if more():
            narrow_attention("x2", "full", True)
        wait_loaded("ffn2")
        if more():
            experts("f2_router", route_sinkhorn, "relu", ("g{}", "u{}", "d{}"), E8, 2, keep_x=True)
        ffn2_room.close()
        place_and_load(late_room, "wide", WIDE)
        if more():
            narrow_attention("a3", None, False)
        place_and_load(late_room, "ffn3", FFN3)
        wait_loaded("wide")
        if more():
            stack, sb = scope()
            with stack:
                k = One()
                inner, inner_sb = scope()
                with inner:
                    k.n = Norm(net, inner_sb, B * QT)
                    router_block(net, k, None)
                k = Wide(net, sb)
                scale = 1.0 / float(np.sqrt(np.float32(XHD)))
                wide_prepare(net, k, scale)
                with nc.Fori(0, B, 1) as b:
                    wide_block(net, b, k, scale)
        wait_loaded("ffn3")
        if more():
            experts("f3_router", route_tokens, "bias", ("w{}", None, "o{}"), E8, 2)

        with nc.Block() as block:

            @block.sync
            def _(sp):
                for name in ("wide", "ffn2", "ffn3", "ffn0"):
                    sp.wait_ge(loads[name][2], 16)
                sp.dma_start(ov, net.x[:]).then_inc(stored, 16)
                sp.wait_ge(stored, 16)
        late_room.close()



def pack(table, inputs, dtype):
    offs, n = offsets(table)
    out = np.zeros((P, n), dtype)
    for name, (_, f) in table.items():
        a = f(inputs) if inputs is not None else f()
        at, cols = offs[name]
        assert a.shape[1] == cols, (name, a.shape, cols)
        out[0:a.shape[0], at:at + cols] = a
    return out


PACKS = (("start", START, "f"), ("attn", ATTN, "f"), ("wide", WIDE, "f"), ("ffn0", FFN0, "f"), ("ffn2", FFN2, "f"), ("ffn3", FFN3, "f"), ("ffn1", FFN1, "i"), ("ints", INTS, "i"))


def arrays_of(inputs):
    inputs = {n: np.asarray(a) for n, a in inputs.items()}
    out = {"x_dram": np.ascontiguousarray(inputs["x"])}
    for name, table, kind in PACKS:
        out[f"{name}_dram"] = pack(table, inputs, np.float32 if kind == "f" else np.int32)
    out["constf_dram"] = pack(CONSTF, None, np.float32)
    out["place_dram"] = pack(PLACE, None, np.float32)
    for name, table in (("constb", CONSTB), ("tril", TRIL)):
        out[f"{name}_dram"] = (pack(table, None, np.float32).view(np.uint32) >> 16).astype(np.uint16)
    return out


def build(nc, arrays, upto=12, after=0):
    aps = {n: nc.dram_tensor(n, a.shape, mybir.dt.from_np(a.dtype), kind="ExternalInput").ap() for n, a in arrays.items()}
    out = nc.dram_tensor("out_dram", (B, S, P), F32, kind="ExternalOutput").ap()
    packs = {n[:-5]: ap for n, ap in aps.items()}
    for name in ("constb", "tril"):
        packs[name] = packs[name].bitcast(BF16)
    program(nc, aps["x_dram"], packs, out, upto, after)


def kernel(**inputs):
    import concourse.bacc as bacc
    from concourse.bass_utils import run_bass_kernel_spmd as run

    nc = bacc.Bacc("TRN2", target_bir_lowering=False, num_devices=1)
    arrays = arrays_of(inputs)
    build(nc, arrays)
    r = run(nc, [arrays], core_ids=[0])
    return r.results[0]["out_dram"]
```

```python
from contextlib import ExitStack

import numpy as np

import concourse.bass as bass
from concourse import mybir

F32 = mybir.dt.float32
F32R = mybir.dt.float32r
BF16 = mybir.dt.bfloat16
I32 = mybir.dt.int32
ALU = mybir.AluOpType
ACT = mybir.ActivationFunctionType
AX = mybir.AxisListType.X

P = 128
B, S, S2 = 4, 512, 154
QT = S // P
HEADS = 16
HD = P // HEADS
XHD = 64
KMAIN, KREM = P, S2 - P
KPAD = KMAIN + 32
E8 = 8
EPS = 1e-5
NEG = -1e30
PAGE = 32
FULLRATE = 256
KSPARE = FULLRATE - KPAD
LN_BN = 6
BODY = 2
GROUP = 4
GROUPS = HEADS // GROUP
MROW, MASKROW = 96, 104
ONEROW = 64



def chunked(a, n):
    return a.reshape(n, P, a.shape[-1]).transpose(1, 0, 2).reshape(P, -1)


def col(a):
    return a.reshape(-1, P).T


def row(a):
    return a.reshape(1, -1)


def swap_pairs(w):
    return w.reshape(w.shape[0], -1, 2)[:, :, ::-1].reshape(w.shape[0], -1)


def quads(a):
    out = np.ones((P, a.shape[1]), a.dtype)
    for j in range(4):
        out[32 * j:32 * j + KREM] = a[KMAIN:]
    return out


def in_turn(gate, up):
    return np.concatenate([gate.reshape(P, -1, P), up.reshape(P, -1, P)], axis=2).reshape(P, -1)


def context(i):
    return np.pad(i["ctx_1024"].transpose(2, 0, 1), ((0, 0), (0, 0), (0, KPAD - S2))).reshape(P, -1)


def by_group(a):
    out = np.zeros((P, GROUPS, P), a.dtype)
    for h in range(HEADS):
        out[32 * (h % GROUP):32 * (h % GROUP) + HD, h // GROUP] = a[HD * h:HD * (h + 1)]
    return out.reshape(P, -1)


START = {
    "a0_wq": (P, lambda i: i["L0_attn_Wq"]), "a0_wk": (P, lambda i: i["L0_attn_Wk"]), "a0_wv": (P, lambda i: i["L0_attn_Wv"]),
    "a0_bq": (1, lambda i: col(i["L0_attn_bq"])), "a0_bk": (1, lambda i: col(i["L0_attn_bk"])), "a0_bv": (P, lambda i: row(i["L0_attn_bv"])),
    "ident": (P, lambda i: np.eye(P)), "ones": (P, lambda i: np.ones((P, P))),
}
ATTN = {
    "ctxT": (B * KPAD, lambda i: context(i)), "restT": (B * P, lambda i: np.repeat(context(i).reshape(P, B, 1, KPAD)[..., KMAIN:], 4, axis=2).reshape(P, -1)),
    "x0_wq": (P, lambda i: i["L0_xattn_wq"].T), "x0_wk": (P, lambda i: i["L0_xattn_wk"].T),
    "x0_wv": (P, lambda i: i["L0_xattn_wv"].T), "x0_wo": (GROUPS * P, lambda i: by_group(i["L0_xattn_wo"].T)),
    "x0_bq": (1, lambda i: col(i["L0_xattn_bq"])), "x0_bk": (1, lambda i: col(i["L0_xattn_bk"])),
    "x0_bv": (P, lambda i: row(i["L0_xattn_bv"])), "x0_bo": (P, lambda i: row(i["L0_xattn_bo"])),
    "f0_router": (E8, lambda i: i["L0_ffn_router_w"].T),
    "a1_wq": (P, lambda i: i["L1_attn_wq"]), "a1_wqs": (P, lambda i: swap_pairs(i["L1_attn_wq"])),
    "a1_down": (64, lambda i: i["L1_attn_w_down"]),
    "a1_wk": (P, lambda i: i["L1_attn_wk_up"]), "a1_wks": (P, lambda i: swap_pairs(i["L1_attn_wk_up"])),
    "a1_wv": (P, lambda i: i["L1_attn_wv_up"]), "a1_wo": (GROUPS * P, lambda i: by_group(i["L1_attn_wo"])),
    "x1_wq": (P, lambda i: i["L1_xattn_Wq"]), "x1_wk": (P, lambda i: i["L1_xattn_Wk"]),
    "x1_wv": (P, lambda i: i["L1_xattn_Wv"]), "x1_wo": (GROUPS * P, lambda i: by_group(i["L1_xattn_Wo"])),
    "x1_bq": (1, lambda i: col(i["L1_xattn_bq"])), "x1_bk": (1, lambda i: col(i["L1_xattn_bk"])),
    "x1_bv": (P, lambda i: row(i["L1_xattn_bv"])), "x1_bo": (P, lambda i: row(i["L1_xattn_bo"])),
    "x1_pad": (B * KPAD, lambda i: np.broadcast_to(np.pad(i["mask_Bx1x1xS2_ff0"].reshape(B, S2), ((0, 0), (0, KPAD - S2))).reshape(1, -1), (P, B * KPAD))),
    "m_in": (4 * P, lambda i: i["L2_attn_in_proj_w"].T), "m_in_b": (4, lambda i: col(i["L2_attn_in_proj_b"])),
    "m_conv": (8, lambda i: chunked(i["L2_attn_conv_w"].reshape(2 * P, 4), 2)), "m_conv_b": (2, lambda i: col(i["L2_attn_conv_b"])),
    "m_xp": (2 * 32, lambda i: chunked(i["L2_attn_x_proj_w"].T[:, 0:32], 2)),
    "m_xp_b": (1, lambda i: i["L2_attn_x_proj_b"][0:32].reshape(32, 1)),
    "m_dt": (2 * P, lambda i: np.repeat(chunked(i["L2_attn_x_proj_w"].T[:, 32:33], 2), P, axis=1)),
    "m_dt_b": (1, lambda i: np.broadcast_to(i["L2_attn_x_proj_b"][32:33].reshape(1, 1), (P, 1))),
    "m_alog": (32, lambda i: chunked(i["L2_attn_A_log"], 2)), "m_d": (2, lambda i: col(i["L2_attn_D"])),
    "m_out": (2 * P, lambda i: chunked(i["L2_attn_out_proj_w"].T, 2)), "m_out_b": (P, lambda i: row(i["L2_attn_out_proj_b"])),
    "m_gamma": (P, lambda i: np.broadcast_to(row(i["L2_attn_ln_gamma"]), (P, P))), "m_beta": (P, lambda i: np.broadcast_to(row(i["L2_attn_ln_beta"]), (P, P))),
    "x2_wq": (P, lambda i: i["L2_xattn_Wq"].T), "x2_wk": (P, lambda i: i["L2_xattn_Wk"].T),
    "x2_wv": (P, lambda i: i["L2_xattn_Wv"].T), "x2_wo": (GROUPS * P, lambda i: by_group(i["L2_xattn_Wo"].T)),
    "x2_bq": (1, lambda i: col(i["L2_xattn_bq"])), "x2_bk": (1, lambda i: col(i["L2_xattn_bk"])),
    "x2_bv": (P, lambda i: row(i["L2_xattn_bv"])), "x2_bo": (P, lambda i: row(i["L2_xattn_bo"])),
    "f2_router": (E8, lambda i: i["L2_ffn_router_w"].T), "f2_router_b": (E8, lambda i: np.broadcast_to(row(i["L2_ffn_router_b"]), (P, E8))),
    "f2_temp": (1, lambda i: np.broadcast_to(i["L2_ffn_temperature"].reshape(1, 1), (P, 1))),
    "a3_g": (P, lambda i: np.broadcast_to(row(i["L3_attn_ln_gamma"]), (P, P))), "a3_b": (P, lambda i: np.broadcast_to(row(i["L3_attn_ln_beta"]), (P, P))),
    "a3_wq": (P, lambda i: i["L3_attn_w_qkv"][:, 0:P]), "a3_wk": (P, lambda i: i["L3_attn_w_qkv"][:, P:2 * P]),
    "a3_wv": (P, lambda i: i["L3_attn_w_qkv"][:, 2 * P:3 * P]), "a3_wo": (GROUPS * P, lambda i: by_group(i["L3_attn_w_out"])),
    "f3_router": (E8, lambda i: i["L3_ffn_gate_w"]),
}
WIDE = {
    "x3_wq": (8 * P, lambda i: i["L3_xattn_WQ"].transpose(1, 0, 2).reshape(P, -1)), "x3_wk": (8 * P, lambda i: i["L3_xattn_WK"].transpose(1, 0, 2).reshape(P, -1)),
    "x3_wv": (8 * P, lambda i: i["L3_xattn_WV"].transpose(1, 0, 2).reshape(P, -1)),
    "x3_bq": (8, lambda i: col(i["L3_xattn_bQ"])), "x3_bk": (8, lambda i: col(i["L3_xattn_bK"])), "x3_bv": (8 * P, lambda i: np.broadcast_to(row(i["L3_xattn_bV"]), (P, 8 * P))),
    "x3_wo": (8 * P, lambda i: chunked(i["L3_xattn_WO"], 8)), "x3_bo": (P, lambda i: row(i["L3_xattn_bO"])),
}
FFN0 = {}
for _e in range(E8):
    FFN0[f"w{_e}"] = (2 * 512, lambda i, e=_e: in_turn(i["L0_ffn_gate_w"][e].T, i["L0_ffn_up_w"][e].T))
    FFN0[f"d{_e}"] = (512, lambda i, e=_e: chunked(i["L0_ffn_down_w"][e].T, 4))
FFN2, FFN3 = {}, {}
for _e in range(E8):
    FFN2[f"w{_e}"] = (2 * 256, lambda i, e=_e: in_turn(i["L2_ffn_wg"][e], i["L2_ffn_wp"][e]))
    FFN2[f"d{_e}"] = (256, lambda i, e=_e: chunked(i["L2_ffn_wo"][e], 2))
for _e in range(E8):
    FFN3[f"w{_e}"] = (256, lambda i, e=_e: i["L3_ffn_w1"][e])
    FFN3[f"o{_e}"] = (256, lambda i, e=_e: chunked(i["L3_ffn_w2"][e], 2))
    FFN3[f"b{_e}"] = (2, lambda i, e=_e: col(i["L3_ffn_b1"][e]))
FFN3["b2"] = (E8 * P, lambda i: row(i["L3_ffn_b2"]))
FFN1 = {
    "L1_w": (2 * 384, lambda i: in_turn(i["L1_ffn_w_gate"].T, i["L1_ffn_w_up"].T)), "L1_d": (384, lambda i: chunked(i["L1_ffn_w_down"].T, 3)),
}
INTS = {
    "m0": (B * KPAD, lambda i: np.broadcast_to(np.pad(i["mask_Bx1x1xS2_ik0"].reshape(B, S2), ((0, 0), (0, KPAD - S2))).reshape(1, -1), (P, B * KPAD))),
    "kq": (B * KPAD, lambda i: np.broadcast_to(np.pad(i["mask_BxS2_ik0"], ((0, 0), (0, KPAD - S2))).reshape(1, -1), (P, B * KPAD))),
    "kt": (B, lambda i: i["mask_BxS2_ik0"].T[0:KMAIN]), "kr": (B, lambda i: quads(i["mask_BxS2_ik0"].T)),
    "aq": (QT * KPAD, lambda i: chunked(np.pad(i["mask_SxS2_ik1"], ((0, 0), (0, KPAD - S2))), QT)),
    "at": (S, lambda i: i["mask_SxS2_ik1"].T[0:KMAIN]), "ar": (S, lambda i: quads(i["mask_SxS2_ik1"].T)),
    "len": (B, lambda i: np.broadcast_to(i["_lenS2"].reshape(1, B), (P, B))),
}


def rope():
    inv = 1.0 / 10000.0 ** (np.arange(0, HD, 2, dtype=np.float32) / HD)
    ang = np.outer(np.arange(S, dtype=np.float32), inv)
    cos, sin = np.cos(ang), np.sin(ang)
    c = np.repeat(cos.T, 2, axis=0)
    s = np.stack([-sin.T, sin.T], axis=1).reshape(HD, S)
    return np.tile(c, (HEADS, 1)).astype(np.float32), np.tile(s, (HEADS, 1)).astype(np.float32)


CONSTF = {
    "cos": (S, lambda: rope()[0]), "sin": (S, lambda: rope()[1]),
    "halfsel": (2, lambda: np.arange(P)[:, None] // XHD == np.arange(2)),
    "sums": (GROUP, lambda: np.arange(P)[:, None] == 32 * np.arange(GROUP) + HD), "stackheads": (GROUP, lambda: stack_heads()), "rank": (E8, lambda: np.broadcast_to(E8 - np.arange(E8), (P, E8))),
    "kidx": (KPAD, lambda: np.broadcast_to(np.arange(KPAD), (P, KPAD))),
}
TRIL = {"tril": (QT * S, lambda: chunked(np.tril(np.ones((S, S))), QT))}
CONSTB = {
    "negi": (P, lambda: NEG * np.eye(P)),
    "sel": (32 * P, lambda: np.repeat((np.arange(P)[:, None] % 32 == np.arange(32)) & (np.arange(P)[:, None] < 96), P, axis=1)),
    "pageq": (P, lambda: np.arange(P)[None] // PAGE > np.arange(P)[:, None] // PAGE),
    "paget": (P, lambda: np.arange(P)[:, None] // PAGE > np.arange(P)[None] // PAGE),
    "cq": (QT * KPAD, lambda: chunked(np.arange(KPAD)[None] > np.arange(S)[:, None], QT)),
}


def placer(group, targets):
    out = np.zeros((P, P))
    for t in targets:
        out[32 * group + np.arange(32), 32 * t + np.arange(32)] = 1
    return out


def key_rows():
    out = np.zeros((P, P))
    out[0, MASKROW] = out[32, MASKROW + 1] = 1
    out[ONEROW, MROW:MROW + 2 * GROUP] = 1
    return out


def query_rows():
    out = np.zeros((P, P))
    out[ONEROW, MASKROW:MASKROW + 2] = 1
    return out


def stack_heads():
    out = np.zeros((P, GROUP))
    for j in range(GROUP):
        for t in range(3):
            out[32 * t + HD * j:32 * t + HD * (j + 1), j] = 1
        out[MROW + 2 * j:MROW + 2 * j + 2, j] = 1
    out[MASKROW:MASKROW + 2] = 1
    return out


PLACE = {}
for _g in range(GROUPS):
    PLACE[f"q_hi{_g}"] = (P, lambda g=_g: placer(g, (0, 1)))
    PLACE[f"q_lo{_g}"] = (P, lambda g=_g: placer(g, (2,)))
    PLACE[f"k_hi{_g}"] = (P, lambda g=_g: placer(g, (0, 2)))
    PLACE[f"k_lo{_g}"] = (P, lambda g=_g: placer(g, (1,)))
PLACE["identr"] = (3 * P, lambda: np.pad(np.eye(P), ((0, 0), (P, P))))
PLACE["key_rows"] = (P, key_rows)
PLACE["query_rows"] = (P, query_rows)


def offsets(table):
    at, out = 0, {}
    for name, (n, _) in table.items():
        out[name] = (at, n)
        at += n
    return out, at



class Sems:

    def __init__(self, nc):
        self.nc, self.by = nc, {}

    def __call__(self, name):
        if name not in self.by:
            self.by[name] = self.nc.alloc_semaphore(name)
        return self.by[name]


class Chain:

    def __init__(self, eng, sem):
        self.eng, self.sem, self.n = eng, sem, 0

    def link(self, ins):
        self.n += 1
        ins.then_inc(self.sem, 1)
        self.eng.wait_ge(self.sem, self.n)


def over(ap, axis, n):
    v = ap.unsqueeze(axis)
    shape = list(v.shape)
    shape[axis] = n
    return v.to_broadcast(shape)


class Net:

    def __init__(self, nc, ctx):
        self.nc, self.ctx = nc, ctx
        self.sem = Sems(nc)
        self.names = 0
        self.x = self.sb("x", [P, B * QT, P])
        self.xnT_all = self.sb("xnT_all", [P, B * S])
        self.logits = self.sb("logits", [P, QT, B, E8])
        self.coef = self.sb("coef", [P, QT, B, E8])
        self.ps = [ctx.enter_context(nc.psum_tensor(f"bank{n}", [P, 512], F32)) for n in range(8)]
        self.weights = {}

    def sb(self, name, shape, dt=F32):
        return self.ctx.enter_context(self.nc.sbuf_tensor(name, shape, dt))

    def table(self, name, table, dt=F32, tile=None):
        offs, n = offsets(table)
        t = self.sb(name, [P, n], dt) if tile is None else tile
        return t, offs, n

    def w(self, name):
        t, (at, n) = self.weights[name]
        return t[:, at:at + n]


def end_of_block(net):
    nums = sorted(s.num for s in net.sem.by.values())
    assert nums[-1] - nums[0] + 1 == len(nums)
    net.nc.vector.sem_clear(range(nums[0], nums[-1] + 1))
    net.nc.all_engine_barrier()



def vector_layernorm(dve, ch, xin, xn, n, done=None):
    for t in range(n.tiles):
        last = dve.bn_stats(n.stats[:, t, :], xin[:, t, :])
    ch.link(last)
    for t in range(n.tiles):
        last = dve.bn_aggr(n.aggr[:, t, :], n.stats[:, t, :])
    ch.link(last)
    ch.link(dve.tensor_scalar(n.var[:], n.aggr[:, :, 1], EPS, None, ALU.add))
    dve.tensor_scalar(n.vh[:], n.var[:], -0.5, None, ALU.mult)
    ch.link(dve.tensor_scalar(n.bits[:], n.var[:].bitcast(I32), 1, None, ALU.logical_shift_right))
    ch.link(dve.tensor_scalar(n.rstd[:].bitcast(I32), n.bits[:], -1.0, float(0x5F3759DF), ALU.mult, ALU.add))
    for _ in range(3):
        ch.link(dve.tensor_tensor(n.sq[:], n.rstd[:], n.rstd[:], ALU.mult))
        ch.link(dve.tensor_tensor(n.sq[:], n.sq[:], n.vh[:], ALU.mult))
        ch.link(dve.scalar_tensor_tensor(n.rstd[:], n.sq[:], 1.5, n.rstd[:], ALU.add, ALU.mult))
    for t in range(n.tiles):
        last = dve.tensor_scalar(xn[:, t, :], xin[:, t, :], n.aggr[:, t, 0:1], n.rstd[:, t:t + 1], ALU.subtract, ALU.mult)
        if done is not None and t % QT == QT - 1:
            last.then_inc(done, 1)
    return last


def tensor_transpose_tiles(pe, out, tiles, ident):
    for t in range(QT):
        last = pe.transpose(out[:, t * P:(t + 1) * P], tiles[:, t, :], ident)
    return last


class Norm:

    def __init__(self, net, sb, tiles=QT):
        self.tiles = tiles
        self.xn = sb("xn", [P, tiles, P])
        self.stats = sb("stats", [P, tiles, LN_BN])
        self.aggr = sb("aggr", [P, tiles, 2])
        self.rstd = sb("rstd", [P, tiles])
        self.var, self.vh, self.sq = sb("var", [P, tiles]), sb("vh", [P, tiles]), sb("sq", [P, tiles])
        self.bits = sb("bits", [P, tiles], I32)
        if tiles == QT:
            self.xnT = sb("xnT", [P, S])


def x_of(net, b):
    return net.x[:, bass.ts(b, QT), :]



def single_head_block(net, b, k):
    nc, sem, ps, w = net.nc, net.sem, net.ps, net.w
    scale = 1.0 / float(np.sqrt(np.float32(P)))
    with nc.Block() as block:

        @block.vector
        def _(dve):
            ch = Chain(dve, sem("dve_chain"))
            vector_layernorm(dve, ch, x_of(net, b), k.n.xn, k.n).then_inc(sem("xn_ready"), 1)
            dve.wait_ge(sem("q_done"), 1)
            dve.tensor_scalar(k.qT[:], ps[0][:], w("a0_bq"), None, ALU.add).then_inc(sem("qT_ready"), 1)
            dve.wait_ge(sem("k_done"), 1)
            dve.tensor_scalar(k.kT[:], ps[1][:], w("a0_bk"), None, ALU.add).then_inc(sem("kT_ready"), 1)
            tril = w("tril").rearrange("p (t k) -> p t k", t=QT)
            for t in range(QT):
                dve.wait_ge(sem("scores_done"), t + 1)
                ch.link(dve.scalar_tensor_tensor(k.s[:, t, :], ps[t][:], scale, tril[:, t, :], ALU.mult, ALU.mult))
                ch.link(dve.reduce_max(k.mx[:, t:t + 1], k.s[:, t, :], AX))
                dve.tensor_scalar(k.negm[:, t:t + 1], k.mx[:, t:t + 1], -1.0, None, ALU.mult).then_inc(sem("negm_ready"), 1)
            dve.wait_ge(sem("exp_done"), QT)
            dve.wait_ge(sem("v_done"), 1)
            ch.link(dve.reciprocal(k.rs[:], k.sum[:]))
            ch.link(dve.tensor_tensor(k.rs[:], k.rs[:], k.sum[:], ALU.mult))
            for t in range(QT):
                last = dve.scalar_tensor_tensor(x_of(net, b)[:, t, :], ps[4][:, t * P:(t + 1) * P], k.rs[:, t:t + 1],
                                                x_of(net, b)[:, t, :], ALU.mult, ALU.add)
            ch.link(last)

        @block.scalar
        def _(act):
            act.wait_ge(sem("xT_done"), 1)
            nc.scalar.copy(k.n.xnT[:], ps[7][:]).then_inc(sem("xnT_ready"), 1)
            for t in range(QT):
                act.wait_ge(sem("negm_ready"), t + 1)
                nc.scalar.activation(k.p[:, t, :], k.s[:, t, :], ACT.Exp, bias=k.negm[:, t:t + 1],
                                     accum_out=k.sum[:, t:t + 1]).then_inc(sem("exp_done"), 1)

        @block.tensor
        def _(pe):
            pe.wait_ge(sem("xn_ready"), 1)
            tensor_transpose_tiles(pe, ps[7], k.n.xn, w("ident")).then_inc(sem("xT_done"), 1)
            pe.wait_ge(sem("xnT_ready"), 1)
            pe.matmul(ps[0][:], w("a0_wq"), k.n.xnT[:], start=True, stop=True).then_inc(sem("q_done"), 1)
            pe.matmul(ps[1][:], w("a0_wk"), k.n.xnT[:], start=True, stop=True).then_inc(sem("k_done"), 1)
            for t in range(QT):
                pe.matmul(ps[4][:, t * P:(t + 1) * P], k.n.xnT[:, t * P:(t + 1) * P], w("a0_wv"), start=True, stop=False)
                last = pe.matmul(ps[4][:, t * P:(t + 1) * P], w("ones")[0:1, :], w("a0_bv")[0:1, :], start=False, stop=True)
            last.then_inc(sem("v_done"), 1)
            pe.wait_ge(sem("qT_ready"), 1)
            pe.wait_ge(sem("kT_ready"), 1)
            for t in range(QT):
                pe.matmul(ps[t][:], k.qT[:, t * P:(t + 1) * P], k.kT[:], start=True, stop=True).then_inc(sem("scores_done"), 1)
    end_of_block(net)





class Narrow:

    def __init__(self, net, sb, kind, ctx_keys):
        self.kind, self.ctx_keys = kind, ctx_keys
        self.nk = KPAD if ctx_keys else S
        self.nkt = 1 if ctx_keys else QT
        self.q_hi, self.q_lo = sb("q_hi", [P, B * S], F32R), sb("q_lo", [P, B * S], F32R)
        self.k_hi, self.k_lo = sb("k_hi", [P, B * self.nk + KSPARE], F32R), sb("k_lo", [P, B * self.nk + KSPARE], F32R)
        self.values = sb("values", [P, B * self.nkt * P])
        self.rests = sb("rests", [P, B * P]) if ctx_keys else None

    def more_buffers(self, net, sb):
        masks = BODY if self.kind in ("row", "add") else 1
        self.rows_all = sb("rows", [P, masks * self.nk + KSPARE], F32R)
        self.rows = self.rows_all[:, 0:masks * self.nk].rearrange("p (e k) -> p e k", e=masks)
        self.Q = sb("Q", [P, 2, S], F32R)
        self.K = sb("K", [P, 2, GROUP, self.nk], F32R)
        self.v = sb("v", [P, 2, self.nkt, GROUP, 32])
        self.p = sb("p", [P, 3, S])
        self.m = sb("m", [P, QT, HEADS])
        self.mp = sb("mp", [P, 2, QT, P], F32R)
        self.o = sb("o", [P, 2, S])
        self.rs = sb("rs", [P, QT * GROUP])
        self.rx = sb("rx", [P, QT, P])
        if self.kind in ("row", "add"):
            self.ones = sb("ones", [P, S], F32R)
        if self.ctx_keys:
            self.kr = sb("kr", [P, 2, GROUP, KPAD - KMAIN], F32R)
            self.vr = sb("vr", [P, 2, P])
            self.rf = sb("rf", [P, KPAD])
            self.rb = sb("rb", [P, 2, KPAD], F32R) if self.kind == "add" else None
        if self.kind == "full":
            self.mq = sb("mq", [P, BODY, QT, KPAD], BF16)
            self.mt = sb("mt", [P, BODY, S], BF16)
            self.mr = sb("mr", [P, BODY, S], BF16)
            self.kc = sb("kc", [P, 2])

    def chunks(self, g):
        if self.ctx_keys:
            return [(t, h, 2, S2) for t in range(QT) for h in (GROUP * g, GROUP * g + 2)]
        return [(t, h, 1, (t + 1) * P if self.kind == "page" else S) for t in range(QT) for h in range(GROUP * g, GROUP * (g + 1))]

    def units(self, g):
        if self.ctx_keys:
            return [("rest", g, 0, 0)] + [("main", h, 0, 0) for h in range(GROUP * g, GROUP * (g + 1))]
        return [("main", h, c, c * P if self.kind == "page" else 0) for h in range(GROUP * g, GROUP * (g + 1)) for c in range(QT)]


def narrow_project(net, k, pre, scale, sb):
    nc, sem, ps, w = net.nc, net.sem, net.ps, net.w
    n = Norm(net, sb, B * QT)
    full = sb("full", [P, 2, 2, S])
    if k.kind == "page":
        lat, turned = sb("lat", [64, B * S]), sb("turned", [P, 2, S])
    bias = pre.startswith("x")
    xnT = net.xnT_all
    with nc.Block() as block:

        @block.vector
        def _(dve):
            ch = Chain(dve, sem("dve_chain"))
            if pre == "a3":
                ch.link(vector_layernorm(dve, ch, net.x, n.xn, n))
                ch.link(vector_layernorm(dve, ch, n.xn, n.xn, n))
                for b in range(B):
                    tiles = n.xn[:, b * QT:(b + 1) * QT, :]
                    ch.link(dve.tensor_tensor(tiles, tiles, over(w("a3_g"), 1, QT), ALU.mult))
                    dve.tensor_tensor(tiles, tiles, over(w("a3_b"), 1, QT), ALU.add).then_inc(sem("xn_ready"), 1)
            else:
                vector_layernorm(dve, ch, net.x, n.xn, n, sem("xn_ready"))
            for parts in (k.k_hi, k.k_lo):
                last = dve.memset(parts[:, B * k.nk:B * k.nk + KSPARE].bitcast(F32), 0.0)
            ch.link(last)
            for b in range(B):
                for i, (name, hi, lo, m) in enumerate((("k", k.k_hi, k.k_lo, k.nk), ("q", k.q_hi, k.q_lo, S))):
                    s = scale if name == "q" else 1.0
                    out, at = full[:, b % 2, i, 0:m], slice(b * m, (b + 1) * m)
                    dve.wait_ge(sem(f"{name}_done"), b + 1)
                    if b >= 2:
                        dve.wait_ge(sem(f"{name}_parts"), b - 1)
                    if k.kind == "page":
                        dve.scalar_tensor_tensor(turned[:, 0, :], ps[2 * i][:], s, w("cos"), ALU.mult, ALU.mult)
                        ch.link(dve.scalar_tensor_tensor(turned[:, 1, :], ps[2 * i + 1][:], s, w("sin"), ALU.mult, ALU.mult))
                        ch.link(dve.tensor_tensor(out, turned[:, 0, :], turned[:, 1, :], ALU.add))
                    elif bias:
                        ch.link(dve.tensor_scalar(out, ps[2 * i][:, 0:m], w(f"{pre}_b{name}"), s, ALU.add, ALU.mult))
                    else:
                        ch.link(dve.tensor_scalar(out, ps[2 * i][:, 0:m], s, None, ALU.mult))
                    dve.tensor_copy(hi[:, at], out).then_inc(sem(f"{name}_high"), 1)
            dve.wait_ge(sem("q_high"), B)

        @block.gpsimd
        def _(pool):
            for b in range(B):
                for i, (name, hi, lo, m) in enumerate((("k", k.k_hi, k.k_lo, k.nk), ("q", k.q_hi, k.q_lo, S))):
                    at = slice(b * m, (b + 1) * m)
                    pool.wait_ge(sem(f"{name}_high"), b + 1)
                    nc.gpsimd.tensor_tensor(lo[:, at], full[:, b % 2, i, 0:m], hi[:, at].bitcast(F32), ALU.subtract).then_inc(sem(f"{name}_parts"), 1)
            pool.wait_ge(sem("q_parts"), B)

        @block.scalar
        def _(act):
            for b in range(B):
                act.wait_ge(sem("xT_done"), b + 1)
                nc.scalar.copy(xnT[:, b * S:(b + 1) * S], ps[6 + b % 2][:]).then_inc(sem("xnT_ready"), 1)
                if k.kind == "page":
                    act.wait_ge(sem("lat_done"), b + 1)
                    nc.scalar.copy(lat[:, b * S:(b + 1) * S], ps[6 + b % 2][0:64, :]).then_inc(sem("lat_ready"), 1)
                act.wait_ge(sem("v_done"), b + 1)
                if k.ctx_keys:
                    nc.scalar.copy(k.values[:, b * P:(b + 1) * P], ps[4 + b % 2][:, 0:P])
                    nc.scalar.copy(k.rests[:, b * P:(b + 1) * P], ps[4 + b % 2][:, P:2 * P]).then_inc(sem("v_kept"), 1)
                else:
                    nc.scalar.copy(k.values[:, b * S:(b + 1) * S], ps[4 + b % 2][:]).then_inc(sem("v_kept"), 1)

        @block.tensor
        def _(pe):
            ctx = w("ctxT").rearrange("p (b k) -> p b k", b=B)

            for b in range(B):
                pe.wait_ge(sem("xn_ready"), b + 1)
                if b >= 2:
                    pe.wait_ge(sem("lat_ready" if k.kind == "page" else "xnT_ready"), b - 1)
                tensor_transpose_tiles(pe, ps[6 + b % 2], n.xn[:, b * QT:(b + 1) * QT, :], w("ident")).then_inc(sem("xT_done"), 1)
                if k.ctx_keys:
                    if b >= 1:
                        pe.wait_ge(sem("k_high"), b)
                    pe.matmul(ps[0][:, 0:k.nk], w(f"{pre}_wk"), ctx[:, b, :], start=True, stop=True).then_inc(sem("k_done"), 1)
                    if b >= 2:
                        pe.wait_ge(sem("v_kept"), b - 1)
                    out = ps[4 + b % 2]
                    pe.matmul(out[:, 0:P], ctx[:, b, 0:P], w(f"{pre}_wv"), start=True, stop=False)
                    pe.matmul(out[:, 0:P], w("ones")[0:1, :], w(f"{pre}_bv")[0:1, :], start=False, stop=True)
                    pe.matmul(out[:, P:2 * P], w("restT")[:, b * P:(b + 1) * P], w(f"{pre}_wv"), start=True, stop=False)
                    pe.matmul(out[:, P:2 * P], w("ones")[0:1, :], w(f"{pre}_bv")[0:1, :], start=False, stop=True).then_inc(sem("v_done"), 1)
                pe.wait_ge(sem("xnT_ready"), b + 1)
                x = xnT[:, b * S:(b + 1) * S]
                if b >= 1:
                    pe.wait_ge(sem("q_high"), b)
                if k.kind == "page":
                    pe.matmul(ps[6 + b % 2][0:64, :], w("a1_down"), x, start=True, stop=True).then_inc(sem("lat_done"), 1)
                    pe.matmul(ps[2][:], w("a1_wq"), x, start=True, stop=True)
                    pe.matmul(ps[3][:], w("a1_wqs"), x, start=True, stop=True).then_inc(sem("q_done"), 1)
                    pe.wait_ge(sem("lat_ready"), b + 1)
                    x = lat[:, b * S:(b + 1) * S]
                    pe.matmul(ps[0][:], w("a1_wk")[0:64, :], x, start=True, stop=True)
                    pe.matmul(ps[1][:], w("a1_wks")[0:64, :], x, start=True, stop=True).then_inc(sem("k_done"), 1)
                else:
                    if not k.ctx_keys:
                        pe.matmul(ps[0][:], w(f"{pre}_wk"), x, start=True, stop=True).then_inc(sem("k_done"), 1)
                    pe.matmul(ps[2][:], w(f"{pre}_wq"), x, start=True, stop=True).then_inc(sem("q_done"), 1)
                if not k.ctx_keys:
                    if b >= 2:
                        pe.wait_ge(sem("v_kept"), b - 1)
                    for c in range(QT):
                        last = pe.matmul(ps[4 + b % 2][:, c * P:(c + 1) * P], x[:, c * P:(c + 1) * P], w(f"{pre}_wv")[0:x.shape[0], :], start=True, stop=True)
                    last.then_inc(sem("v_done"), 1)
    end_of_block(net)


def narrow_prepare(net, k):
    with net.nc.Block() as block:

        @block.gpsimd
        def _(pool):
            pool.memset(k.mp[:].bitcast(F32), 0.0).then_inc(net.sem("zeroed"), 1)
            pool.memset(k.m[:], 0.0).then_inc(net.sem("m_zeroed"), 1)
            pool.wait_ge(net.sem("m_zeroed"), 1)

        @block.vector
        def _(dve):
            ch = Chain(dve, net.sem("dve_chain"))
            if k.kind in ("row", "add"):
                dve.memset(k.ones[:].bitcast(F32), 0.0)
            if k.ctx_keys:
                dve.memset(k.vr[:], 0.0)
            dve.memset(k.rows_all[:].bitcast(F32), 0.0)
            ch.link(dve.memset(k.v[:], 0.0))
            dve.memset(k.v[:, :, :, :, HD:HD + 1], 1.0)
            last = dve.memset(k.rows[ONEROW:ONEROW + 1].bitcast(F32), 1.0)
            if k.kind in ("row", "add"):
                dve.memset(k.ones[ONEROW:ONEROW + 1, :].bitcast(F32), 1.0)
                last = dve.memset(k.rows[0:1, :, S2:KPAD].bitcast(F32), NEG)
            if k.ctx_keys:
                for j in range(GROUP):
                    last = dve.memset(k.vr[32 * j:32 * j + KREM, :, 32 * j + HD:32 * j + HD + 1], 1.0)
            dve.wait_ge(net.sem("zeroed"), 1)
            if k.kind in ("row", "add"):
                last = dve.memset(k.mp[:, :, :, MASKROW:MASKROW + 2].bitcast(F32), 1.0)
            ch.link(last)
    end_of_block(net)


def vector_narrow_masks(net, dve, ch, k, b, e):
    w = net.w
    if k.kind == "row":
        m0 = w("m0").rearrange("p (b k) -> p b k", b=B)
        ch.link(dve.tensor_copy(k.rf[:], m0[:, b, :]))
        ch.link(dve.tensor_scalar(k.rows[0:1, e, 0:S2], k.rf[0:1, 0:S2], 0.0, NEG, ALU.is_equal, ALU.mult))
    if k.kind == "add":
        pad = w("x1_pad").rearrange("p (b k) -> p b k", b=B)
        ch.link(dve.tensor_scalar(k.rf[:], pad[:, b, :], -1e12, None, ALU.mult))
        ch.link(dve.tensor_copy(k.rb[:, 0, :], k.rf[:]))
        ch.link(dve.tensor_tensor(k.rb[:, 1, :], k.rf[:], k.rb[:, 0, :].bitcast(F32), ALU.subtract))
        for n in range(2):
            last = dve.tensor_copy(k.rows[32 * n:32 * n + 1, e, 0:S2], k.rb[32 * n:32 * n + 1, n, 0:S2].bitcast(F32))
        ch.link(last)
    if k.kind == "full":
        kq = w("kq").rearrange("p (b k) -> p b k", b=B)
        aq = w("aq").rearrange("p (t k) -> p t k", t=QT)
        dve.tensor_scalar(k.rf[:], kq[:, b, :], 0, None, ALU.not_equal)
        dve.tensor_scalar(k.kc[:, 0:1], w("kt")[:, bass.ts(b, 1)], 0, None, ALU.not_equal)
        ch.link(dve.tensor_scalar(k.kc[:, 1:2], w("kr")[:, bass.ts(b, 1)], 0, None, ALU.not_equal))
        for t in range(QT):
            dve.scalar_tensor_tensor(k.mq[:, e, t, :], aq[:, t, :], 0.0, k.rf[:], ALU.not_equal, ALU.max)
        dve.tensor_scalar(k.mt[:, e], w("at"), 0.0, k.kc[:, 0:1], ALU.not_equal, ALU.max)
        ch.link(dve.tensor_scalar(k.mr[:, e], w("ar"), 0.0, k.kc[:, 1:2], ALU.not_equal, ALU.max))



def narrow_block(net, b0, k, pre):
    nc, sem, ps, w = net.nc, net.sem, net.ps, net.w
    bias = pre.startswith("x")
    nk = k.nk
    groups = BODY * GROUPS
    units = [(n,) + u for n in range(groups) for u in k.units(n % GROUPS)]
    chunks = [(n,) + c for n in range(groups) for c in k.chunks(n % GROUPS)]
    per_group, nchunks = len(units) // groups, len(chunks) // groups
    oT = net.xnT_all[:].rearrange("p (g q) -> p g q", g=GROUPS)

    def ends(n):
        return n % GROUPS == GROUPS - 1

    with nc.Block() as block:

        @block.vector
        def _(dve):
            ch = Chain(dve, sem("dve_chain"))

            def masks(e):
                if k.kind in ("row", "add", "full"):
                    vector_narrow_masks(net, dve, ch, k, b0 + e, e)
                    dve.sem_inc(sem("masks_ready"), 1)

            def stack_keys(n):
                if n >= 2:
                    dve.wait_ge(sem("st_done"), per_group * (n - 1))
                dve.wait_ge(sem("k_stacked"), n + 1)
                if k.ctx_keys:
                    dve.tensor_tensor(k.kr[:, n % 2], over(ps[7][:, KMAIN:KPAD], 1, GROUP), over(w("stackheads"), 2, KPAD - KMAIN), ALU.mult)
                dve.tensor_tensor(k.K[:, n % 2], over(ps[7][:, 0:nk], 1, GROUP), over(w("stackheads"), 2, nk), ALU.mult).then_inc(sem("K_ready"), 1)

            def maxima(n):
                for i in range(nchunks * n, nchunks * (n + 1)):
                    _, t, h, m, keys = chunks[i]
                    dve.wait_ge(sem("scores_done"), i + 1)
                    dve.reduce_max(k.m[:, t, h:h + m], ps[3 + i % 2][:, 0:m * keys].rearrange("p (h k) -> p h k", h=m), AX).then_inc(sem("max_done"), 1)
                dve.wait_ge(sem("max_done"), nchunks * (n + 1))
                if n >= 2:
                    dve.wait_ge(sem("mT_done"), n - 1)
                g = n % GROUPS
                hi = k.mp[:, n % 2, :, MROW:MROW + 2 * GROUP:2]
                lo = k.mp[:, n % 2, :, MROW + 1:MROW + 2 * GROUP:2]
                top = k.m[:, :, GROUP * g:GROUP * (g + 1)]
                ch.link(dve.tensor_scalar(hi, top, -1.0, None, ALU.mult))
                dve.scalar_tensor_tensor(lo, top, -1.0, hi.bitcast(F32), ALU.mult, ALU.subtract).then_inc(sem("mp_ready"), 1)

            def normalise(n):
                dve.wait_ge(sem("sums_done"), n + 1)
                ch.link(dve.reciprocal(k.rs[:], ps[5 + n % 2][:, 0:QT * GROUP]))
                dve.tensor_copy(k.rx[:].rearrange("p t (j r) -> p (t j) r", j=GROUP), over(k.rs[:], 2, 32)).then_inc(sem("rx_ready"), 1)
                dve.wait_ge(sem("factors_done"), n + 1)
                if n >= GROUPS:
                    dve.wait_ge(sem("y_done"), n // GROUPS)
                dve.tensor_tensor(oT[:, n % GROUPS, :], k.o[:, n % 2, :], ps[5 + n % 2][:], ALU.mult).then_inc(sem("oT_ready"), 1)

            def add_output(e):
                x = x_of(net, b0 + e)
                dve.wait_ge(sem("y_done"), e + 1)
                dve.tensor_tensor(x, x, ps[2][:].rearrange("p (t d) -> p t d", t=QT), ALU.add).then_inc(sem("x_added"), 1)

            masks(0)
            for n in range(groups):
                stack_keys(n)
                if n + 1 < BODY:
                    masks(n + 1)
                maxima(n)
                if n >= 2:
                    normalise(n - 2)
                if n >= 3 and ends(n - 3):
                    add_output((n - 3) // GROUPS)
            normalise(groups - 2)
            normalise(groups - 1)
            add_output(BODY - 1)
            dve.wait_ge(sem("x_added"), BODY)

        @block.gpsimd
        def _(pool):
            def values(n):
                e, g = divmod(n, GROUPS)
                if n >= 2:
                    pool.wait_ge(sem("pv_done"), per_group * (n - 1))
                all_heads = k.values[:, bass.ts(b0 + e, k.nkt * P)].rearrange("p (c h d) -> p c h d", c=k.nkt, h=HEADS)
                nc.gpsimd.tensor_copy(k.v[:, n % 2, :, :, 0:HD], all_heads[:, :, GROUP * g:GROUP * (g + 1), :]).then_inc(sem("v_ready"), 1)
                if k.ctx_keys:
                    rests = k.rests[:, bass.ts(b0 + e, P)].rearrange("p (h d) -> p h d", h=HEADS)
                    for j in range(GROUP):
                        pool.wait_ge(sem("v_ready"), (GROUP + 1) * n + j + 1)
                        rows = slice(32 * j, 32 * j + KREM)
                        nc.gpsimd.tensor_copy(k.vr[rows, n % 2, 32 * j:32 * j + HD], rests[rows, GROUP * g + j, :]).then_inc(sem("v_ready"), 1)
                    pool.wait_ge(sem("v_ready"), (GROUP + 1) * (n + 1))
                else:
                    pool.wait_ge(sem("v_ready"), n + 1)

            for n in range(groups):
                values(n)

        @block.scalar
        def _(act):
            def copy_queries(n):
                act.wait_ge(sem("q_stacked"), n + 1)
                nc.scalar.copy(k.Q[:, n % 2, :], ps[2][:]).then_inc(sem("Q_ready"), 1)

            def copy_maxima(n):
                act.wait_ge(sem("mT_done"), n + 1)
                nc.scalar.copy(k.Q[MROW:P, n % 2, :], ps[7][MROW:P, :]).then_inc(sem("maxima_in"), 1)

            def copy_products(n):
                act.wait_ge(sem("pv_done"), per_group * (n + 1))
                if n >= 2:
                    act.wait_ge(sem("oT_ready"), n - 1)
                nc.scalar.copy(k.o[:, n % 2, :], ps[5 + n % 2][:]).then_inc(sem("o_ready"), 1)

            copy_queries(0)
            copy_maxima(0)
            for u, (n, what, h, kt, q0) in enumerate(units):
                at = u % per_group
                act.wait_ge(sem("st_done"), u + 1)
                if u >= 3:
                    act.wait_ge(sem("pv_done"), u - 2)
                nc.scalar.activation(k.p[:, u % 3, q0:S], ps[u % 2][:, q0:S], ACT.Exp).then_inc(sem("exp_done"), 1)
                if at == 0 and n + 1 < groups:
                    copy_queries(n + 1)
                if at == 2 and n >= 1:
                    copy_products(n - 1)
                if at == per_group - 1 and n + 1 < groups:
                    copy_maxima(n + 1)
            copy_products(groups - 1)

        @block.tensor
        def _(pe):
            def stack_parts(n):
                e, g = divmod(n, GROUPS)
                width = max(nk, FULLRATE)
                q_at, k_at = bass.ts(b0 + e, S), bass.ds((b0 + e) * nk, width)
                r_at = e * nk if k.kind in ("row", "add") else 0
                rowmask = k.kind in ("row", "add")
                if g == 0 and k.ctx_keys:
                    pe.wait_ge(sem("masks_ready"), e + 1)
                if n >= 1:
                    pe.wait_ge(sem("maxima_in"), n)
                keys = ps[7][:, 0:width]
                pe.matmul(keys, w(f"k_hi{g}"), k.k_hi[:, k_at], start=True, stop=False)
                pe.matmul(keys, w(f"k_lo{g}"), k.k_lo[:, k_at], start=False, stop=False)
                pe.matmul(keys, w("key_rows"), k.rows_all[:, r_at:r_at + width], start=False, stop=True).then_inc(sem("k_stacked"), 1)
                if n >= 1:
                    pe.wait_ge(sem("Q_ready"), n)
                if n >= 4 and ends(n - 4):
                    pe.wait_ge(sem("x_added"), (n - 4) // GROUPS + 1)
                pe.matmul(ps[2][:], w(f"q_hi{g}"), k.q_hi[:, q_at], start=True, stop=False)
                last = pe.matmul(ps[2][:], w(f"q_lo{g}"), k.q_lo[:, q_at], start=False, stop=not rowmask)
                if rowmask:
                    last = pe.matmul(ps[2][:], w("query_rows"), k.ones[:], start=False, stop=True)
                last.then_inc(sem("q_stacked"), 1)

            def first_scores(i):
                n, t, h, m, keys = chunks[i]
                if i % nchunks == 0:
                    pe.wait_ge(sem("Q_ready"), n + 1)
                    pe.wait_ge(sem("K_ready"), n + 1)
                if i >= 2:
                    pe.wait_ge(sem("max_done"), i - 1)
                j = h % GROUP
                out = ps[3 + i % 2][:, 0:m * keys].rearrange("p (h k) -> p h k", h=m)
                if m == 1:
                    keys = max(keys, FULLRATE)
                    out = ps[3 + i % 2][:, 0:keys].rearrange("p (h k) -> p h k", h=1)
                last = pe.matmul(out, k.Q[:, n % 2, t * P:(t + 1) * P], k.K[:, n % 2, j:j + m, 0:keys], start=True, stop=k.kind != "full")
                if k.kind == "full":
                    last = pe.matmul(out, w("negi"), over(k.mq[:, n // GROUPS, t, 0:keys], 1, m), start=False, stop=True)
                if k.kind == "page":
                    last = pe.matmul(ps[3 + i % 2][:, t * P:(t + 1) * P], w("negi"), w("pageq"), start=False, stop=True, skip_group_check=True)
                last.then_inc(sem("scores_done"), 1)

            def turn_maxima(n):
                pe.wait_ge(sem("mp_ready"), n + 1)
                for t in range(QT):
                    half, first = ps[7][:, (t // 2) * 2 * P:(t // 2 + 1) * 2 * P], t % 2 == 0
                    last = pe.matmul(half, k.mp[:, n % 2, t, :], w("identr")[:, P if first else 0:3 * P if first else 2 * P], start=first, stop=not first)
                last.then_inc(sem("mT_done"), 1)

            def second_scores(u):
                n, what, h, kt, q0 = units[u]
                if u % per_group == 0:
                    pe.wait_ge(sem("maxima_in"), n + 1)
                if u >= 2:
                    pe.wait_ge(sem("exp_done"), u - 1)
                out = ps[u % 2][:, q0:S]
                keys = k.kr[:, n % 2] if what == "rest" else k.K[:, n % 2, h % GROUP, kt * P:(kt + 1) * P]
                first = min(q0, S - FULLRATE)
                last = pe.matmul(ps[u % 2][:, first:S], keys, k.Q[:, n % 2, first:S], start=True, stop=k.kind != "full")
                if k.kind == "full":
                    last = pe.matmul(out, w("negi"), (k.mr if what == "rest" else k.mt)[:, n // GROUPS, q0:S], start=False, stop=True)
                if k.kind == "page":
                    last = pe.matmul(ps[u % 2][:, kt * P:(kt + 1) * P], w("negi"), w("paget"), start=False, stop=True, skip_group_check=True)
                last.then_inc(sem("st_done"), 1)

            def products(u):
                n, what, h, kt, q0 = units[u]
                j = h % GROUP
                if u % per_group == 0:
                    pe.wait_ge(sem("v_ready"), (n + 1) * (1 + GROUP if k.ctx_keys else 1))
                    if n >= 2:
                        pe.wait_ge(sem("oT_ready"), n - 1)
                pe.wait_ge(sem("exp_done"), u + 1)
                if what == "rest":
                    last = pe.matmul(ps[5 + n % 2][:], k.vr[:, n % 2, :], k.p[:, u % 3, :], start=True, stop=True, skip_group_check=True)
                else:
                    last = pe.matmul(ps[5 + n % 2][32 * j:32 * (j + 1), q0:S], k.v[:, n % 2, kt, j, :], k.p[:, u % 3, q0:S],
                                     start=not k.ctx_keys and kt == 0, stop=True, skip_group_check=True)
                last.then_inc(sem("pv_done"), 1)

            def pick_sums(n):
                pe.wait_ge(sem("o_ready"), n + 1)
                for t in range(QT):
                    last = pe.matmul(ps[5 + n % 2][:, t * GROUP:(t + 1) * GROUP], k.o[:, n % 2, t * P:(t + 1) * P], w("sums"), start=True, stop=True)
                last.then_inc(sem("sums_done"), 1)

            def spread_factors(n):
                pe.wait_ge(sem("rx_ready"), n + 1)
                tensor_transpose_tiles(pe, ps[5 + n % 2], k.rx, w("ident")).then_inc(sem("factors_done"), 1)

            def output(e, g):
                pe.wait_ge(sem("oT_ready"), GROUPS * e + g + 1)
                if g == 0:
                    pe.wait_ge(sem("Q_ready"), min(groups, GROUPS * (e + 1) + 3))
                for t in range(QT):
                    last = pe.matmul(ps[2][:, t * P:(t + 1) * P], oT[:, g, t * P:(t + 1) * P], w(f"{pre}_wo")[:, g * P:(g + 1) * P],
                                     start=(g == 0 and t == 0), stop=(g == GROUPS - 1), skip_group_check=True)
                    if bias and g == 0:
                        pe.matmul(ps[2][:, t * P:(t + 1) * P], w("ones")[0:1, :], w(f"{pre}_bo")[0:1, :], start=False, stop=False, skip_group_check=True)
                if g == GROUPS - 1:
                    last.then_inc(sem("y_done"), 1)

            start = 1 if k.ctx_keys else 4
            stack_parts(0)
            for i in range(nchunks):
                first_scores(i)
            turn_maxima(0)
            i, used = nchunks, 0

            def products_up_to(u):
                nonlocal used
                while used < u:
                    products(used)
                    used += 1

            for u in range(len(units)):
                n, at = divmod(u, per_group)
                if at == 0:
                    if n >= 2:
                        spread_factors(n - 2)
                    products_up_to(u - 1)
                second_scores(u)
                upto = i
                if n + 1 < groups:
                    if at == 0:
                        stack_parts(n + 1)
                    elif at >= start:
                        upto = nchunks * (n + 1) + min(nchunks, -(-nchunks * (at - start + 1) // (per_group - 1 - start)))
                middle = (i + upto + 1) // 2
                while i < middle:
                    first_scores(i)
                    i += 1
                products_up_to(u - 1)
                while i < upto:
                    first_scores(i)
                    i += 1
                if at == 2 and n >= 2 and ends(n - 2):
                    for g in range(GROUPS):
                        output((n - 2) // GROUPS, g)
                if at == 3 and n >= 1:
                    pick_sums(n - 1)
                if at == per_group - 1 and n + 1 < groups:
                    turn_maxima(n + 1)
            spread_factors(groups - 2)
            while used < len(units):
                products(used)
                used += 1
            for g in range(GROUPS - 1):
                output(BODY - 1, g)
            pick_sums(groups - 1)
            spread_factors(groups - 1)
            output(BODY - 1, GROUPS - 1)
    end_of_block(net)



class Wide:

    def __init__(self, net, sb):
        self.src = sb("src", [P, KPAD + P])
        self.qT = sb("qT", [P, HEADS // 2, S])
        self.kk = sb("kk", [P, HEADS, KPAD])
        self.v = sb("v", [P, HEADS, XHD])
        self.vr = sb("vr", [P, HEADS, XHD])
        self.p = sb("p", [P, 2, GROUP, KPAD])
        self.pr = sb("pr", [P, 2, P])
        self.pT = sb("pT", [P, 2, GROUP, P])
        self.prT = sb("prT", [P, 2, P])
        self.m = sb("m", [P, 2, GROUP])
        self.negm = sb("negm", [P, 2, GROUP])
        self.sum = sb("sum", [P, 4, GROUP])
        self.rs = sb("rs", [P, 2, GROUP])
        self.o = sb("o", [P, 2, HEADS * XHD])
        self.oT = sb("oT", [P, 2, 4, P])
        self.mq = sb("mq", [P, QT, KPAD], BF16)
        self.kf = sb("kf", [P, KPAD])
        self.lf = sb("lf", [P, 1])
        self.bq = sb("bq", [P, HEADS // 2])


def wide_prepare(net, k, scale):
    with net.nc.Block() as block:

        @block.vector
        def _(dve):
            ch = Chain(dve, net.sem("dve_chain"))
            dve.memset(k.kk[:], 0.0)
            dve.memset(k.vr[:], 0.0)
            dve.tensor_scalar(k.bq[:], net.w("x3_bq"), scale, None, ALU.mult)
            ch.link(dve.memset(k.p[:], 0.0))
    end_of_block(net)



def wide_block(net, b, k, scale):
    nc, sem, ps, w = net.nc, net.sem, net.ps, net.w
    steps, pairs = QT * GROUPS, HEADS // 2
    rest_cols = slice(3 * P, 4 * P)

    with nc.Block() as block:

        @block.vector
        def _(dve):
            ch = Chain(dve, sem("dve_chain"))
            cq = w("cq").rearrange("p (t k) -> p t k", t=QT)
            ch.link(dve.tensor_copy(k.lf[:], w("len")[:, bass.ts(b, 1)]))
            ch.link(dve.tensor_scalar(k.kf[:], w("kidx"), k.lf[:], None, ALU.is_ge))
            for t in range(QT):
                last = dve.tensor_tensor(k.mq[:, t, :], cq[:, t, :], k.kf[:], ALU.max)
            last.then_inc(sem("mask_ready"), 1)
            for c in range(pairs):
                if c % 4 == 0:
                    heads = slice(2 * c, 2 * c + 8)
                    bias = w("x3_bv").rearrange("p (h d) -> p h d", h=HEADS)
                    dve.wait_ge(sem("v_done"), c // 4 + 1)
                    dve.tensor_tensor(k.v[:, heads, :], ps[4][:].rearrange("p (h d) -> p h d", h=8), bias[:, heads, :], ALU.add).then_inc(sem("v_ready"), 1)
                    for j in range(GROUP):
                        rows, own = slice(32 * j, 32 * j + KREM), slice(2 * c + j, 2 * c + 8, GROUP)
                        dve.tensor_tensor(k.vr[rows, own, :], ps[5][rows, :].rearrange("p (h d) -> p h d", h=8)[:, j::GROUP, :],
                                          bias[rows, own, :], ALU.add).then_inc(sem("v_ready"), 1)
                dve.wait_ge(sem("k_done"), c + 1)
                dve.scalar_tensor_tensor(k.kk[:, 2 * c:2 * c + 2, 0:S2], over(ps[2 + c % 2][:, 0:S2], 1, 2), w("x3_bk")[:, c:c + 1],
                                         over(w("halfsel"), 2, S2), ALU.add, ALU.mult).then_inc(sem("kk_ready"), 1)

            def maxima(n):
                for i in range(2):
                    dve.wait_ge(sem("scores_done"), 2 * n + i + 1)
                    last = dve.reduce_max(k.m[:, n % 2, 2 * i:2 * i + 2], ps[2 * (n % 2) + i][:, 0:2 * S2].rearrange("p (h k) -> p h k", h=2), AX)
                ch.link(last)
                if n >= 2:
                    dve.wait_ge(sem("exp_done"), GROUP * (n - 1))
                dve.tensor_scalar(k.negm[:, n % 2, :], k.m[:, n % 2, :], -1.0, None, ALU.mult).then_inc(sem("negm_ready"), 1)

            def copy_turned(n):
                dve.wait_ge(sem("tr_done"), n + 1)
                if n >= 2:
                    dve.wait_ge(sem("pv_done"), n - 1)
                dve.tensor_copy(k.pT[:, n % 2], ps[4 + n % 2][:].rearrange("p (h q) -> p h q", h=GROUP)).then_inc(sem("pT_ready"), 1)
                dve.wait_ge(sem("rest_done"), n + 1)
                dve.tensor_copy(k.prT[:, n % 2, :], ps[2 * (n % 2)][:, rest_cols]).then_inc(sem("prT_ready"), 1)

            def normalise(n):
                t, g = divmod(n, GROUPS)
                dve.wait_ge(sem("pv_done"), n + 1)
                ch.link(dve.reciprocal(k.rs[:, n % 2, :], k.sum[:, n % 4, :]))
                if g == 0 and t >= 2:
                    dve.wait_ge(sem("oT_done"), 2 * (t - 1))
                width = GROUP * XHD
                dve.tensor_tensor(k.o[:, t % 2, g * width:(g + 1) * width].rearrange("p (h d) -> p h d", h=GROUP),
                                  ps[6 + n % 2][:, 0:width].rearrange("p (h d) -> p h d", h=GROUP), over(k.rs[:, n % 2, :], 2, XHD), ALU.mult).then_inc(sem("o_ready"), 1)

            def add_output(t):
                x = x_of(net, b)[:, t, :]
                dve.wait_ge(sem("y_done"), t + 1)
                dve.tensor_tensor(x, x, ps[1][:, 0:P], ALU.add).then_inc(sem("x_added"), 1)

            maxima(0)
            for n in range(steps):
                if n + 1 < steps:
                    maxima(n + 1)
                copy_turned(n)
                if n >= 1:
                    normalise(n - 1)
                if n >= 6 and n % GROUPS == 2:
                    add_output((n - 6) // GROUPS)
            normalise(steps - 1)
            add_output(QT - 1)
            dve.wait_ge(sem("x_added"), QT)

        @block.gpsimd
        def _(pool):
            nc.gpsimd.tensor_copy(k.src[:, 0:KPAD], w("ctxT")[:, bass.ts(b, KPAD)]).then_inc(sem("src_ready"), 1)
            pool.wait_ge(sem("src_ready"), 1)
            nc.gpsimd.tensor_copy(k.src[:, KPAD:KPAD + P], w("restT")[:, bass.ts(b, P)]).then_inc(sem("src_ready"), 1)
            pool.wait_ge(sem("src_ready"), 2)
            for n in range(steps):
                pool.wait_ge(sem("exp_done"), GROUP * (n + 1))
                if n >= 2:
                    pool.wait_ge(sem("tr_done"), n - 1)
                nc.gpsimd.tensor_copy(k.pr[:, n % 2, :].rearrange("p (h k) -> p h k", h=GROUP), k.p[:, n % 2, :, KMAIN:KPAD]).then_inc(sem("pr_ready"), 1)

        @block.scalar
        def _(act):
            for c in range(pairs):
                act.wait_ge(sem("q_done"), c + 1)
                nc.scalar.activation(k.qT[:, c, :], ps[c % 2][:], ACT.Identity, scale=scale, bias=k.bq[:, c:c + 1]).then_inc(sem("qT_ready"), 1)

            def exponentials(n):
                act.wait_ge(sem("negm_ready"), n + 1)
                if n >= 2:
                    act.wait_ge(sem("tr_done"), n - 1)
                    act.wait_ge(sem("pr_ready"), n - 1)
                if n >= 4:
                    act.wait_ge(sem("o_ready"), n - 3)
                for j in range(GROUP):
                    nc.scalar.activation(k.p[:, n % 2, j, 0:S2], ps[2 * (n % 2) + j // 2][:, j % 2 * S2:(j % 2 + 1) * S2], ACT.Exp,
                                         bias=k.negm[:, n % 2, j:j + 1], accum_out=k.sum[:, n % 4, j:j + 1]).then_inc(sem("exp_done"), 1)

            def copy_outputs(t):
                for i in range(2):
                    act.wait_ge(sem("oT_done"), 2 * t + i + 1)
                    if t >= 1:
                        act.wait_ge(sem("y_done"), t)
                    nc.scalar.copy(k.oT[:, i], ps[4 + i][:].rearrange("p (c q) -> p c q", c=4)).then_inc(sem("oT_ready"), 1)

            exponentials(0)
            for n in range(steps):
                if n + 1 < steps:
                    exponentials(n + 1)
                if n >= 5 and n % GROUPS == 1:
                    copy_outputs((n - 5) // GROUPS)
            copy_outputs(QT - 1)

        @block.tensor
        def _(pe):
            ones = w("ones")[0:1, :]
            x = net.xnT_all[:, bass.ts(b, S)]
            pe.wait_ge(sem("src_ready"), 2)
            for half in range(2):
                cols = slice(512 * half, 512 * half + 512)
                if half:
                    pe.wait_ge(sem("v_ready"), 1 + GROUP)
                pe.matmul(ps[4][:], k.src[:, 0:P], w("x3_wv")[:, cols], start=True, stop=True)
                pe.matmul(ps[5][:], k.src[:, KPAD:KPAD + P], w("x3_wv")[:, cols], start=True, stop=True).then_inc(sem("v_done"), 1)
                for c in range(4 * half, 4 * half + 4):
                    if c >= 2:
                        pe.wait_ge(sem("qT_ready"), c - 1)
                    pe.matmul(ps[c % 2][:], w("x3_wq")[:, c * P:(c + 1) * P], x, start=True, stop=True).then_inc(sem("q_done"), 1)
                    if c >= 2:
                        pe.wait_ge(sem("kk_ready"), c - 1)
                    pe.matmul(ps[2 + c % 2][:, 0:KPAD], w("x3_wk")[:, c * P:(c + 1) * P], k.src[:, 0:KPAD], start=True, stop=True).then_inc(sem("k_done"), 1)
            pe.wait_ge(sem("mask_ready"), 1)
            pe.wait_ge(sem("qT_ready"), pairs)
            pe.wait_ge(sem("kk_ready"), pairs)
            pe.wait_ge(sem("v_ready"), 2 * (1 + GROUP))

            def scores(n):
                t, g = divmod(n, GROUPS)
                if n >= 2:
                    pe.wait_ge(sem("exp_done"), GROUP * (n - 1))
                    pe.wait_ge(sem("prT_ready"), n - 1)
                if n >= 8 and g == 0:
                    pe.wait_ge(sem("x_added"), t - 1)
                for i in range(2):
                    c = 2 * g + i
                    out = ps[2 * (n % 2) + i][:, 0:2 * S2].rearrange("p (h k) -> p h k", h=2)
                    pe.matmul(out, k.qT[:, c, t * P:(t + 1) * P], k.kk[:, 2 * c:2 * c + 2, 0:S2], start=True, stop=False)
                    pe.matmul(out, w("negi"), over(k.mq[:, t, 0:S2], 1, 2), start=False, stop=True).then_inc(sem("scores_done"), 1)

            def turn(n):
                t, g = divmod(n, GROUPS)
                pe.wait_ge(sem("exp_done"), GROUP * (n + 1))
                if n >= 6 and g >= 2:
                    pe.wait_ge(sem("oT_ready"), 2 * ((n - 6) // GROUPS) + n % 2 + 1)
                elif n >= 2:
                    pe.wait_ge(sem("pT_ready"), n - 1)
                for j in range(GROUP):
                    last = pe.transpose(ps[4 + n % 2][:, j * P:(j + 1) * P], k.p[:, n % 2, j, 0:KMAIN], w("ident"))
                last.then_inc(sem("tr_done"), 1)
                pe.wait_ge(sem("pr_ready"), n + 1)
                pe.transpose(ps[2 * (n % 2)][:, rest_cols], k.pr[:, n % 2, :], w("ident")).then_inc(sem("rest_done"), 1)

            def products(n):
                g = n % GROUPS
                pe.wait_ge(sem("prT_ready"), n + 1)
                pe.wait_ge(sem("pT_ready"), n + 1)
                if n >= 2:
                    pe.wait_ge(sem("o_ready"), n - 1)
                out = ps[6 + n % 2]
                heads = slice(GROUP * g, GROUP * (g + 1))
                pe.matmul(out[:, 0:GROUP * XHD], k.prT[:, n % 2, :], k.vr[:, heads, :].rearrange("p h d -> p (h d)"), start=True, stop=False, skip_group_check=True)
                for j in range(GROUP):
                    last = pe.matmul(out[:, j * XHD:(j + 1) * XHD], k.pT[:, n % 2, j, :], k.v[:, GROUP * g + j, :], start=False, stop=True, skip_group_check=True)
                last.then_inc(sem("pv_done"), 1)

            def turn_outputs(t):
                pe.wait_ge(sem("o_ready"), GROUPS * (t + 1))
                for i in range(2):
                    pe.wait_ge(sem("pT_ready"), min(steps - 1 + i, GROUPS * t + 5 + i))
                    for c in range(4):
                        at = (4 * i + c) * P
                        last = pe.transpose(ps[4 + i][:, c * P:(c + 1) * P], k.o[:, t % 2, at:at + P], w("ident"))
                    last.then_inc(sem("oT_done"), 1)

            def output(t):
                pe.wait_ge(sem("oT_ready"), 2 * t + 2)
                out = ps[1][:, 0:P]
                for c in range(pairs):
                    pe.matmul(out, k.oT[:, c // 4, c % 4, :], w("x3_wo")[:, c * P:(c + 1) * P], start=(c == 0), stop=False, skip_group_check=True)
                pe.matmul(out, ones, w("x3_bo")[0:1, :], start=False, stop=True, skip_group_check=True).then_inc(sem("y_done"), 1)

            scores(0)
            for n in range(steps):
                if n + 1 < steps:
                    scores(n + 1)
                turn(n)
                if n >= 1:
                    products(n - 1)
                if n >= 5 and n % GROUPS == 1:
                    turn_outputs((n - 5) // GROUPS)
                if n >= 6 and n % GROUPS == 2:
                    output((n - 6) // GROUPS)
            products(steps - 1)
            turn_outputs(QT - 1)
            output(QT - 1)
    end_of_block(net)



def router_block(net, k, weight, keep_x=False, parts=None):
    nc, sem, ps, w = net.nc, net.sem, net.ps, net.w
    n = k.n
    with nc.Block() as block:

        @block.vector
        def _(dve):
            ch = Chain(dve, sem("dve_chain"))
            vector_layernorm(dve, ch, net.x, n.xn, n, sem("xn_ready"))
            if keep_x:
                dve.wait_ge(sem("xn_ready"), B)
                ch.link(dve.tensor_tensor(net.x[:], net.x[:], n.xn[:], ALU.add))
            if parts:
                for b in range(B):
                    at = slice(b * S, (b + 1) * S)
                    dve.wait_ge(sem("xnT_ready"), b + 1)
                    ch.link(dve.tensor_copy(parts.x_hi[:, at], net.xnT_all[:, at]))
                    ch.link(dve.tensor_tensor(parts.x_lo[:, at], net.xnT_all[:, at], parts.x_hi[:, at].bitcast(F32), ALU.subtract))
            if weight is not None:
                for b in range(B):
                    dve.wait_ge(sem("logits_done"), b + 1)
                    ch.link(dve.tensor_copy(net.logits[:, :, b, :], ps[b][:, 0:QT * E8].rearrange("p (t e) -> p t e", t=QT)))

        @block.scalar
        def _(act):
            for b in range(B):
                act.wait_ge(sem("xT_done"), b + 1)
                nc.scalar.copy(net.xnT_all[:, b * S:(b + 1) * S], ps[6 + b % 2][:]).then_inc(sem("xnT_ready"), 1)

        @block.tensor
        def _(pe):
            def scores(b):
                pe.wait_ge(sem("xnT_ready"), b + 1)
                for t in range(QT):
                    at = b * S + t * P
                    last = pe.matmul(ps[b][:, t * E8:(t + 1) * E8], net.xnT_all[:, at:at + P], w(weight), start=True, stop=True)
                last.then_inc(sem("logits_done"), 1)

            for b in range(B):
                pe.wait_ge(sem("xn_ready"), b + 1)
                if b >= 2:
                    pe.wait_ge(sem("xnT_ready"), b - 1)
                tensor_transpose_tiles(pe, ps[6 + b % 2], n.xn[:, b * QT:(b + 1) * QT, :], w("ident")).then_inc(sem("xT_done"), 1)
                if weight is not None and b >= 1:
                    scores(b - 1)
            if weight is not None:
                scores(B - 1)
    end_of_block(net)


class Router:

    def __init__(self, net, sb):
        n = QT * B
        self.g = sb("g", [P, n, E8])
        self.t = sb("t", [P, n, E8])
        self.sel = [sb(f"sel{i}", [P, n, E8]) for i in range(2)]
        self.top = sb("top", [P, n, 2])
        self.rm = sb("rm", [P, n])
        self.sum = sb("sum", [P, n])
        self.pair = sb("pair", [P, 2, n, E8])
        self.tot = sb("tot", [P, 2, E8])
        self.one = sb("one", [P, E8])
        self.temp = sb("temp", [P, 1])
        self.u = sb("u", [32, S])
        self.ue = sb("ue", [32, S])
        self.um = sb("um", [32, 1])
        self.us = sb("us", [32, 1])
        self.ul = sb("ul", [32, 1])


def vector_top2(dve, ch, k, rank):
    n = QT * B
    src = k.g
    for i in range(2):
        ch.link(dve.reduce_max(k.top[:, :, i], src[:], AX))
        ch.link(dve.tensor_tensor(k.sel[i][:], src[:], over(k.top[:, :, i], 2, E8), ALU.is_equal))
        ch.link(dve.tensor_tensor(k.sel[i][:], k.sel[i][:], over(rank, 1, n), ALU.mult))
        ch.link(dve.reduce_max(k.rm[:], k.sel[i][:], AX))
        last = dve.tensor_tensor(k.sel[i][:], k.sel[i][:], over(k.rm[:], 2, E8), ALU.is_equal)
        if i == 0:
            ch.link(last)
            ch.link(dve.scalar_tensor_tensor(k.t[:], k.sel[0][:], NEG, k.g[:], ALU.mult, ALU.add))
            src = k.t
    return last


def flat(t):
    return t[:].rearrange("p t b e -> p (t b) e")


def route_mean(net, k):
    nc, sem, ps, w = net.nc, net.sem, net.ps, net.w
    n = QT * B
    with nc.Block() as block:

        @block.vector
        def _(dve):
            ch = Chain(dve, sem("dve_chain"))
            lg = flat(net.logits)
            ch.link(dve.reduce_max(k.rm[:], lg, AX))
            dve.tensor_tensor(k.g[:], lg, over(k.rm[:], 2, E8), ALU.subtract).then_inc(sem("centred"), 1)
            dve.wait_ge(sem("exp_done"), 1)
            ch.link(dve.reduce_sum(k.sum[:], k.t[:], AX))
            ch.link(dve.reciprocal(k.sum[:], k.sum[:]))
            ch.link(dve.tensor_tensor(k.g[:], k.t[:], over(k.sum[:], 2, E8), ALU.mult))
            ch.link(vector_top2(dve, ch, k, w("rank")))
            ch.link(dve.tensor_tensor(k.sum[:], k.top[:, :, 0], k.top[:, :, 1], ALU.add))
            ch.link(dve.reciprocal(k.sum[:], k.sum[:]))
            ch.link(dve.tensor_tensor(k.pair[:, 1], k.sel[0][:], k.sel[1][:], ALU.add))
            ch.link(dve.tensor_tensor(k.t[:], k.g[:], k.pair[:, 1], ALU.mult))
            dve.tensor_tensor(k.pair[:, 0], k.t[:], over(k.sum[:], 2, E8), ALU.mult).then_inc(sem("pair_ready"), 1)
            dve.wait_ge(sem("sums_done"), 1)
            ch.link(dve.reduce_sum(k.tot[:], ps[0][:, 0:2 * n * E8].rearrange("p (a n e) -> p a e n", a=2, n=n), AX))
            ch.link(dve.tensor_scalar(k.one[:], k.tot[:, 1], 1.0, None, ALU.max))
            ch.link(dve.reciprocal(k.one[:], k.one[:]))
            ch.link(dve.tensor_tensor(k.one[:], k.one[:], k.tot[:, 0], ALU.mult))
            ch.link(dve.tensor_tensor(flat(net.coef), k.pair[:, 1], over(k.one[:], 1, n), ALU.mult))

        @block.scalar
        def _(act):
            act.wait_ge(sem("centred"), 1)
            nc.scalar.activation(k.t[:], k.g[:], ACT.Exp).then_inc(sem("exp_done"), 1)

        @block.tensor
        def _(pe):
            pe.wait_ge(sem("pair_ready"), 1)
            pe.matmul(ps[0][:, 0:2 * n * E8], w("ones"), k.pair[:].rearrange("p a n e -> p (a n e)"), start=True, stop=True).then_inc(sem("sums_done"), 1)
    end_of_block(net)


SINKHORN = 3


def route_sinkhorn(net, k):
    nc, sem, ps, w = net.nc, net.sem, net.ps, net.w
    n = QT * B
    tok = k.g[:].rearrange("p (t b) e -> p t (b e)", t=QT)
    with nc.Block() as block:

        @block.vector
        def _(dve):
            ch = Chain(dve, sem("dve_chain"))
            lg = flat(net.logits)
            ch.link(dve.tensor_scalar(k.temp[:], w("f2_temp"), 0.1, None, ALU.max))
            ch.link(dve.reciprocal(k.temp[:], k.temp[:]))
            ch.link(dve.tensor_tensor(k.g[:], lg, over(w("f2_router_b"), 1, n), ALU.add))
            ch.link(dve.tensor_scalar(k.g[:], k.g[:], k.temp[:], None, ALU.mult))
            for i in range(SINKHORN):
                ch.link(dve.reduce_max(k.rm[:], k.g[:], AX))
                dve.tensor_tensor(k.g[:], k.g[:], over(k.rm[:], 2, E8), ALU.subtract).then_inc(sem("row_centred"), 1)
                dve.wait_ge(sem("row_exp"), i + 1)
                dve.reduce_sum(k.sum[:], k.t[:], AX).then_inc(sem("row_sum"), 1)
                dve.wait_ge(sem("row_log"), i + 1)
                dve.tensor_tensor(k.g[:], k.g[:], over(k.rm[:], 2, E8), ALU.subtract).then_inc(sem("row_ready"), 1)
                dve.wait_ge(sem("turned"), i + 1)
                ch.link(dve.reduce_max(k.um[:], ps[0][0:32, :], AX))
                dve.tensor_scalar(k.u[:], ps[0][0:32, :], k.um[:], None, ALU.subtract).then_inc(sem("col_centred"), 1)
                dve.wait_ge(sem("col_log"), i + 1)
                dve.tensor_scalar(k.u[:], k.u[:], k.ul[:], None, ALU.subtract).then_inc(sem("col_ready"), 1)
                dve.wait_ge(sem("turned_back"), i + 1)
                dve.tensor_copy(tok, ps[1][:, 0:QT * 32].rearrange("p (t c) -> p t c", t=QT)).then_inc(sem("log_gates"), 1)
                dve.wait_ge(sem("log_gates"), i + 1)
            dve.wait_ge(sem("gates_exp"), 1)
            ch.link(dve.reduce_sum(k.sum[:], k.t[:], AX))
            ch.link(dve.tensor_scalar(k.sum[:], k.sum[:], 1e-8, None, ALU.add))
            ch.link(dve.reciprocal(k.sum[:], k.sum[:]))
            ch.link(dve.tensor_tensor(k.g[:], k.t[:], over(k.sum[:], 2, E8), ALU.mult))
            ch.link(vector_top2(dve, ch, k, w("rank")))
            ch.link(dve.tensor_tensor(k.sum[:], k.top[:, :, 0], k.top[:, :, 1], ALU.add))
            ch.link(dve.tensor_scalar(k.sum[:], k.sum[:], 1e-8, None, ALU.add))
            ch.link(dve.reciprocal(k.sum[:], k.sum[:]))
            ch.link(dve.tensor_tensor(k.t[:], k.sel[0][:], k.sel[1][:], ALU.add))
            ch.link(dve.tensor_tensor(k.t[:], k.g[:], k.t[:], ALU.mult))
            ch.link(dve.tensor_tensor(flat(net.coef), k.t[:], over(k.sum[:], 2, E8), ALU.mult))

        @block.scalar
        def _(act):
            for i in range(SINKHORN):
                act.wait_ge(sem("row_centred"), i + 1)
                nc.scalar.activation(k.t[:], k.g[:], ACT.Exp).then_inc(sem("row_exp"), 1)
                act.wait_ge(sem("row_sum"), i + 1)
                nc.scalar.activation(k.rm[:], k.sum[:], ACT.Ln).then_inc(sem("row_log"), 1)
                act.wait_ge(sem("col_centred"), i + 1)
                nc.scalar.activation(k.ue[:], k.u[:], ACT.Exp, accum_out=k.us[:]).then_inc(sem("col_exp"), 1)
                act.wait_ge(sem("col_exp"), i + 1)
                nc.scalar.activation(k.ul[:], k.us[:], ACT.Ln).then_inc(sem("col_log"), 1)
            act.wait_ge(sem("log_gates"), SINKHORN)
            nc.scalar.activation(k.t[:], k.g[:], ACT.Exp).then_inc(sem("gates_exp"), 1)

        @block.tensor
        def _(pe):
            for i in range(SINKHORN):
                pe.wait_ge(sem("row_ready"), i + 1)
                for t in range(QT):
                    last = pe.transpose(ps[0][0:32, t * P:(t + 1) * P], tok[:, t, :], w("ident"))
                last.then_inc(sem("turned"), 1)
                pe.wait_ge(sem("col_ready"), i + 1)
                for t in range(QT):
                    last = pe.transpose(ps[1][:, t * 32:(t + 1) * 32], k.u[:, t * P:(t + 1) * P], w("ident")[0:32, 0:32])
                last.then_inc(sem("turned_back"), 1)
    end_of_block(net)


def route_tokens(net, k):
    nc, sem, ps, w = net.nc, net.sem, net.ps, net.w
    n = QT * B
    top = k.top[:].rearrange("p (t b) c -> p t (b c)", t=QT)
    nb = 2 * B
    with nc.Block() as block:

        @block.vector
        def _(dve):
            ch = Chain(dve, sem("dve_chain"))
            ch.link(dve.tensor_copy(k.g[:], flat(net.logits)))
            vector_top2(dve, ch, k, w("rank")).then_inc(sem("top_ready"), 1)
            dve.wait_ge(sem("top_ready"), 1)
            dve.wait_ge(sem("turned"), 1)
            ch.link(dve.reduce_max(k.um[0:nb], ps[0][0:nb, :], AX))
            dve.tensor_scalar(k.u[0:nb, :], ps[0][0:nb, :], k.um[0:nb], None, ALU.subtract).then_inc(sem("centred"), 1)
            dve.wait_ge(sem("exp_done"), 1)
            ch.link(dve.reciprocal(k.us[0:nb], k.us[0:nb]))
            dve.tensor_scalar(k.u[0:nb, :], k.ue[0:nb, :], k.us[0:nb], None, ALU.mult).then_inc(sem("weights_ready"), 1)
            dve.wait_ge(sem("turned_back"), 1)
            ch.link(dve.tensor_copy(top, ps[1][:, 0:QT * nb].rearrange("p (t c) -> p t c", t=QT)))
            ch.link(dve.tensor_tensor(k.g[:], k.sel[0][:], over(k.top[:, :, 0], 2, E8), ALU.mult))
            ch.link(dve.tensor_tensor(k.t[:], k.sel[1][:], over(k.top[:, :, 1], 2, E8), ALU.mult))
            ch.link(dve.tensor_tensor(flat(net.coef), k.g[:], k.t[:], ALU.add))

        @block.scalar
        def _(act):
            act.wait_ge(sem("centred"), 1)
            nc.scalar.activation(k.ue[0:nb, :], k.u[0:nb, :], ACT.Exp, accum_out=k.us[0:nb]).then_inc(sem("exp_done"), 1)

        @block.tensor
        def _(pe):
            pe.wait_ge(sem("top_ready"), 1)
            for t in range(QT):
                last = pe.transpose(ps[0][0:nb, t * P:(t + 1) * P], top[:, t, :], w("ident"))
            last.then_inc(sem("turned"), 1)
            pe.wait_ge(sem("weights_ready"), 1)
            for t in range(QT):
                last = pe.transpose(ps[1][:, t * nb:(t + 1) * nb], k.u[0:nb, t * P:(t + 1) * P], w("ident")[0:nb, 0:nb])
            last.then_inc(sem("turned_back"), 1)
    end_of_block(net)


RING = 3
WRING = 6


class Experts:

    def __init__(self, net, sb, act_kind):
        self.kinds = 1 if act_kind == "bias" else 2
        self.x_hi, self.x_lo = sb("x_hi", [P, B * S], F32R), sb("x_lo", [P, B * S], F32R)
        self.w_hi, self.w_lo = sb("w_hi", [P, WRING, self.kinds * P], F32R), sb("w_lo", [P, WRING, self.kinds * P], F32R)
        self.t = sb("et", [P, 2, S])
        self.a = sb("ea", [P, 2, S])
        self.h = sb("eh", [P, RING, S])


def cut_weights(net, k, name, tiles):
    src = net.w(name).rearrange("p (i c) -> p i c", i=tiles)
    with net.nc.Block() as block:

        @block.vector
        def _(dve):
            ch = Chain(dve, net.sem("dve_chain"))
            ch.link(dve.tensor_copy(k.w_hi[:, 0:tiles], src))
            ch.link(dve.tensor_tensor(k.w_lo[:, 0:tiles], src, k.w_hi[:, 0:tiles].bitcast(F32), ALU.subtract))
    end_of_block(net)



def experts_block(net, b, k, act_kind, names, experts, tiles):
    nc, sem, ps, w = net.nc, net.sem, net.ps, net.w
    first, down = names
    width = k.kinds * P
    work = [(e, i) for e in range(experts) for i in range(tiles)]
    weighed = experts > 1
    with nc.Block() as block:

        @block.gpsimd
        def _(pool):
            for n, (e, i) in enumerate(work if weighed else []):
                if n >= WRING:
                    pool.wait_ge(sem("h_ready"), n - WRING + 1)
                src = w(first.format(e))[:, i * width:(i + 1) * width]
                nc.gpsimd.tensor_copy(k.w_hi[:, n % WRING], src).then_inc(sem("w_hi_ready"), 1)
                pool.wait_ge(sem("w_hi_ready"), n + 1)
                nc.gpsimd.tensor_tensor(k.w_lo[:, n % WRING], src, k.w_hi[:, n % WRING].bitcast(F32), ALU.subtract).then_inc(sem("w_ready"), 1)
                pool.wait_ge(sem("w_ready"), n + 1)

        @block.vector
        def _(dve):
            ch = Chain(dve, sem("dve_chain"))
            x = x_of(net, b)

            def add_expert(e):
                if act_kind == "bias":
                    dve.wait_ge(sem("out_done"), e + 1)
                else:
                    dve.wait_ge(sem("h_used"), tiles * (e + 1))
                if e >= 1:
                    dve.wait_ge(sem("x_added"), e)
                y = ps[6 + e % 2][:].rearrange("p (t d) -> p t d", t=QT)
                if weighed:
                    for t in range(QT):
                        last = dve.scalar_tensor_tensor(x[:, t, :], y[:, t, :], net.coef[:, t, b, e:e + 1], x[:, t, :], ALU.mult, ALU.add)
                else:
                    last = dve.tensor_tensor(x, x, y, ALU.add)
                last.then_inc(sem("x_added"), 1)

            for n, (e, i) in enumerate(work):
                if act_kind != "bias":
                    g, u = ps[n % RING], ps[3 + n % RING]
                    dve.wait_ge(sem("act_done"), n + 1)
                    if n >= RING:
                        dve.wait_ge(sem("h_used"), n - RING + 1)
                    dve.wait_ge(sem("up_done"), n + 1)
                    if act_kind == "silu":
                        ch.link(dve.scalar_tensor_tensor(k.a[:, n % 2], k.t[:, n % 2], 1.0, g[:], ALU.add, ALU.mult))
                        dve.scalar_tensor_tensor(k.h[:, n % RING], u[:], 0.5, k.a[:, n % 2], ALU.mult, ALU.mult).then_inc(sem("h_ready"), 1)
                    else:
                        dve.tensor_tensor(k.h[:, n % RING], u[:], k.t[:, n % 2], ALU.mult).then_inc(sem("h_ready"), 1)
                if i == 1 and e >= 1:
                    add_expert(e - 1)
            add_expert(experts - 1)
            dve.wait_ge(sem("x_added"), experts)

        @block.scalar
        def _(act):
            for n, (e, i) in enumerate(work):
                act.wait_ge(sem("gate_done"), n + 1)
                if act_kind == "bias":
                    if n >= RING:
                        act.wait_ge(sem("h_used"), n - RING + 1)
                    nc.scalar.activation(k.h[:, n % RING], ps[n % RING][:], ACT.Relu, bias=w(f"b{e}")[:, i:i + 1]).then_inc(sem("h_ready"), 1)
                    continue
                if n >= 2:
                    act.wait_ge(sem("h_ready"), n - 1)
                if act_kind == "silu":
                    nc.scalar.activation(k.t[:, n % 2], ps[n % RING][:], ACT.Tanh, scale=0.5).then_inc(sem("act_done"), 1)
                else:
                    nc.scalar.activation(k.t[:, n % 2], ps[n % RING][:], ACT.Relu).then_inc(sem("act_done"), 1)

        @block.tensor
        def _(pe):
            x_hi, x_lo = k.x_hi[:, bass.ts(b, S)], k.x_lo[:, bass.ts(b, S)]

            def hidden(n):
                if weighed:
                    pe.wait_ge(sem("w_ready"), n + 1)
                if n >= RING:
                    pe.wait_ge(sem("h_ready"), n - RING + 1)
                for which, done in enumerate(("gate_done", "up_done")[0:k.kinds]):
                    out, cols = ps[3 * which + n % RING][:], slice(which * P, (which + 1) * P)
                    pe.matmul(out, k.w_hi[:, n % WRING, cols], x_hi, start=True, stop=False)
                    pe.matmul(out, k.w_hi[:, n % WRING, cols], x_lo, start=False, stop=False)
                    pe.matmul(out, k.w_lo[:, n % WRING, cols], x_hi, start=False, stop=True).then_inc(sem(done), 1)

            def output(n):
                e, i = work[n]
                pe.wait_ge(sem("h_ready"), n + 1)
                if i == 0 and e >= 2:
                    pe.wait_ge(sem("x_added"), e - 1)
                bank = ps[6 + e % 2]
                for t in range(QT):
                    last = pe.matmul(bank[:, t * P:(t + 1) * P], k.h[:, n % RING, t * P:(t + 1) * P], w(down.format(e))[:, i * P:(i + 1) * P],
                                     start=(i == 0 and t == 0), stop=(i == tiles - 1), skip_group_check=True)
                last.then_inc(sem("h_used"), 1)
                if i == tiles - 1 and act_kind == "bias":
                    for t in range(QT):
                        last = pe.matmul(bank[:, t * P:(t + 1) * P], w("ones")[0:1, :], w("b2")[0:1, e * P:(e + 1) * P],
                                         start=False, stop=True, skip_group_check=True)
                    last.then_inc(sem("out_done"), 1)

            for n in range(len(work) + 2):
                if n < len(work):
                    hidden(n)
                if n >= 2:
                    output(n - 2)
    end_of_block(net)



NSTATE, NCONV = 16, 4


class Scan:

    def __init__(self, net, sb):
        self.n = Norm(net, sb, B * QT)
        self.xc = sb("xc", [P, B, 2, S])
        self.zs = sb("zs", [P, B, 2, S])
        self.dt = sb("dt", [P, B, S])
        self.bc = sb("bc", [P, B * S], BF16)

    def more_buffers(self, net, sb):
        self.A = sb("A", [P, 2 * NSTATE])
        self.D = sb("D", [P, 2, P])
        self.dtx = sb("dtx", [P, 2, S])
        self.dA = sb("dA", [P, 2, 2, S])
        self.cb = sb("cb", [P, 2, S])
        self.dbx = sb("dbx", [P, 2, 2, S])
        self.h = sb("sh", [P, 2, 2, S])
        self.hc = sb("hc", [P, 2, 2, S])
        self.g = sb("gated", [P, 2, S])



def scan_inputs(net, k, sb):
    nc, sem, ps, w = net.nc, net.sem, net.ps, net.w
    xp = sb("xp", [P, 2, 2, NCONV - 1 + S])
    c, z, zt, t = sb("c", [P, 2, 2, S]), sb("z", [P, 2, S]), sb("zt", [P, 2, S]), sb("st", [P, 2, S])
    bf, bh = sb("bf", [32, S]), sb("bh", [32, S], BF16)
    raw, e, ln, d, iz = (sb(name, [P, S]) for name in ("raw", "e", "ln", "d", "iz"))
    cw, cbias, zbias = sb("cw", [P, 8]), sb("cbias", [P, 2]), sb("zbias", [P, 2])
    with nc.Block() as block:

        @block.vector
        def _(dve):
            ch = Chain(dve, sem("dve_chain"))
            dve.memset(xp[:, :, :, 0:NCONV - 1], 0.0)
            dve.memset(k.bc[:], 0.0)
            dve.tensor_scalar(cw[:], w("m_conv"), 0.5, None, ALU.mult)
            dve.tensor_scalar(cbias[:], w("m_conv_b"), 0.5, None, ALU.mult)
            dve.tensor_scalar(zbias[:], w("m_in_b")[:, 2:4], 0.5, None, ALU.mult).then_inc(sem("halved"), 1)

            def convolve(b):
                dve.wait_ge(sem("tap_ready"), 2 * (b + 1))
                for j in range(1, NCONV):
                    for i in range(2):
                        last = dve.scalar_tensor_tensor(c[:, b % 2, i], xp[:, b % 2, i, j:j + S], cw[:, 4 * i + j:4 * i + j + 1], c[:, b % 2, i], ALU.mult, ALU.add)
                    if j < NCONV - 1:
                        ch.link(last)
                last.then_inc(sem("conv_ready"), 1)

            def activate(b):
                dve.wait_ge(sem("tanh_c"), b + 1)
                dve.scalar_tensor_tensor(k.xc[:, b], t[:], 1.0, c[:, b % 2], ALU.add, ALU.mult).then_inc(sem("xc_ready"), 1)

            def split(b):
                dve.wait_ge(sem("dt_done"), b + 1)
                ch.link(dve.tensor_scalar(raw[:], ps[5][:], w("m_dt_b"), None, ALU.add))
                dve.scalar_tensor_tensor(e[:], raw[:], -1.0, raw[:], ALU.mult, ALU.max).then_inc(sem("abs_ready"), 1)
                at = slice(b * S, (b + 1) * S)
                dve.wait_ge(sem("bc_done"), b + 1)
                ch.link(dve.tensor_scalar(bf[:], ps[4][0:32, :], w("m_xp_b")[0:32, :], None, ALU.add))
                for part in range(2):
                    ch.link(dve.tensor_copy(bh[:], bf[:]))
                    dve.tensor_copy(k.bc[32 * part:32 * part + 32, at], bh[:])
                    ch.link(dve.tensor_tensor(bf[:], bf[:], bh[:], ALU.subtract))
                ch.link(dve.tensor_copy(k.bc[64:96, at], bf[:]))

            def step_sizes(b):
                dve.wait_ge(sem("log_ready"), b + 1)
                ch.link(dve.tensor_scalar(iz[:], d[:], -1.0, 0.0, ALU.add, ALU.is_equal))
                ch.link(dve.scalar_tensor_tensor(d[:], d[:], -1.0, iz[:], ALU.add, ALU.add))
                ch.link(dve.reciprocal(d[:], d[:]))
                dve.tensor_tensor(ln[:], ln[:], iz[:], ALU.add)
                ch.link(dve.tensor_tensor(d[:], d[:], e[:], ALU.mult))
                ch.link(dve.tensor_tensor(d[:], d[:], ln[:], ALU.mult))
                dve.scalar_tensor_tensor(k.dt[:, b], raw[:], 0.0, d[:], ALU.max, ALU.add).then_inc(sem("dt_ready"), 1)
                dve.wait_ge(sem("dt_ready"), b + 1)

            convolve(0)
            activate(0)
            convolve(1)
            for b in range(B):
                split(b)
                if b + 1 < B:
                    activate(b + 1)
                step_sizes(b)
                if b + 2 < B:
                    convolve(b + 2)

        @block.gpsimd
        def _(pool):
            for b in range(B):
                pool.wait_ge(sem("tanh_z"), b + 1)
                nc.gpsimd.tensor_tensor(k.zs[:, b], zt[:], z[:], ALU.mult).then_inc(sem("z_times"), 1)
                pool.wait_ge(sem("z_times"), b + 1)
                nc.gpsimd.tensor_tensor(k.zs[:, b], k.zs[:, b], z[:], ALU.add).then_inc(sem("zs_ready"), 1)
            pool.wait_ge(sem("zs_ready"), B)

        @block.scalar
        def _(act):
            def first_tap(b):
                if b >= 2:
                    act.wait_ge(sem("conv_ready"), b - 1)
                    act.wait_ge(sem("xc_ready"), b - 1)
                for i in range(2):
                    act.wait_ge(sem("in_done"), 4 * b + i + 1)
                    nc.scalar.activation(xp[:, b % 2, i, NCONV - 1:NCONV - 1 + S], ps[i][:], ACT.Identity, bias=w("m_in_b")[:, i:i + 1]).then_inc(sem("xm_ready"), 1)
                for i in range(2):
                    act.wait_ge(sem("xm_ready"), 2 * b + i + 1)
                    nc.scalar.activation(c[:, b % 2, i], xp[:, b % 2, i, 0:S], ACT.Identity, scale=cw[:, 4 * i:4 * i + 1], bias=cbias[:, i:i + 1]).then_inc(sem("tap_ready"), 1)

            def gate(b):
                if b >= 1:
                    act.wait_ge(sem("zs_ready"), b)
                for i in range(2):
                    act.wait_ge(sem("in_done"), 4 * b + i + 3)
                    nc.scalar.activation(z[:, i], ps[2 + i][:], ACT.Identity, scale=0.5, bias=zbias[:, i:i + 1]).then_inc(sem("z_ready"), 1)
                act.wait_ge(sem("z_ready"), 2 * b + 2)
                nc.scalar.activation(zt[:], z[:], ACT.Tanh).then_inc(sem("tanh_z"), 1)

            def activate(b):
                act.wait_ge(sem("conv_ready"), b + 1)
                if b >= 1:
                    act.wait_ge(sem("xc_ready"), b)
                nc.scalar.activation(t[:], c[:, b % 2], ACT.Tanh).then_inc(sem("tanh_c"), 1)

            def logarithms(b):
                act.wait_ge(sem("abs_ready"), b + 1)
                nc.scalar.activation(e[:], e[:], ACT.Exp, scale=-1.0).then_inc(sem("e_ready"), 1)
                act.wait_ge(sem("e_ready"), b + 1)
                nc.scalar.activation(d[:], e[:], ACT.Identity, bias=1.0).then_inc(sem("e1_ready"), 1)
                act.wait_ge(sem("e1_ready"), b + 1)
                nc.scalar.activation(ln[:], d[:], ACT.Ln).then_inc(sem("log_ready"), 1)

            act.wait_ge(sem("halved"), 1)
            first_tap(0)
            activate(0)
            gate(0)
            first_tap(1)
            for b in range(B):
                logarithms(b)
                if b + 1 < B:
                    activate(b + 1)
                    gate(b + 1)
                if b + 2 < B:
                    first_tap(b + 2)

        @block.tensor
        def _(pe):
            def project(b):
                x = net.xnT_all[:, b * S:(b + 1) * S]
                for i in range(4):
                    if b >= 1:
                        if i < 2:
                            pe.wait_ge(sem("xm_ready"), 2 * (b - 1) + i + 1)
                        else:
                            pe.wait_ge(sem("z_ready"), 2 * (b - 1) + i - 1)
                    pe.matmul(ps[i][:], w("m_in")[:, i * P:(i + 1) * P], x, start=True, stop=True).then_inc(sem("in_done"), 1)

            project(0)
            for b in range(B):
                if b + 1 < B:
                    project(b + 1)
                pe.wait_ge(sem("xc_ready"), b + 1)
                if b >= 1:
                    pe.wait_ge(sem("dt_ready"), b)
                for i in range(2):
                    last = pe.matmul(ps[5][:], w("m_dt")[:, i * P:(i + 1) * P], k.xc[:, b, i], start=(i == 0), stop=(i == 1))
                last.then_inc(sem("dt_done"), 1)
                for i in range(2):
                    last = pe.matmul(ps[4][0:32, :], w("m_xp")[:, i * 32:(i + 1) * 32], k.xc[:, b, i], start=(i == 0), stop=(i == 1))
                last.then_inc(sem("bc_done"), 1)
    end_of_block(net)


def scan_prepare(net, k):
    nc, sem, w = net.nc, net.sem, net.w
    with nc.Block() as block:

        @block.scalar
        def _(act):
            nc.scalar.activation(k.A[:], w("m_alog"), ACT.Exp).then_inc(sem("A_exp"), 1)

        @block.vector
        def _(dve):
            ch = Chain(dve, sem("dve_chain"))
            for i in range(2):
                last = dve.tensor_scalar(k.D[:, i, :], w("ident"), w("m_d")[:, i:i + 1], None, ALU.mult)
            ch.link(last)
            dve.wait_ge(sem("A_exp"), 1)
            ch.link(dve.tensor_scalar(k.A[:], k.A[:], -1.0, None, ALU.mult))
    end_of_block(net)



def scan_block(net, b0, k):
    nc, sem, ps, w = net.nc, net.sem, net.ps, net.w
    steps = BODY * NSTATE

    with nc.Block() as block:

        @block.vector
        def _(dve):
            ch = Chain(dve, sem("dve_chain"))

            def apply_gate(e):
                dve.wait_ge(sem("hc_used"), NSTATE * (e + 1))
                for i in range(2):
                    last = dve.tensor_tensor(k.g[:, i], ps[4 + 2 * (e % 2) + i][:], k.zs[:, bass.ts(b0 + e, 1), i].rearrange("p o q -> p (o q)"), ALU.mult)
                last.then_inc(sem("gated_ready"), 1)

            def residual(e):
                dve.wait_ge(sem("out_done"), e + 1)
                xn = k.n.xn[:, bass.ts(b0 + e, QT), :]
                dve.tensor_tensor(xn, ps[4 + 2 * (e % 2)][:].rearrange("p (t d) -> p t d", t=QT), xn, ALU.add).then_inc(sem("r_ready"), 1)

            for u in range(steps):
                e, s = divmod(u, NSTATE)
                if s == 0:
                    dt = k.dt[:, bass.ts(b0 + e, 1), :]
                    xc = k.xc[:, bass.ts(b0 + e, 1)].rearrange("p o i q -> p (o i) q")
                    ch.link(dve.tensor_tensor(k.dtx[:], xc, dt.to_broadcast([P, 2, S]), ALU.mult))
                dve.wait_ge(sem("B_done"), u + 1)
                dve.tensor_tensor(k.dbx[:, u % 2], k.dtx[:], over(ps[u % 2][:], 1, 2), ALU.mult).then_inc(sem("dbx_ready"), 1)
                dve.wait_ge(sem("dbx_ready"), u + 1)
                for i in range(2):
                    dve.wait_ge(sem("dA_ready"), 2 * u + i + 1)
                    if u >= 2 and i == 0:
                        dve.wait_ge(sem("hc_ready"), u - 1)
                    dve.tensor_tensor_scan(k.h[:, u % 2, i], k.dA[:, u % 2, i], k.dbx[:, u % 2, i], 0.0, ALU.mult, ALU.add).then_inc(sem("h_ready"), 1)
                if e >= 1 and s == 2:
                    apply_gate(e - 1)
                if e >= 1 and s == 5:
                    residual(e - 1)
            apply_gate(BODY - 1)
            residual(BODY - 1)
            dve.wait_ge(sem("r_ready"), BODY)

        @block.gpsimd
        def _(pool):
            for u in range(steps):
                pool.wait_ge(sem("C_ready"), u + 1)
                pool.wait_ge(sem("h_ready"), 2 * u + 2)
                if u >= 2:
                    pool.wait_ge(sem("hc_used"), u - 1)
                nc.gpsimd.tensor_tensor(k.hc[:, u % 2], k.h[:, u % 2], over(k.cb[:, u % 2], 1, 2), ALU.mult).then_inc(sem("hc_ready"), 1)

        @block.scalar
        def _(act):
            for u in range(steps):
                e, s = divmod(u, NSTATE)
                for i in range(2):
                    if u >= 2:
                        act.wait_ge(sem("h_ready"), 2 * (u - 2) + i + 1)
                    dt = k.dt[:, bass.ts(b0 + e, 1), :].rearrange("p o q -> p (o q)")
                    nc.scalar.activation(k.dA[:, u % 2, i], dt, ACT.Exp, scale=k.A[:, i * NSTATE + s:i * NSTATE + s + 1]).then_inc(sem("dA_ready"), 1)
                act.wait_ge(sem("C_done"), u + 1)
                if u >= 2:
                    act.wait_ge(sem("hc_ready"), u - 1)
                nc.scalar.copy(k.cb[:, u % 2], ps[2 + u % 2][:]).then_inc(sem("C_ready"), 1)

        @block.tensor
        def _(pe):
            def spread(u):
                e, s = divmod(u, NSTATE)
                bc = k.bc[:, bass.ts(b0 + e, S)]
                if u >= 2:
                    pe.wait_ge(sem("dbx_ready"), u - 1)
                pe.matmul(ps[u % 2][:], w("sel")[:, s * P:(s + 1) * P], bc, start=True, stop=True).then_inc(sem("B_done"), 1)
                if u >= 2:
                    pe.wait_ge(sem("C_ready"), u - 1)
                pe.matmul(ps[2 + u % 2][:], w("sel")[:, (NSTATE + s) * P:(NSTATE + s + 1) * P], bc, start=True, stop=True).then_inc(sem("C_done"), 1)

            def output(e):
                out = ps[4 + 2 * (e % 2)]
                pe.wait_ge(sem("gated_ready"), e + 1)
                for t in range(QT):
                    for i in range(2):
                        pe.matmul(out[:, t * P:(t + 1) * P], k.g[:, i, t * P:(t + 1) * P], w("m_out")[:, i * P:(i + 1) * P], start=(i == 0), stop=False)
                    last = pe.matmul(out[:, t * P:(t + 1) * P], w("ones")[0:1, :], w("m_out_b")[0:1, :], start=False, stop=True)
                last.then_inc(sem("out_done"), 1)

            spread(0)
            spread(1)
            for u in range(steps):
                e, s = divmod(u, NSTATE)
                if u + 2 < steps:
                    spread(u + 2)
                if s == 0:
                    if e >= 2:
                        pe.wait_ge(sem("r_ready"), e - 1)
                    for i in range(2):
                        pe.matmul(ps[4 + 2 * (e % 2) + i][:], k.D[:, i, :], k.xc[:, bass.ts(b0 + e, 1), i].rearrange("p o q -> p (o q)"), start=True, stop=False)
                pe.wait_ge(sem("hc_ready"), u + 1)
                for i in range(2):
                    last = pe.matmul(ps[4 + 2 * (e % 2) + i][:], w("ident"), k.hc[:, u % 2, i], start=False, stop=(s == NSTATE - 1))
                last.then_inc(sem("hc_used"), 1)
                if e >= 1 and s == 4:
                    output(e - 1)
            output(BODY - 1)
    end_of_block(net)


def scan_finish(net, k):
    sem, w = net.sem, net.w
    with net.nc.Block() as block:

        @block.vector
        def _(dve):
            ch = Chain(dve, sem("dve_chain"))
            xn = k.n.xn
            ch.link(vector_layernorm(dve, ch, xn, xn, k.n))
            ch.link(dve.tensor_tensor(xn[:], xn[:], over(w("m_gamma"), 1, B * QT), ALU.mult))
            ch.link(dve.tensor_tensor(xn[:], xn[:], over(w("m_beta"), 1, B * QT), ALU.add))
            ch.link(dve.tensor_tensor(net.x[:], net.x[:], xn[:], ALU.add))
    end_of_block(net)



def program(nc, x_dram, packs, out_dram):
    with ExitStack() as ctx:
        net = Net(nc, ctx)
        loads = {}
        loaded = {name: nc.alloc_semaphore(f"loaded_{name}") for name in packs if name != "x"}
        x_loaded = nc.alloc_semaphore("x_loaded")
        stored = nc.alloc_semaphore("stored")

        def place(stack, name, table, dt=F32):
            offs, n = offsets(table)
            t = stack.enter_context(nc.sbuf_tensor(f"w_{name}", [P, n], dt))
            for key, at in offs.items():
                net.weights[key] = (t, at)
            loads[name] = (t, packs[name], loaded[name])

        for name, table, dt in (("start", START, F32), ("constf", CONSTF, F32), ("constb", CONSTB, BF16), ("attn", ATTN, F32), ("ints", INTS, I32)):
            place(ctx, name, table, dt)
        offs, n = offsets(PLACE)
        placers = net.sb("placers", [P, n], F32R)
        for key, at in offs.items():
            net.weights[key] = (placers, at)
        xv = x_dram.rearrange("b (t p) d -> p (b t) d", p=P)
        ov = out_dram.rearrange("b (t p) d -> p (b t) d", p=P)

        ffn1_room, ffn0_room, first_room = ExitStack(), ExitStack(), ExitStack()
        place(ffn1_room, "ffn1", FFN1, I32)
        place(ffn0_room, "ffn0", FFN0)
        ffn1 = loads["ffn1"][0]
        l1w = ffn1[:, :].bitcast(F32)
        for key in FFN1:
            net.weights[key] = (l1w, net.weights[key][1])
        place(first_room, "tril", TRIL, BF16)
        place_f = first_room.enter_context(nc.sbuf_tensor("place_f", [P, n], F32))

        def load(queue, name):
            t, src, s = loads[name]
            queue.dma_start(t[:, :], src).then_inc(s, 16)

        with nc.Block() as block:

            @block.sync
            def _(sp):
                sp.dma_start(net.x[:], xv).then_inc(x_loaded, 16)
                for name in ("tril", "constf", "attn"):
                    load(sp, name)

            @block.scalar
            def _(act):
                load(act, "start")
                act.dma_start(place_f[:, :], packs["place"]).then_inc(loaded["place"], 16)
                for name in ("constb", "ints", "ffn1", "ffn0"):
                    load(act, name)

            @block.vector
            def _(dve):
                dve.wait_ge(x_loaded, 16)
                dve.wait_ge(loads["start"][2], 16)
                dve.wait_ge(loads["tril"][2], 16)

        def scope():
            stack = ExitStack()

            def sb(name, shape, dt=F32):
                net.names += 1
                return stack.enter_context(nc.sbuf_tensor(f"{name}_{net.names}", shape, dt))
            return stack, sb

        def wait_loaded(name):
            with nc.Block() as block:

                @block.vector
                def _(dve):
                    dve.wait_ge(loads[name][2], 16)

        def narrow_attention(pre, kind, ctx_keys):
            stack, sb = scope()
            with stack:
                k = Narrow(net, sb, kind, ctx_keys)
                inner, inner_sb = scope()
                with inner:
                    narrow_project(net, k, pre, 1.0 / float(np.sqrt(np.float32(HD))), inner_sb)
                k.more_buffers(net, sb)
                narrow_prepare(net, k)
                with nc.Fori(0, B // BODY, 1) as i:
                    narrow_block(net, i * BODY, k, pre)

        class One:
            pass

        def experts(weight, route, act_kind, names, n, tiles, keep_x=False):
            stack, sb = scope()
            with stack:
                k = One()
                k.n = Norm(net, sb, B * QT)
                r = Router(net, sb) if route else None
                e = Experts(net, sb, act_kind)
                router_block(net, k, weight, keep_x, e)
                if route:
                    route(net, r)
                else:
                    cut_weights(net, e, names[0], tiles)
                with nc.Fori(0, B, 1) as b:
                    experts_block(net, b, e, act_kind, names, n, tiles)

        stack, sb = scope()
        with stack:
            k = One()
            k.n = Norm(net, sb)
            k.qT, k.kT = sb("qT", [P, S]), sb("kT", [P, S])
            k.s, k.p = sb("s", [P, QT, S]), sb("p", [P, QT, S])
            k.mx, k.negm, k.sum, k.rs = sb("mx", [P, QT]), sb("negm", [P, QT]), sb("sum", [P, QT]), sb("rs", [P, QT])
            with nc.Fori(0, B, 1) as b:
                single_head_block(net, b, k)
        with nc.Block() as block:

            @block.vector
            def _(dve):
                for name in ("constf", "attn", "constb", "ints"):
                    dve.wait_ge(loads[name][2], 16)
                dve.wait_ge(loaded["place"], 16)
                dve.tensor_copy(placers[:], place_f[:, :]).then_inc(net.sem("placers_ready"), 1)
                dve.wait_ge(net.sem("placers_ready"), 1)
        end_of_block(net)
        first_room.close()
        narrow_attention("x0", "row", True)
        wait_loaded("ffn0")
        experts("f0_router", route_mean, "silu", ("w{}", "d{}"), E8, 4)
        ffn0_room.close()
        narrow_attention("a1", "page", False)
        narrow_attention("x1", "add", True)
        with nc.Block() as block:

            @block.vector
            def _(dve):
                dve.wait_ge(loads["ffn1"][2], 16)
                dve.tensor_scalar(l1w, ffn1[:, :], 1.0 / 127.0, None, ALU.mult).then_inc(net.sem("weights_scaled"), 1)
                dve.wait_ge(net.sem("weights_scaled"), 1)
        end_of_block(net)
        experts(None, None, "silu", ("L1_w", "L1_d"), 1, 3)
        ffn1_room.close()
        stack, sb = scope()
        with stack:
            k = Scan(net, sb)
            router_block(net, k, None)
            inner, inner_sb = scope()
            with inner:
                scan_inputs(net, k, inner_sb)
            k.more_buffers(net, sb)
            scan_prepare(net, k)
            with nc.Fori(0, B // BODY, 1) as i:
                scan_block(net, i * BODY, k)
            scan_finish(net, k)
        def place_and_load(room, name, table):
            place(room, name, table)
            with nc.Block() as block:

                @block.sync
                def _(sp):
                    load(sp, name)

        late_room, ffn2_room = ExitStack(), ExitStack()
        place_and_load(ffn2_room, "ffn2", FFN2)
        narrow_attention("x2", "full", True)
        wait_loaded("ffn2")
        experts("f2_router", route_sinkhorn, "relu", ("w{}", "d{}"), E8, 2, keep_x=True)
        ffn2_room.close()
        place_and_load(late_room, "wide", WIDE)
        narrow_attention("a3", None, False)
        place_and_load(late_room, "ffn3", FFN3)
        wait_loaded("wide")
        stack, sb = scope()
        with stack:
            k = One()
            inner, inner_sb = scope()
            with inner:
                k.n = Norm(net, inner_sb, B * QT)
                router_block(net, k, None)
            k = Wide(net, sb)
            scale = 1.0 / float(np.sqrt(np.float32(XHD)))
            wide_prepare(net, k, scale)
            with nc.Fori(0, B, 1) as b:
                wide_block(net, b, k, scale)
        wait_loaded("ffn3")
        experts("f3_router", route_tokens, "bias", ("w{}", "o{}"), E8, 2)

        with nc.Block() as block:

            @block.sync
            def _(sp):
                for name in ("wide", "ffn2", "ffn3", "ffn0"):
                    sp.wait_ge(loads[name][2], 16)
                sp.dma_start(ov, net.x[:]).then_inc(stored, 16)
                sp.wait_ge(stored, 16)
        late_room.close()



def pack(table, inputs, dtype):
    offs, n = offsets(table)
    out = np.zeros((P, n), dtype)
    for name, (_, f) in table.items():
        a = f(inputs) if inputs is not None else f()
        at, cols = offs[name]
        assert a.shape[1] == cols, (name, a.shape, cols)
        out[0:a.shape[0], at:at + cols] = a
    return out


PACKS = (("start", START, "f"), ("attn", ATTN, "f"), ("wide", WIDE, "f"), ("ffn0", FFN0, "f"), ("ffn2", FFN2, "f"), ("ffn3", FFN3, "f"), ("ffn1", FFN1, "i"), ("ints", INTS, "i"))


def arrays_of(inputs):
    inputs = {n: np.asarray(a) for n, a in inputs.items()}
    out = {"x_dram": np.ascontiguousarray(inputs["x"])}
    for name, table, kind in PACKS:
        out[f"{name}_dram"] = pack(table, inputs, np.float32 if kind == "f" else np.int32)
    out["constf_dram"] = pack(CONSTF, None, np.float32)
    out["place_dram"] = pack(PLACE, None, np.float32)
    for name, table in (("constb", CONSTB), ("tril", TRIL)):
        out[f"{name}_dram"] = (pack(table, None, np.float32).view(np.uint32) >> 16).astype(np.uint16)
    return out


def build(nc, arrays):
    aps = {n: nc.dram_tensor(n, a.shape, mybir.dt.from_np(a.dtype), kind="ExternalInput").ap() for n, a in arrays.items()}
    out = nc.dram_tensor("out_dram", (B, S, P), F32, kind="ExternalOutput").ap()
    packs = {n[:-5]: ap for n, ap in aps.items()}
    for name in ("constb", "tril"):
        packs[name] = packs[name].bitcast(BF16)
    program(nc, aps["x_dram"], packs, out)


def kernel(**inputs):
    import concourse.bacc as bacc
    from concourse.bass_utils import run_bass_kernel_spmd as run

    nc = bacc.Bacc("TRN2", target_bir_lowering=False, num_devices=1)
    arrays = arrays_of(inputs)
    build(nc, arrays)
    r = run(nc, [arrays], core_ids=[0])
    return r.results[0]["out_dram"]
```
